# Optimizing a Trainium2 kernel written in Bass

```python
import numpy as np
import jax
import jax.numpy as jnp

def _softmax(x, axis=-1):
    return jax.nn.softmax(x, axis=axis)

def _gelu(x):
    return jax.nn.gelu(x, approximate=True)

def _silu(x):
    return jax.nn.silu(x)

def _sigmoid(x):
    return jax.nn.sigmoid(x)

def _layernorm(x, axis=-1, eps=1e-05):
    m = jnp.mean(x, axis=axis, keepdims=True)
    v = jnp.var(x, axis=axis, keepdims=True)
    return (x - m) / jnp.sqrt(v + eps)

def _scatter_add(tgt, idx, src, axis=0):
    return tgt.at[idx].add(src)

def _segment_sum(src, seg, n):
    return jax.ops.segment_sum(src, seg, n)
kernel_name = 'mk_macaron_d2_jaxref_r8_279534'

def setup_inputs(seed: int=0):
    np.random.seed(seed)
    _w = jnp.asarray

    def _L0_attn_setup():
        import jax, jax.numpy as jnp
        import numpy as np
        B, S, HID = (1, 256, 512)
        H, NOPE, ROPE, VD = (32, 128, 64, 128)
        QKD = NOPE + ROPE
        Q_RANK, KV_RANK = (192, 64)
        IDX_H, IDX_D, TOPK = (16, 128, 128)
        EPS, THETA = (1e-05, 10000.0)

        def rmsnorm(x, w):
            return x * jax.lax.rsqrt(jnp.mean(x * x, axis=-1, keepdims=True) + EPS) * w

        def rope_interleaved(x, pos):
            d = x.shape[-1]
            inv_freq = 1.0 / THETA ** (jnp.arange(0, d, 2, dtype=jnp.float32) / d)
            ang = pos[:, None] * inv_freq[None, :]
            cos, sin = (jnp.cos(ang), jnp.sin(ang))
            x2 = x.reshape(*x.shape[:-1], d // 2, 2)
            x0, x1 = (x2[..., 0], x2[..., 1])
            return jnp.stack([x0 * cos - x1 * sin, x1 * cos + x0 * sin], axis=-1).reshape(x.shape)
        key = jax.random.key(seed)
        ks = jax.random.split(key, 12)
        s = 0.02
        return {'hidden_states': jax.random.normal(ks[0], (B, S, HID), jnp.float32), 'q_a_w': jax.random.normal(ks[1], (HID, Q_RANK), jnp.float32) * s, 'q_a_norm_w': jnp.ones((Q_RANK,), jnp.float32), 'q_b_w': jax.random.normal(ks[2], (Q_RANK, H * QKD), jnp.float32) * s, 'kv_a_w': jax.random.normal(ks[3], (HID, KV_RANK + ROPE), jnp.float32) * s, 'kv_a_norm_w': jnp.ones((KV_RANK,), jnp.float32), 'kv_b_w': jax.random.normal(ks[4], (KV_RANK, H * (NOPE + VD)), jnp.float32) * s, 'o_w': jax.random.normal(ks[5], (H * VD, HID), jnp.float32) * s, 'idx_wq_w': jax.random.normal(ks[6], (HID, IDX_H * IDX_D), jnp.float32) * s, 'idx_wk_w': jax.random.normal(ks[7], (HID, IDX_D), jnp.float32) * s, 'idx_weights_w': jax.random.normal(ks[8], (HID, IDX_H), jnp.float32) * s}
    _L0_attn_in = _L0_attn_setup()

    def _L0_ffn_setup():
        import jax, jax.numpy as jnp
        import numpy as np
        B_, S, D_IN, D_OUT = (4, 256, 512, 512)
        N, RANK, ALPHA = (8, 16, 32)
        SCALE = ALPHA / RANK
        key = jax.random.key(seed)
        kx, ka, kb, kw, kbias = jax.random.split(key, 5)
        x = jax.random.normal(kx, (B_, S, D_IN), dtype=jnp.float32)
        lora_A = jax.random.normal(ka, (N, RANK, D_IN), dtype=jnp.float32) * (1.0 / np.sqrt(D_IN))
        lora_B = jax.random.normal(kb, (N, D_OUT, RANK), dtype=jnp.float32) * (1.0 / np.sqrt(RANK))
        W = jax.random.normal(kw, (D_OUT, D_IN), dtype=jnp.float32) * (1.0 / np.sqrt(D_IN))
        bias = jax.random.normal(kbias, (D_OUT,), dtype=jnp.float32) * 0.01
        lora_weights = jnp.full((N,), 1.0 / N, dtype=jnp.float32)
        return {'x': x, 'lora_A': lora_A, 'lora_B': lora_B, 'W': W, 'bias': bias, 'lora_weights': lora_weights}
    _L0_ffn_in = _L0_ffn_setup()

    def _L1_attn_setup():
        import jax, jax.numpy as jnp
        import numpy as np
        import math
        DIM, NH, NKV, HD = (512, 32, 8, 128)
        BLOCK, NBLK, TOPK = (32, 128, 16)

        def apply_rope(x, cos, sin):
            b, l, h, d = x.shape
            xr = x.reshape(b, l, h, d // 2, 2)
            xe, xo = (xr[..., 0], xr[..., 1])
            c = cos[None, :, None, :]
            s = sin[None, :, None, :]
            oe = xe * c - xo * s
            oo = xe * s + xo * c
            return jnp.stack([oe, oo], axis=-1).reshape(b, l, h, d)
        key = jax.random.key(seed)
        ks = jax.random.split(key, 8)
        x = jax.random.normal(ks[0], (1, 1, DIM), dtype=jnp.float32)
        start_pos = 512
        inv_freq = 1.0 / 500000.0 ** (np.arange(0, HD, 2, dtype=np.float32) / HD)
        ang = np.float32(start_pos) * inv_freq
        freqs_cos = jnp.asarray(np.cos(ang))[None, :]
        freqs_sin = jnp.asarray(np.sin(ang))[None, :]
        sc = 0.02
        wq = jax.random.normal(ks[1], (NH * HD, DIM), dtype=jnp.float32) * sc
        wk = jax.random.normal(ks[2], (NKV * HD, DIM), dtype=jnp.float32) * sc
        wv = jax.random.normal(ks[3], (NKV * HD, DIM), dtype=jnp.float32) * sc
        wo = jax.random.normal(ks[4], (DIM, NH * HD), dtype=jnp.float32) * sc
        k_cache = jax.random.normal(ks[5], (NBLK, BLOCK, NKV, HD), dtype=jnp.float32)
        v_cache = jax.random.normal(ks[6], (NBLK, BLOCK, NKV, HD), dtype=jnp.float32)
        block_idx = jnp.sort(jax.random.randint(ks[7], (TOPK,), 0, NBLK, dtype=jnp.int32))
        return {'x': x, 'freqs_cos': freqs_cos, 'freqs_sin': freqs_sin, 'wq': wq, 'wk': wk, 'wv': wv, 'wo': wo, 'k_cache': k_cache, 'v_cache': v_cache, 'block_idx': block_idx}
    _L1_attn_in = _L1_attn_setup()

    def _L1_ffn_setup():
        import jax, jax.numpy as jnp
        import numpy as np
        NF4_CODE = jnp.array([-1.0, -0.6961928009986877, -0.5250730514526367, -0.39491748809814453, -0.28444138169288635, -0.18477343022823334, -0.09105003625154495, 0.0, 0.07958029955625534, 0.16093020141124725, 0.24611230194568634, 0.33791524171829224, 0.44070982933044434, 0.5626170039176941, 0.7229568362236023, 1.0], dtype=jnp.float32)
        BLOCKSIZE = 64

        def nf4_quant_dequant(w):
            shape = w.shape
            flat = w.reshape(-1, BLOCKSIZE)
            absmax = jnp.max(jnp.abs(flat), axis=1, keepdims=True)
            normalized = flat / jnp.where(absmax == 0, 1.0, absmax)
            bounds = (NF4_CODE[:-1] + NF4_CODE[1:]) * 0.5
            idx = jnp.searchsorted(bounds, normalized)
            return (NF4_CODE[idx] * absmax).reshape(shape)
        key = jax.random.key(seed)
        k1, k2, k3, kx = jax.random.split(key, 4)
        D, H = (512, 1376)
        scale = 0.02
        w1 = jax.random.normal(k1, (H, D), jnp.float32) * scale
        w2 = jax.random.normal(k2, (H, D), jnp.float32) * scale
        w3 = jax.random.normal(k3, (D, H), jnp.float32) * scale
        x = jax.random.normal(kx, (2, 256, D), jnp.float32)
        return {'x': x, 'w1': w1, 'w2': w2, 'w3': w3}
    _L1_ffn_in = _L1_ffn_setup()
    _d = {'L0_attn_hidden_states': _L0_attn_in['hidden_states'], 'L0_attn_q_a_w': _L0_attn_in['q_a_w'], 'L0_attn_q_a_norm_w': _L0_attn_in['q_a_norm_w'], 'L0_attn_q_b_w': _L0_attn_in['q_b_w'], 'L0_attn_kv_a_w': _L0_attn_in['kv_a_w'], 'L0_attn_kv_a_norm_w': _L0_attn_in['kv_a_norm_w'], 'L0_attn_kv_b_w': _L0_attn_in['kv_b_w'], 'L0_attn_o_w': _L0_attn_in['o_w'], 'L0_attn_idx_wq_w': _L0_attn_in['idx_wq_w'], 'L0_attn_idx_wk_w': _L0_attn_in['idx_wk_w'], 'L0_attn_idx_weights_w': _L0_attn_in['idx_weights_w'], 'L0_ffn_lora_A': _L0_ffn_in['lora_A'], 'L0_ffn_lora_B': _L0_ffn_in['lora_B'], 'L0_ffn_W': _L0_ffn_in['W'], 'L0_ffn_bias': _L0_ffn_in['bias'], 'L0_ffn_lora_weights': _L0_ffn_in['lora_weights'], 'L1_attn_freqs_cos': _L1_attn_in['freqs_cos'], 'L1_attn_freqs_sin': _L1_attn_in['freqs_sin'], 'L1_attn_wq': _L1_attn_in['wq'], 'L1_attn_wk': _L1_attn_in['wk'], 'L1_attn_wv': _L1_attn_in['wv'], 'L1_attn_wo': _L1_attn_in['wo'], 'L1_attn_k_cache': _L1_attn_in['k_cache'], 'L1_attn_v_cache': _L1_attn_in['v_cache'], 'L1_attn_block_idx': _L1_attn_in['block_idx'], 'L1_ffn_w1': _L1_ffn_in['w1'], 'L1_ffn_w2': _L1_ffn_in['w2'], 'L1_ffn_w3': _L1_ffn_in['w3']}
    _x0 = _d['L0_attn_hidden_states']
    _d['L0_attn_hidden_states'] = jax.random.normal(jax.random.fold_in(jax.random.key(seed), 1), (4, 256, 512), dtype=_x0.dtype)
    del _x0
    return _d

def reference(L0_attn_hidden_states, L0_attn_q_a_w, L0_attn_q_a_norm_w, L0_attn_q_b_w, L0_attn_kv_a_w, L0_attn_kv_a_norm_w, L0_attn_kv_b_w, L0_attn_o_w, L0_attn_idx_wq_w, L0_attn_idx_wk_w, L0_attn_idx_weights_w, L0_ffn_lora_A, L0_ffn_lora_B, L0_ffn_W, L0_ffn_bias, L0_ffn_lora_weights, L1_attn_freqs_cos, L1_attn_freqs_sin, L1_attn_wq, L1_attn_wk, L1_attn_wv, L1_attn_wo, L1_attn_k_cache, L1_attn_v_cache, L1_attn_block_idx, L1_ffn_w1, L1_ffn_w2, L1_ffn_w3):

    def _L0_attn_ref(hidden_states, q_a_w, q_a_norm_w, q_b_w, kv_a_w, kv_a_norm_w, kv_b_w, o_w, idx_wq_w, idx_wk_w, idx_weights_w):
        import jax, jax.numpy as jnp
        import numpy as np
        B, S, HID = (1, 256, 512)
        H, NOPE, ROPE, VD = (32, 128, 64, 128)
        QKD = NOPE + ROPE
        Q_RANK, KV_RANK = (192, 64)
        IDX_H, IDX_D, TOPK = (16, 128, 128)
        EPS, THETA = (1e-05, 10000.0)

        def rmsnorm(x, w):
            return x * jax.lax.rsqrt(jnp.mean(x * x, axis=-1, keepdims=True) + EPS) * w

        def rope_interleaved(x, pos):
            d = x.shape[-1]
            inv_freq = 1.0 / THETA ** (jnp.arange(0, d, 2, dtype=jnp.float32) / d)
            ang = pos[:, None] * inv_freq[None, :]
            cos, sin = (jnp.cos(ang), jnp.sin(ang))
            x2 = x.reshape(*x.shape[:-1], d // 2, 2)
            x0, x1 = (x2[..., 0], x2[..., 1])
            return jnp.stack([x0 * cos - x1 * sin, x1 * cos + x0 * sin], axis=-1).reshape(x.shape)
        b, s, _ = hidden_states.shape
        pos = jnp.arange(s, dtype=jnp.float32)
        q_lat = rmsnorm(hidden_states @ q_a_w, q_a_norm_w)
        q = (q_lat @ q_b_w).reshape(b, s, H, QKD).transpose(0, 2, 1, 3)
        q_nope, q_pe = (q[..., :NOPE], q[..., NOPE:])
        ckv = hidden_states @ kv_a_w
        kv_lat, k_pe = (ckv[..., :KV_RANK], ckv[..., KV_RANK:])
        kv = (rmsnorm(kv_lat, kv_a_norm_w) @ kv_b_w).reshape(b, s, H, NOPE + VD).transpose(0, 2, 1, 3)
        k_nope, v = (kv[..., :NOPE], kv[..., NOPE:])
        q_pe = rope_interleaved(q_pe, pos)
        k_pe = rope_interleaved(k_pe[:, None, :, :], pos)
        scores = (jnp.einsum('bhqd,bhkd->bhqk', q_nope, k_nope) + jnp.einsum('bhqd,bhkd->bhqk', q_pe, k_pe)) * QKD ** (-0.5)
        iq = (hidden_states @ idx_wq_w).reshape(b, s, IDX_H, IDX_D)
        ik = hidden_states @ idx_wk_w
        iw = hidden_states @ idx_weights_w * IDX_H ** (-0.5)
        idx_scores = jnp.einsum('bqn,bnqk->bqk', iw, jax.nn.relu(jnp.einsum('bqnd,bkd->bnqk', iq, ik))) * IDX_D ** (-0.5)
        causal = pos[:, None] >= pos[None, :]
        idx_scores = jnp.where(causal, idx_scores, -jnp.inf)
        _, topk_idx = jax.lax.top_k(idx_scores, TOPK)
        bi = jnp.arange(b)[:, None, None]
        qi = jnp.arange(s)[None, :, None]
        topk_mask = jnp.zeros((b, s, s), bool).at[bi, qi, topk_idx].set(True)
        mask = topk_mask & causal
        scores = jnp.where(mask[:, None], scores, -jnp.inf)
        attn = jax.nn.softmax(scores, axis=-1)
        out = jnp.einsum('bhqk,bhkd->bqhd', attn, v).reshape(b, s, H * VD)
        return out @ o_w

    def _L0_ffn_ref(x, lora_A, lora_B, W, bias, lora_weights):
        import jax, jax.numpy as jnp
        import numpy as np
        B_, S, D_IN, D_OUT = (4, 256, 512, 512)
        N, RANK, ALPHA = (8, 16, 32)
        SCALE = ALPHA / RANK
        h = jnp.einsum('bsd,nrd->nbsr', x, lora_A)
        coef = (SCALE * lora_weights)[:, None, None]
        lora_out = jnp.einsum('nbsr,nor->bso', h, lora_B * coef)
        base = jnp.einsum('bsd,od->bso', x, W) + bias
        return base + lora_out

    def _L1_attn_ref(x, freqs_cos, freqs_sin, wq, wk, wv, wo, k_cache, v_cache, block_idx):
        import jax, jax.numpy as jnp
        import numpy as np
        import math
        DIM, NH, NKV, HD = (512, 32, 8, 128)
        BLOCK, NBLK, TOPK = (32, 128, 16)

        def apply_rope(x, cos, sin):
            b, l, h, d = x.shape
            xr = x.reshape(b, l, h, d // 2, 2)
            xe, xo = (xr[..., 0], xr[..., 1])
            c = cos[None, :, None, :]
            s = sin[None, :, None, :]
            oe = xe * c - xo * s
            oo = xe * s + xo * c
            return jnp.stack([oe, oo], axis=-1).reshape(b, l, h, d)
        b, l, _ = x.shape
        n_rep = NH // NKV
        q = (x @ wq.T).reshape(b, l, NH, HD)
        k = (x @ wk.T).reshape(b, l, NKV, HD)
        v = (x @ wv.T).reshape(b, l, NKV, HD)
        q = apply_rope(q, freqs_cos, freqs_sin)
        k = apply_rope(k, freqs_cos, freqs_sin)
        k_sel = k_cache[block_idx].reshape(-1, NKV, HD)
        v_sel = v_cache[block_idx].reshape(-1, NKV, HD)
        k_full = jnp.concatenate([k_sel, k[0]], axis=0)
        v_full = jnp.concatenate([v_sel, v[0]], axis=0)
        k_full = jnp.repeat(k_full.transpose(1, 0, 2)[None], n_rep, axis=1)
        v_full = jnp.repeat(v_full.transpose(1, 0, 2)[None], n_rep, axis=1)
        qh = q.transpose(0, 2, 1, 3)
        scores = jnp.einsum('bhld,bhtd->bhlt', qh, k_full) / math.sqrt(HD)
        attn = jax.nn.softmax(scores, axis=-1)
        out = jnp.einsum('bhlt,bhtd->bhld', attn, v_full)
        out = out.transpose(0, 2, 1, 3).reshape(b, l, NH * HD)
        return out @ wo.T

    def _L1_ffn_ref(x, w1, w2, w3):
        import jax, jax.numpy as jnp
        import numpy as np
        NF4_CODE = jnp.array([-1.0, -0.6961928009986877, -0.5250730514526367, -0.39491748809814453, -0.28444138169288635, -0.18477343022823334, -0.09105003625154495, 0.0, 0.07958029955625534, 0.16093020141124725, 0.24611230194568634, 0.33791524171829224, 0.44070982933044434, 0.5626170039176941, 0.7229568362236023, 1.0], dtype=jnp.float32)
        BLOCKSIZE = 64

        def nf4_quant_dequant(w):
            shape = w.shape
            flat = w.reshape(-1, BLOCKSIZE)
            absmax = jnp.max(jnp.abs(flat), axis=1, keepdims=True)
            normalized = flat / jnp.where(absmax == 0, 1.0, absmax)
            bounds = (NF4_CODE[:-1] + NF4_CODE[1:]) * 0.5
            idx = jnp.searchsorted(bounds, normalized)
            return (NF4_CODE[idx] * absmax).reshape(shape)
        dq1 = nf4_quant_dequant(w1)
        dq2 = nf4_quant_dequant(w2)
        dq3 = nf4_quant_dequant(w3)
        gate = jnp.einsum('bsd,hd->bsh', x, dq1)
        up = jnp.einsum('bsd,hd->bsh', x, dq2)
        h = jax.nn.silu(gate) * up
        return jnp.einsum('bsh,dh->bsd', h, dq3)
    x = L0_attn_hidden_states
    x = x + 0.5 * _L0_ffn_ref(_layernorm(x, axis=-1), L0_ffn_lora_A, L0_ffn_lora_B, L0_ffn_W, L0_ffn_bias, L0_ffn_lora_weights)
    x = x + _L0_attn_ref(_layernorm(x, axis=-1), L0_attn_q_a_w, L0_attn_q_a_norm_w, L0_attn_q_b_w, L0_attn_kv_a_w, L0_attn_kv_a_norm_w, L0_attn_kv_b_w, L0_attn_o_w, L0_attn_idx_wq_w, L0_attn_idx_wk_w, L0_attn_idx_weights_w)
    x = x + 0.5 * _L0_ffn_ref(_layernorm(x, axis=-1), L0_ffn_lora_A, L0_ffn_lora_B, L0_ffn_W, L0_ffn_bias, L0_ffn_lora_weights)
    x = x + 0.5 * _L1_ffn_ref(_layernorm(x, axis=-1), L1_ffn_w1, L1_ffn_w2, L1_ffn_w3)
    x = x + _L1_attn_ref(_layernorm(x, axis=-1), L1_attn_freqs_cos, L1_attn_freqs_sin, L1_attn_wq, L1_attn_wk, L1_attn_wv, L1_attn_wo, L1_attn_k_cache, L1_attn_v_cache, L1_attn_block_idx)
    x = x + 0.5 * _L1_ffn_ref(_layernorm(x, axis=-1), L1_ffn_w1, L1_ffn_w2, L1_ffn_w3)
    return x

_drawn_inputs = setup_inputs


def setup_inputs(seed=0):
    import zlib

    import numpy as np

    out = dict(_drawn_inputs(seed))
    spreads = {'L0_attn_q_a_norm_w': (1.0, 0.6),
     'L0_attn_kv_a_norm_w': (1.0, 0.6),
     'L0_ffn_lora_weights': (0.125, 0.2)}
    factors = {'L0_attn_q_a_w': 8.0,
     'L0_attn_q_b_w': 8.0,
     'L0_attn_idx_wq_w': 8.0,
     'L0_attn_idx_wk_w': 8.0,
     'L0_attn_idx_weights_w': 8.0,
     'L0_ffn_bias': 8.0,
     'L1_attn_freqs_cos': 5.607,
     'L1_attn_freqs_sin': 8.0,
     'L1_attn_wq': 4.69,
     'L1_attn_wk': 8.0,
     'L1_attn_wv': 8.0,
     'L1_attn_k_cache': 4.669}
    for name, (base, spread) in spreads.items():
        noise = np.random.default_rng([zlib.crc32(name.encode()), seed]).standard_normal(out[name].shape)
        drawn = base * np.exp(spread * noise) if base else spread * noise
        out[name] = jnp.asarray(drawn.astype(out[name].dtype))
    for name, factor in factors.items():
        out[name] = (out[name] * factor).astype(out[name].dtype)
    return out
```

```python
from contextlib import ExitStack

import numpy as np

import concourse.bass as bass
from concourse import mybir

F32 = mybir.dt.float32
F32R = mybir.dt.float32r
BF16 = mybir.dt.bfloat16
I32 = mybir.dt.int32
ALU = mybir.AluOpType
ACT = mybir.ActivationFunctionType
AX_X = mybir.AxisListType.X

P = 128
D = 512
KT = D // P
B, S = 4, 256
T = B * S
TT = T // P
EPS = 1e-5
NEG = -1e30

H0, NOPE, ROPE, VD = 32, 128, 64, 128
Q_RANK, KV_RANK = 192, 64
IDX_H, IDX_D, TOPK = 16, 128, 128
SCALE0 = float(NOPE + ROPE) ** -0.5
THETA = 10000.0
PROJ = Q_RANK + KV_RANK + ROPE + IDX_D + IDX_H
G0 = 4
NG0 = H0 // G0
R_QN, R_KK, R_KV, R_OW, R_PE = G0 * 256, G0 * 64, G0 * 64, G0 * D, G0 * 128
R0 = R_QN + R_KK + R_KV + R_OW + R_PE

LORA_N, LORA_R, ALPHA = 8, 16, 32

NKV, HD, REP = 8, 128, 4
BLOCK, NBLK, NSEL = 32, 128, 16
CT = NSEL * BLOCK // P
NKT = CT + S // P
NKEY = NKT * P
SCALE1 = float(HD) ** -0.5
WG = REP * HD + 2 * HD

FH = 1376
FC = (FH + P - 1) // P
FHP = FC * P
QB = 64
NF4 = np.array([-1.0, -0.6961928009986877, -0.5250730514526367, -0.39491748809814453, -0.28444138169288635,
                -0.18477343022823334, -0.09105003625154495, 0.0, 0.07958029955625534, 0.16093020141124725,
                0.24611230194568634, 0.33791524171829224, 0.44070982933044434, 0.5626170039176941,
                0.7229568362236023, 1.0], np.float32)
NF4_BOUNDS = (NF4[:-1] + NF4[1:]) * np.float32(0.5)
NF4_STEPS = NF4[1:] - NF4[:-1]
STEEP = 2.0 ** 60
FLAT = FH * D // P
QC = FLAT // 2

SWAP16 = [(i + 16) % 32 for i in range(32)]


class Chip:
    pass


def passes(pe, out, pairs, start=True, stop=True):
    n = len(pairs)
    for i, (w, x) in enumerate(pairs):
        last = pe.matmul(out, w, x, start=start and i == 0, stop=stop and i == n - 1)
    return last


def three(wh, wl, xh, xl):
    return [(wh, xh), (wh, xl), (wl, xh)]


def f32(ap):
    return ap.bitcast(F32)


class Norm:

    def __init__(self, c, ctx, name):
        self.c = c
        nc = c.nc
        sem = lambda n: c.sem(f"{name}_{n}")
        self.stats_done, self.stats_chain = sem("stats_done"), sem("stats_chain")
        self.var_ready, self.std_ready, self.rstd_chain = sem("var_ready"), sem("std_ready"), sem("rstd_chain")
        self.z_ready, self.z_turned = sem("z_ready"), sem("z_turned")
        self.hi_done, self.lo_done = sem("hi_done"), sem("lo_done")
        sb = lambda n, s, d=F32: ctx.enter_context(nc.sbuf_tensor(f"{name}_{n}", s, d))
        self.stats, self.mv = sb("stats", [P, TT, 6]), sb("mv", [P, TT, 2])
        self.tmp = sb("tmp", [P, 5, TT])
        self.z = sb("z", [P, 2, D])

    def vector(self, dve, after=lambda t: None):
        c, nc = self.c, self.c.nc
        for t in range(TT):
            nc.vector.bn_stats(self.stats[:, t, :], c.X[:, t, :]).then_inc(self.stats_done, 1)
        for t in range(TT):
            dve.wait_ge(self.stats_done, t + 1)
            nc.vector.bn_aggr(self.mv[:, t, :], self.stats[:, t, :]).then_inc(self.stats_chain, 1)
        dve.wait_ge(self.stats_chain, TT)
        ve, std, r0, a, rstd = (self.tmp[:, i, :] for i in range(5))
        nc.vector.tensor_scalar(ve, self.mv[:, :, 1], EPS, None, ALU.add).then_inc(self.var_ready, 1)
        dve.wait_ge(self.std_ready, 1)
        newton(nc, dve, self.rstd_chain, ve, std, r0, a, rstd)
        for t in range(TT):
            if t >= 2:
                dve.wait_ge(self.z_turned, t - 1)
            nc.vector.tensor_scalar(self.z[:, t % 2, :], c.X[:, t, :], self.mv[:, t, 0:1], rstd[:, t:t + 1],
                                    ALU.subtract, ALU.mult).then_inc(self.z_ready, 1)
            if t:
                self.low(dve, t - 1)
                after(t - 1)
        self.low(dve, TT - 1)
        after(TT - 1)

    def low(self, dve, t):
        c = self.c
        cols = slice(t * P, (t + 1) * P)
        dve.wait_ge(self.hi_done, t + 1)
        c.nc.vector.tensor_tensor(c.ZL[:, :, cols], c.bank(t % 2).rearrange("p (k n) -> p k n", k=KT),
                                  f32(c.ZH[:, :, cols]), ALU.subtract).then_inc(self.lo_done, 1)

    def scalar_std(self, act):
        act.wait_ge(self.var_ready, 1)
        self.c.nc.scalar.activation(self.tmp[:, 1, :], self.tmp[:, 0, :], ACT.Sqrt).then_inc(self.std_ready, 1)

    def scalar_hi(self, act, t):
        c = self.c
        act.wait_ge(self.z_turned, t + 1)
        c.nc.scalar.activation(c.ZH[:, :, t * P:(t + 1) * P], c.bank(t % 2).rearrange("p (k n) -> p k n", k=KT),
                               ACT.Copy).then_inc(self.hi_done, 1)

    def turn(self, pe, t):
        c = self.c
        pe.wait_ge(self.z_ready, t + 1)
        if t >= 2:
            pe.wait_ge(self.lo_done, t - 1)
        for k in range(KT):
            last = pe.transpose(c.bank(t % 2)[:, k * P:(k + 1) * P], self.z[:, t % 2, k * P:(k + 1) * P], c.ident[:, :])
        last.then_inc(self.z_turned, 1)


def newton(nc, dve, chain, v, std, r0, a, rstd):
    nc.vector.reciprocal(r0, std).then_inc(chain, 1)
    dve.wait_ge(chain, 1)
    nc.vector.tensor_tensor(a, v, r0, ALU.mult).then_inc(chain, 1)
    dve.wait_ge(chain, 2)
    nc.vector.tensor_tensor(rstd, a, r0, ALU.mult).then_inc(chain, 1)
    dve.wait_ge(chain, 3)
    nc.vector.tensor_scalar(a, rstd, -0.5, 1.5, ALU.mult, ALU.add).then_inc(chain, 1)
    dve.wait_ge(chain, 4)
    nc.vector.tensor_tensor(rstd, r0, a, ALU.mult).then_inc(chain, 1)
    dve.wait_ge(chain, 5)


def setup(c):
    nc = c.nc
    with ExitStack() as ctx:
        sb = lambda n, s, d=F32: ctx.enter_context(nc.sbuf_tensor(n, s, d))
        w_raw, la, lb, lw = sb("w_raw", [P, KT, D]), sb("lora_a", [P, D]), sb("lora_b", [P, D]), sb("lora_w", [P, 1])
        loaded, ident_made, scaled, merged = c.sem("su_loaded"), c.sem("su_ident"), c.sem("su_scaled"), c.sem("su_mm")
        summed, hi_done, lo_done = c.sem("su_summed"), c.sem("su_hi"), c.sem("su_lo")
        x_loaded = c.sem("su_x")
        with nc.Block() as block:

            @block.sync
            def _(sp):
                sp.dma_start(la[:, :], c.ins["lora_a"]).then_inc(loaded, 16)
                sp.dma_start(lb[:, :], c.ins["lora_b"]).then_inc(loaded, 16)
                sp.dma_start(lw[:, :], c.ins["lora_w"].unsqueeze(1).broadcast_to([LORA_N, LORA_R]).unsqueeze(2)
                             ).then_inc(loaded, 16)
                sp.dma_start(w_raw[:, :, :], c.ins["w0"].rearrange("(k p) n -> p k n", p=P)).then_inc(loaded, 16)
                sp.dma_start(c.X[:, :, :], c.ins["x"].rearrange("(t p) n -> p t n", p=P)).then_inc(x_loaded, 16)
                sp.dma_start(c.bias[:, :], c.ins["bias"].partition_broadcast(P)).then_inc(x_loaded, 16)
                sp.dma_start(c.nf_bias[:, :], c.ins["nf_bias"].partition_broadcast(P)).then_inc(x_loaded, 16)
                sp.wait_ge(x_loaded, 48)

            @block.gpsimd
            def _(pool):
                nc.gpsimd.memset(c.ident[:, :], 0.0).then_inc(ident_made, 1)
                pool.wait_ge(ident_made, 1)
                nc.gpsimd.affine_select(out=c.ident[:, :], in_=c.ident[:, :], compare_op=ALU.not_equal, fill=1.0,
                                        base=0, pattern=[[-1, P]], channel_multiplier=1).then_inc(ident_made, 1)
                nc.gpsimd.memset(c.zero_bf[:, :], 0.0).then_inc(ident_made, 1)
                pool.wait_ge(ident_made, 2)
                nc.gpsimd.tensor_copy(c.ident_bf[:, :], c.ident[:, :]).then_inc(ident_made, 1)

            @block.vector
            def _(dve):
                dve.wait_ge(loaded, 64)
                nc.vector.tensor_scalar(lb[:, :], lb[:, :], lw[:, 0:1], float(ALPHA) / LORA_R, ALU.mult, ALU.mult
                                        ).then_inc(scaled, 1)
                for k in range(KT):
                    dve.wait_ge(merged, k + 1)
                    nc.vector.tensor_tensor(w_raw[:, k, :], c.bank(k), w_raw[:, k, :], ALU.add).then_inc(summed, 1)
                dve.wait_ge(hi_done, 1)
                nc.vector.tensor_tensor(c.W0L[:, :, :], w_raw[:, :, :], f32(c.W0H[:, :, :]), ALU.subtract
                                        ).then_inc(lo_done, 1)

            @block.scalar
            def _(act):
                act.wait_ge(summed, KT)
                nc.scalar.activation(c.W0H[:, :, :], w_raw[:, :, :], ACT.Copy).then_inc(hi_done, 1)

            @block.tensor
            def _(pe):
                pe.wait_ge(scaled, 1)
                for k in range(KT):
                    pe.matmul(c.bank(k), la[:, k * P:(k + 1) * P], lb[:, :], start=True, stop=True).then_inc(merged, 1)


def dequant(c):
    nc = c.nc
    nb = QC // QB
    steps = len(NF4_STEPS)
    with ExitStack() as ctx:
        sb = lambda n, s, d=F32: ctx.enter_context(nc.sbuf_tensor(n, s, d))
        w, v, acc = sb("dq_w", [P, QC]), sb("dq_v", [P, QC]), sb("dq_acc", [P, QC])
        rel = sb("dq_rel", [P, 3, QC])
        amax, safe, inv = sb("dq_amax", [P, nb]), sb("dq_safe", [P, nb]), sb("dq_inv", [P, nb])
        zeros = sb("dq_zeros", [P, D])
        loaded, chain = c.sem("dq_loaded"), c.sem("dq_chain")
        v_ready, rel_ready = c.sem("dq_v"), c.sem("dq_rel")
        stored, zeroed, pad = c.sem("dq_stored"), c.sem("dq_zeroed"), c.sem("dq_pad")
        blocks = lambda ap: ap.rearrange("p (b n) -> p b n", n=QB)
        wide = lambda ap: ap.unsqueeze(2).broadcast_to([P, nb, QB])
        PER = 3 + 1 + steps + 1
        with nc.Block() as block:

            @block.sync
            def _(sp):
                sp.wait_ge(zeroed, 1)
                for k in range(2):
                    sp.dma_start(c.dq12[k * FHP + FH:(k + 1) * FHP, :], zeros[0:FHP - FH, :]).then_inc(pad, 16)
                for k in range(KT):
                    sp.dma_start(c.dq3[k * P:(k + 1) * P, FH:FHP], zeros[:, 0:FHP - FH]).then_inc(pad, 16)
                sp.wait_ge(pad, 16 * (2 + KT))

                def load(n):
                    m, i = n // 2, n % 2
                    src = c.ins[("w1", "w2", "w3")[m]].rearrange("a b -> (a b)").rearrange("(p f) -> p f", p=P)
                    sp.wait_ge(v_ready, n + 1)
                    sp.dma_start(w[:, :], src[:, i * QC:(i + 1) * QC]).then_inc(loaded, 16)

                load(0)
                for n in range(6):
                    m, i = n // 2, n % 2
                    if n + 1 < 6:
                        load(n + 1)
                    sp.wait_ge(chain, (n + 2) * PER)
                    if m < 2:
                        flat = c.dq12[m * FHP:m * FHP + FH, :].rearrange("a b -> (a b)")
                        sp.dma_start(flat.rearrange("(p f) -> p f", p=P)[:, i * QC:(i + 1) * QC], acc[:, :]
                                     ).then_inc(stored, 16)
                    else:
                        sp.dma_start(c.dq3[:, 0:FH].rearrange("(p e) n -> p e n", e=4)[:, i * 2:i * 2 + 2, :],
                                     acc[:, :].rearrange("p (e n) -> p e n", e=2)).then_inc(stored, 16)
                sp.wait_ge(stored, 16 * 7)

            @block.gpsimd
            def _(pool):
                nc.gpsimd.memset(zeros[:, :], 0.0).then_inc(zeroed, 1)

            @block.scalar
            def _(act):
                with act.Fori(0, 6) as n:
                    act.wait_ge(v_ready, n + 2)
                    for s in range(steps):
                        act.wait_ge(chain, n * PER + PER + 2 + s if s >= 3 else n * PER + 2 + s + steps)
                        nc.scalar.activation(rel[:, s % 3, :], v[:, :], ACT.Relu,
                                             bias=c.nf_bias[:, s:s + 1], scale=STEEP).then_inc(rel_ready, 1)

            @block.vector
            def _(dve):
                dve.sem_inc(v_ready, 1)
                dve.sem_inc(stored, 16)
                dve.sem_inc(chain, PER)
                dve.sem_inc(rel_ready, 1)
                with dve.Fori(0, 6) as n:
                    base = n * PER + PER
                    dve.wait_ge(loaded, n * 16 + 16)
                    dve.wait_ge(chain, base)
                    nc.vector.tensor_reduce(amax[:, :], blocks(w[:, :]), AX_X, ALU.max, apply_absolute_value=True
                                            ).then_inc(chain, 1)
                    dve.wait_ge(chain, base + 1)
                    nc.vector.tensor_scalar(safe[:, :], amax[:, :], 1e-37, None, ALU.max).then_inc(chain, 1)
                    dve.wait_ge(chain, base + 2)
                    nc.vector.reciprocal(inv[:, :], safe[:, :]).then_inc(chain, 1)
                    dve.wait_ge(chain, base + 3)
                    dve.wait_ge(rel_ready, n * steps + 1)
                    nc.vector.tensor_tensor(blocks(v[:, :]), blocks(w[:, :]), wide(inv[:, :]), ALU.mult
                                            ).then_inc(v_ready, 1)
                    dve.wait_ge(stored, n * 16 + 16)
                    nc.vector.memset(acc[:, :], float(NF4[0])).then_inc(chain, 1)
                    for s in range(steps):
                        dve.wait_ge(chain, base + 4 + s)
                        dve.wait_ge(rel_ready, n * steps + s + 2)
                        nc.vector.scalar_tensor_tensor(acc[:, :], rel[:, s % 3, :], float(NF4_STEPS[s]), acc[:, :],
                                                       ALU.min, ALU.add).then_inc(chain, 1)
                    dve.wait_ge(chain, base + 4 + steps)
                    nc.vector.tensor_tensor(blocks(acc[:, :]), blocks(acc[:, :]), wide(amax[:, :]), ALU.mult
                                            ).then_inc(chain, 1)


def turn_weights(c):
    nc = c.nc
    with ExitStack() as ctx:
        sb = lambda n, s, d=F32: ctx.enter_context(nc.sbuf_tensor(n, s, d))
        rows, w3c, out = sb("tw_rows", [P, 2, D]), sb("tw_w3", [P, KT, P]), sb("tw_out", [P, 3, D])
        loaded, turned, copied, stored = c.sem("tw_loaded"), c.sem("tw_turned"), c.sem("tw_copied"), c.sem("tw_stored")
        with nc.Block() as block:

            @block.sync
            def _(sp):
                def load(i):
                    sp.wait_ge(turned, i + 1)
                    sp.dma_start(rows[:, :, :], c.dq12.rearrange("(m h) n -> h m n", m=2)[bass.ds(i * P, P), :, :]
                                 ).then_inc(loaded, 16)
                    sp.dma_start(w3c[:, :, :], c.dq3.rearrange("(k p) h -> p k h", p=P)[:, :, bass.ds(i * P, P)]
                                 ).then_inc(loaded, 16)

                def keep(i):
                    sp.wait_ge(copied, i * 3 + 3)
                    sp.dma_start(c.wd[bass.ds(i, 1), :, :].rearrange("o p n -> (o p) n"),
                                 out[:, :, :].rearrange("p m n -> p (m n)")).then_inc(stored, 16)

                sp.sem_inc(stored, 16)
                load(0)
                with sp.Fori(0, FC - 1) as i:
                    load(i + 1)
                    keep(i)
                keep(FC - 1)
                sp.wait_ge(stored, 16 * FC + 16)

            @block.tensor
            def _(pe):
                pe.sem_inc(turned, 1)
                with pe.Fori(0, FC) as i:
                    pe.wait_ge(loaded, i * 32 + 32)
                    pe.wait_ge(stored, i * 16 + 16)
                    for m in range(3):
                        for k in range(KT):
                            src = rows[:, m, k * P:(k + 1) * P] if m < 2 else w3c[:, k, :]
                            last = pe.transpose(c.bank(m)[:, k * P:(k + 1) * P], src, c.ident[:, :])
                    last.then_inc(turned, 1)

            @block.scalar
            def _(act):
                with act.Fori(0, FC) as i:
                    act.wait_ge(turned, i + 2)
                    act.wait_ge(stored, i * 16 + 16)
                    nc.scalar.activation(out[:, 0, :], c.bank(0), ACT.Copy).then_inc(copied, 1)
                    nc.scalar.activation(out[:, 1, :], c.bank(1), ACT.Copy).then_inc(copied, 1)

            @block.vector
            def _(dve):
                with dve.Fori(0, FC) as i:
                    dve.wait_ge(turned, i + 2)
                    dve.wait_ge(stored, i * 16 + 16)
                    nc.vector.tensor_copy(out[:, 2, :], c.bank(2)).then_inc(copied, 1)


def ffn0(c, name):
    nc = c.nc
    with ExitStack() as ctx:
        norm = Norm(c, ctx, name)
        product, biased, added = c.sem(f"{name}_product"), c.sem(f"{name}_biased"), c.sem(f"{name}_added")
        with nc.Block() as block:

            @block.tensor
            def _(pe):
                def product_of(t):
                    pe.wait_ge(norm.lo_done, t + 1)
                    if t >= 4:
                        pe.wait_ge(added, t - 3)
                    pairs = []
                    for k in range(KT):
                        zh, zl = (z[:, k, t * P:(t + 1) * P] for z in (c.ZH, c.ZL))
                        pairs += three(zh, zl, c.W0H[:, k, :], c.W0L[:, k, :])
                    passes(pe, c.bank(2 + t % 4), pairs).then_inc(product, 1)

                for t in range(TT):
                    norm.turn(pe, t)
                    if t:
                        product_of(t - 1)
                product_of(TT - 1)

            @block.scalar
            def _(act):
                norm.scalar_std(act)
                for t in range(TT):
                    norm.scalar_hi(act, t)

            @block.vector
            def _(dve):
                def add(t):
                    dve.wait_ge(product, t + 1)
                    dve.wait_ge(biased, t + 1)
                    nc.vector.scalar_tensor_tensor(c.X[:, t, :], c.bank(2 + t % 4), 0.5, c.X[:, t, :],
                                                   ALU.mult, ALU.add).then_inc(added, 1)

                def after(t):
                    dve.wait_ge(norm.z_ready, t + 1)
                    nc.vector.scalar_tensor_tensor(c.X[:, t, :], c.bias[:, :], 0.5, c.X[:, t, :],
                                                   ALU.mult, ALU.add).then_inc(biased, 1)
                    if t >= 2:
                        add(t - 2)

                norm.vector(dve, after)
                add(TT - 2)
                add(TT - 1)


def ffn1(c, name):
    nc = c.nc
    HALF = T // 2
    with ExitStack() as ctx:
        norm = Norm(c, ctx, name)
        sb = lambda n, s, d=F32: ctx.enter_context(nc.sbuf_tensor(f"{name}_{n}", s, d))
        raw = sb("raw", [P, 2, 3, D])
        wh, wl = sb("wh", [P, 2, 3, D], F32R), sb("wl", [P, 2, 3, D], F32R)
        act_g, h = sb("silu", [P, 2, D]), sb("h", [P, 2, D])
        hh, hl = sb("hh", [P, 2, D], F32R), sb("hl", [P, 2, D], F32R)
        sem = lambda n: c.sem(f"{name}_{n}")
        loaded = [sem("loaded0"), sem("loaded1")]
        w_hi, w_lo, gated, silu_done = sem("w_hi"), sem("w_lo"), sem("gated"), sem("silu")
        h_done, h_hi, h_lo, down, summed, added = (sem("h"), sem("h_hi"), sem("h_lo"), sem("down"), sem("summed"),
                                                   sem("added"))
        gate = lambda p: c.bank(p)
        up = lambda p: c.bank(2 + p)
        accs = [c.bank(4 + t) for t in range(4)]
        CH = 2 * FC

        def chunks(eng, f, half):
            first = half * FC
            with eng.Fori(0, FC // 2) as i:
                for e in range(2):
                    f(i * 2 + (first + e), (first + e) % 2, i + (first + e) // 2)
            last = first + FC - 1
            f(last, last % 2, last // 2)

        with nc.Block() as block:

            @block.sync
            def _(sp):
                def load(n, par, half):
                    sp.wait_ge(w_lo, n + 1)
                    sp.dma_start(raw[:, par, :, :].rearrange("p m n -> p (m n)"),
                                 c.wd[bass.ds(n - half * FC, 1), :, :].rearrange("o p n -> (o p) n")).then_inc(loaded[par], 16)
                for half in range(2):
                    chunks(sp, lambda n, par, nth: load(n, par, half), half)

            @block.gpsimd
            def _(pool):
                pool.sem_inc(w_lo, 2)
                def split_low(n, par, nth):
                    pool.wait_ge(w_hi, n + 1)
                    nc.gpsimd.tensor_tensor(wl[:, par, :, :], raw[:, par, :, :], f32(wh[:, par, :, :]), ALU.subtract
                                            ).then_inc(w_lo, 1)
                for half in range(2):
                    chunks(pool, split_low, half)

            @block.tensor
            def _(pe):
                pe.sem_inc(down, 2)
                pe.sem_inc(gated, 2)

                def gate_up(n, par, half):
                    pe.wait_ge(w_lo, n + 3)
                    pe.wait_ge(h_done, n + 1)
                    for m, bank in ((0, gate(par)), (1, up(par))):
                        pairs = []
                        for k in range(KT):
                            w = [x[:, par, m, k * P:(k + 1) * P] for x in (wh, wl)]
                            z = [x[:, k, half * HALF:(half + 1) * HALF] for x in (c.ZH, c.ZL)]
                            pairs += three(*w, *z)
                        last = passes(pe, bank, pairs)
                    last.then_inc(gated, 1)

                def down_of(n, par, stop=False):
                    pe.wait_ge(h_lo, n + 3)
                    for t in range(4):
                        hhl = [x[:, par, t * P:(t + 1) * P] for x in (hh, hl)]
                        last = passes(pe, accs[t], three(*hhl, wh[:, par, 2, :], wl[:, par, 2, :]), start=False, stop=stop)
                    last.then_inc(down, 1)

                for t in range(TT):
                    norm.turn(pe, t)
                pe.wait_ge(norm.lo_done, TT)
                for half in range(2):
                    first = half * FC
                    if half:
                        pe.wait_ge(added, 4)
                    for t in range(4):
                        pe.matmul(accs[t], c.zero_bf[:, 0:P], c.zero_bf[:, :], start=True, stop=False)
                    gate_up(first, first % 2, half)
                    with pe.Fori(0, FC // 2) as i:
                        for e in range(2):
                            gate_up(i * 2 + (first + e + 1), (first + e + 1) % 2, half)
                            down_of(i * 2 + (first + e), (first + e) % 2)
                    down_of(first + FC - 1, (first + FC - 1) % 2, stop=True)

            @block.scalar
            def _(act):
                act.sem_inc(h_hi, 2)
                norm.scalar_std(act)
                for t in range(TT):
                    norm.scalar_hi(act, t)

                def w_split(n, par, nth):
                    act.wait_ge(loaded[par], nth * 16 + 16)
                    act.wait_ge(down, n + 1)
                    nc.scalar.activation(wh[:, par, :, :], raw[:, par, :, :], ACT.Copy).then_inc(w_hi, 1)

                def hidden(n, par):
                    act.wait_ge(gated, n + 3)
                    act.wait_ge(h_done, n + 1)
                    nc.scalar.activation(act_g[:, par, :], gate(par), ACT.Silu).then_inc(silu_done, 1)
                    act.wait_ge(h_done, n + 3)
                    act.wait_ge(down, n + 1)
                    nc.scalar.activation(hh[:, par, :], h[:, par, :], ACT.Copy).then_inc(h_hi, 1)

                w_split(0, 0, 0)
                for half in range(2):
                    first = half * FC
                    def step(n, par, nth):
                        w_split(n + 1, 1 - par, nth + par)
                        hidden(n, par)
                    if half == 0:
                        chunks(act, step, half)
                    else:
                        with act.Fori(0, FC // 2) as i:
                            for e in range(2):
                                step(i * 2 + (first + e), (first + e) % 2, i + (first + e) // 2)
                        hidden(CH - 1, (CH - 1) % 2)

            @block.vector
            def _(dve):
                dve.sem_inc(h_done, 2)
                dve.sem_inc(h_lo, 2)
                norm.vector(dve)

                def hidden(n, par, nth):
                    dve.wait_ge(silu_done, n + 1)
                    dve.wait_ge(h_lo, n + 1)
                    nc.vector.tensor_tensor(h[:, par, :], act_g[:, par, :], up(par), ALU.mult).then_inc(h_done, 1)
                    dve.wait_ge(h_hi, n + 3)
                    nc.vector.tensor_tensor(hl[:, par, :], h[:, par, :], f32(hh[:, par, :]), ALU.subtract
                                            ).then_inc(h_lo, 1)

                for half in range(2):
                    chunks(dve, hidden, half)
                    dve.wait_ge(down, (half + 1) * FC + 2)
                    for t in range(4):
                        x = c.X[:, 4 * half + t, :]
                        nc.vector.scalar_tensor_tensor(x, accs[t], 0.5, x, ALU.mult, ALU.add).then_inc(added, 1)


def latents(c):
    nc = c.nc
    with ExitStack() as ctx:
        norm = Norm(c, ctx, "lt_norm")
        sb = lambda n, s, d=F32: ctx.enter_context(nc.sbuf_tensor(f"lt_{n}", s, d))
        sem = lambda n: c.sem(f"lt_{n}")
        w = sb("w", [P, KT, PROJ])
        wh, wl = sb("wh", [P, KT, PROJ], F32R), sb("wl", [P, KT, PROJ], F32R)
        pj, junk, ss = sb("pj", [P, TT, PROJ]), sb("junk", [P, Q_RANK]), sb("ss", [P, 2, TT])
        qw, kw, cos, sin = sb("qw", [P, Q_RANK]), sb("kw", [P, KV_RANK]), sb("cos", [P, 2, ROPE]), sb("sin", [P, 2, ROPE])
        tmp, u, rot = sb("tmp", [P, 5, 2 * TT]), sb("u", [P, 2, 512]), sb("rot", [P, 2, 2, ROPE])
        w_loaded, w_hi, w_lo, tables = sem("w_loaded"), sem("w_hi"), sem("w_lo"), sem("tables")
        projected, copied, squared, ms_ready, rms_ready, chain = (sem("projected"), sem("copied"), sem("squared"),
                                                                  sem("ms"), sem("rms"), sem("chain"))
        turned_part, u_ready, u_turned, u_hi, u_lo = sem("part"), sem("u"), sem("u_turned"), sem("u_hi"), sem("u_lo")
        v_base, v_hi, iw_done = sem("v"), sem("v_hi"), sem("iw")
        KV0, KP0, IK0, IW0 = Q_RANK, Q_RANK + KV_RANK, Q_RANK + KV_RANK + ROPE, PROJ - IDX_H
        with nc.Block() as block:

            def sums(act, t):
                bank = c.bank(2 + t % 2)
                act.wait_ge(projected, t + 1)
                nc.scalar.activation(pj[:, t, :], bank[:, 0:PROJ], ACT.Copy).then_inc(copied, 1)
                if t:
                    act.wait_ge(squared, 2 * t)
                nc.scalar.activation(junk[:, 0:Q_RANK], bank[:, 0:Q_RANK], ACT.Square,
                                     accum_out=ss[:, 0, t:t + 1]).then_inc(squared, 1)
                act.wait_ge(squared, 2 * t + 1)
                nc.scalar.activation(junk[:, 0:KV_RANK], bank[:, KV0:KP0], ACT.Square,
                                     accum_out=ss[:, 1, t:t + 1]).then_inc(squared, 1)

            @block.sync
            def _(sp):
                sp.dma_start(w[:, :, :], c.ins["proj"].rearrange("(k p) n -> p k n", p=P)).then_inc(w_loaded, 16)
                sp.dma_start(qw[:, :], c.ins["q_norm"].partition_broadcast(P)).then_inc(tables, 16)
                sp.dma_start(kw[:, :], c.ins["kv_norm"].partition_broadcast(P)).then_inc(tables, 16)
                sp.dma_start(cos[:, :, :], c.ins["key_cos"].rearrange("(h p) n -> p h n", p=P)).then_inc(tables, 16)
                sp.dma_start(sin[:, :, :], c.ins["key_sin"].rearrange("(h p) n -> p h n", p=P)).then_inc(tables, 16)

            @block.gpsimd
            def _(pool):
                pool.wait_ge(w_hi, 1)
                nc.gpsimd.tensor_tensor(wl[:, :, :], w[:, :, :], f32(wh[:, :, :]), ALU.subtract).then_inc(w_lo, 1)

            @block.tensor
            def _(pe):
                def project(t):
                    pe.wait_ge(norm.lo_done, t + 1)
                    if t >= 2:
                        pe.wait_ge(squared, 2 * t - 2)
                    pairs = []
                    for k in range(KT):
                        z = [x[:, k, t * P:(t + 1) * P] for x in (c.ZH, c.ZL)]
                        pairs += three(*z, wh[:, k, :], wl[:, k, :])
                    passes(pe, c.bank(2 + t % 2)[:, 0:PROJ], pairs).then_inc(projected, 1)

                for t in range(TT):
                    norm.turn(pe, t)
                    if t == 1:
                        pe.wait_ge(w_lo, 1)
                    if t:
                        project(t - 1)
                project(TT - 1)
                for t in range(TT):
                    pe.wait_ge(u_ready, t + 1)
                    if t >= 2:
                        pe.wait_ge(u_lo, t - 1)
                    for k in range(4):
                        last = pe.transpose(c.bank(4 + t % 2)[:, k * P:(k + 1) * P], u[:, t % 2, k * P:(k + 1) * P],
                                            c.ident[:, :])
                    last.then_inc(u_turned, 1)

            @block.scalar
            def _(act):
                act.wait_ge(w_loaded, 16)
                nc.scalar.activation(wh[:, :, :], w[:, :, :], ACT.Copy).then_inc(w_hi, 1)
                norm.scalar_std(act)
                for t in range(TT):
                    norm.scalar_hi(act, t)
                    if t:
                        sums(act, t - 1)
                sums(act, TT - 1)
                act.wait_ge(ms_ready, 1)
                nc.scalar.activation(tmp[:, 1, :], tmp[:, 0, :], ACT.Sqrt).then_inc(rms_ready, 1)
                for t in range(TT):
                    act.wait_ge(u_turned, t + 1)
                    nc.scalar.activation(c.UH[:, :, t * P:(t + 1) * P],
                                         c.bank(4 + t % 2).rearrange("p (k n) -> p k n", k=4), ACT.Copy
                                         ).then_inc(u_hi, 1)
                act.wait_ge(v_base, TT + 1)
                nc.scalar.activation(c.VH[:, :, :], c.V[:, :, :], ACT.Copy).then_inc(v_hi, 1)

            @block.vector
            def _(dve):
                norm.vector(dve)
                nc.vector.memset(c.V[:, :, :], 0.0).then_inc(v_base, 1)
                dve.wait_ge(squared, 2 * TT)
                ms, rms, r0, a, rinv = (tmp[:, i, :] for i in range(5))
                for i, n in enumerate((Q_RANK, KV_RANK)):
                    nc.vector.tensor_scalar(ms[:, i * TT:(i + 1) * TT], ss[:, i, :], 1.0 / n, EPS, ALU.mult, ALU.add
                                            ).then_inc(ms_part := c.sem(f"lt_ms{i}"), 1)
                    dve.wait_ge(ms_part, 1)
                dve.sem_inc(ms_ready, 1)
                dve.wait_ge(rms_ready, 1)
                newton(nc, dve, chain, ms, rms, r0, a, rinv)
                dve.wait_ge(copied, TT)
                dve.wait_ge(tables, 64)
                nc.vector.tensor_scalar(c.IW[:, :, :], pj[:, :, IW0:PROJ], float(IDX_H) ** -0.5, float(IDX_D) ** -0.5,
                                        ALU.mult, ALU.mult).then_inc(iw_done, 1)
                dve.wait_ge(v_base, 1)

                def u_low(t):
                    dve.wait_ge(u_hi, t + 1)
                    cols = slice(t * P, (t + 1) * P)
                    nc.vector.tensor_tensor(c.UL[:, :, cols], c.bank(4 + t % 2).rearrange("p (k n) -> p k n", k=4),
                                            f32(c.UH[:, :, cols]), ALU.subtract).then_inc(u_lo, 1)

                parts = 0
                for t in range(TT):
                    row, par, x = u[:, t % 2, :], t % 2, pj[:, t, :]
                    if t >= 2:
                        dve.wait_ge(u_turned, t - 1)
                    rq, rk = rinv[:, t:t + 1], rinv[:, TT + t:TT + t + 1]
                    nc.vector.scalar_tensor_tensor(row[:, 0:Q_RANK], x[:, 0:Q_RANK], rq, qw[:, :], ALU.mult, ALU.mult
                                                   ).then_inc(turned_part, 1)
                    nc.vector.scalar_tensor_tensor(row[:, Q_RANK:256], x[:, P:Q_RANK], rq, qw[:, P:Q_RANK],
                                                   ALU.mult, ALU.mult).then_inc(turned_part, 1)
                    nc.vector.scalar_tensor_tensor(row[:, 256:320], x[:, KV0:KP0], rk, kw[:, :], ALU.mult, ALU.mult
                                                   ).then_inc(turned_part, 1)
                    nc.vector.scalar_tensor_tensor(c.V[:, t, 64:128], x[:, KV0:KP0], rk, kw[:, :], ALU.mult, ALU.mult
                                                   ).then_inc(v_base, 1)
                    pe_ = x[:, KP0:IK0]
                    halves = lambda ap: ap.rearrange("p (q s f) -> p q s f", q=2, s=2)
                    r = rot[:, par, :, :]
                    nc.vector.tensor_tensor(r[:, 0, :], pe_, cos[:, par, :], ALU.mult).then_inc(turned_part, 1)
                    for s in range(2):
                        nc.vector.tensor_tensor(halves(r[:, 1, :])[:, :, s, :], halves(pe_)[:, :, 1 - s, :],
                                                halves(sin[:, par, :])[:, :, s, :], ALU.mult).then_inc(turned_part, 1)
                    nc.vector.tensor_copy(row[:, 384:512], x[:, IK0:IW0]).then_inc(turned_part, 1)
                    parts += 7
                    dve.wait_ge(turned_part, parts)
                    nc.vector.tensor_tensor(row[:, 320:384], r[:, 0, :], r[:, 1, :], ALU.add).then_inc(u_ready, 1)
                    if t:
                        u_low(t - 1)
                u_low(TT - 1)
                dve.wait_ge(v_hi, 1)
                nc.vector.tensor_tensor(c.VL[:, :, :], c.V[:, :, :], f32(c.VH[:, :, :]), ALU.subtract).then_inc(v_hi, 1)


def indexer(c):
    nc = c.nc
    with ExitStack() as ctx:
        sb = lambda n, s, d=F32: ctx.enter_context(nc.sbuf_tensor(f"ix_{n}", s, d))
        sem = lambda n: c.sem(f"ix_{n}")
        raw = sb("raw", [P, 2, KT, IDX_D])
        wh, wl = sb("wh", [P, 2, KT, IDX_D], F32R), sb("wl", [P, 2, KT, IDX_D], F32R)
        qh, ql = sb("qh", [P, 2, B * P], F32R), sb("ql", [P, 2, B * P], F32R)
        relu = sb("relu", [P, 2, B, S])
        score, work, same = sb("score", [P, B, S]), sb("work", [P, B, S]), sb("same", [P, B, S])
        max8 = sb("max8", [P, B, 8])
        loaded = [sem("loaded0"), sem("loaded1")]
        w_hi, w_lo, q_done, q_hi, q_lo = ( sem("w_hi"), sem("w_lo"), sem("q"), sem("q_hi"),
                                                  sem("q_lo"))
        scored, relued, summed = sem("scored"), sem("relu"), sem("summed")
        step = sem("step")
        base, masked, found, replaced, compared = sem("base"), sem("masked"), sem("found"), sem("replaced"), sem("same")
        pairs_of_heads = IDX_H // 2

        def heads(eng, f):
            with eng.Fori(0, pairs_of_heads) as i:
                for e in range(2):
                    f(i * 2 + e, e, i)

        with nc.Block() as block:

            @block.sync
            def _(sp):
                def load(n, par, nth):
                    sp.wait_ge(w_lo, n + 1)
                    sp.dma_start(raw[:, par, :, :], c.ins["idx_wq"].rearrange("(k p) n -> p k n", p=P)
                                 [:, :, bass.ds(n * IDX_D, IDX_D)]).then_inc(loaded[par], 16)
                heads(sp, load)

            @block.gpsimd
            def _(pool):
                pool.sem_inc(w_lo, 2)
                nc.gpsimd.memset(c.mask[:, :, :, :], 0.0).then_inc(masked, 1)
                pool.wait_ge(masked, 1)
                nc.gpsimd.affine_select(out=c.mask[:, :, 0, :], in_=c.mask[:, :, 0, :], compare_op=ALU.is_ge, fill=NEG,
                                        base=0, pattern=[[0, B], [-1, S]], channel_multiplier=1).then_inc(masked, 1)

                def w_low(n, par, nth):
                    pool.wait_ge(w_hi, n + 1)
                    nc.gpsimd.tensor_tensor(wl[:, par, :, :], raw[:, par, :, :], f32(wh[:, par, :, :]), ALU.subtract
                                            ).then_inc(w_lo, 1)
                heads(pool, w_low)
                pool.wait_ge(summed, IDX_H * B + 2 * B)
                nc.gpsimd.affine_select(out=work[:, :, :], in_=score[:, :, :], compare_op=ALU.is_ge, fill=NEG,
                                        base=P, pattern=[[0, B], [-1, S]], channel_multiplier=1).then_inc(base, 1)

            @block.tensor
            def _(pe):
                pe.sem_inc(q_done, 2)
                def head(n, par):
                    pe.wait_ge(w_lo, n + 3)
                    pe.wait_ge(q_lo, n + 1)
                    pairs = []
                    for k in range(KT):
                        z = [x[:, k, :].rearrange("p (b s) -> p b s", b=B)[:, :, P:S] for x in (c.ZH, c.ZL)]
                        pairs += three(wh[:, par, k, :], wl[:, par, k, :], *z)
                    passes(pe, c.bank(par), pairs).then_inc(q_done, 1)

                def score_of(n, par):
                    pe.wait_ge(q_lo, n + 3)
                    pe.wait_ge(relued, n + 1)
                    for b in range(B):
                        q = [x[:, par, b * P:(b + 1) * P] for x in (qh, ql)]
                        k = [x[:, 3, b * S:(b + 1) * S] for x in (c.UH, c.UL)]
                        out = c.bank(2 + 2 * par + b // 2)[:, (b % 2) * S:(b % 2 + 1) * S]
                        last = passes(pe, out, three(*q, *k))
                    last.then_inc(scored, 1)

                heads(pe, lambda n, par, nth: (head(n, par), score_of(n, par)))

            @block.scalar
            def _(act):
                act.sem_inc(relued, 2)
                def head(n, par, nth):
                    act.wait_ge(loaded[par], nth * 16 + 16)
                    act.wait_ge(q_done, n + 1)
                    nc.scalar.activation(wh[:, par, :, :], raw[:, par, :, :], ACT.Copy).then_inc(w_hi, 1)
                    act.wait_ge(q_done, n + 3)
                    act.wait_ge(scored, n + 1)
                    nc.scalar.activation(qh[:, par, :], c.bank(par), ACT.Copy).then_inc(q_hi, 1)
                    act.wait_ge(scored, n + 3)
                    act.wait_ge(summed, n * B + 1)
                    nc.scalar.activation(relu[:, par, :, :].rearrange("p b s -> p (b s)"),
                                         c.banks(2 + 2 * par, 2), ACT.Relu).then_inc(relued, 1)
                heads(act, head)

            @block.vector
            def _(dve):
                dve.sem_inc(q_lo, 2)
                dve.sem_inc(scored, 2)
                dve.sem_inc(summed, 2 * B)
                nc.vector.memset(score[:, :, :], 0.0).then_inc(found_zero := sem("score_zero"), 1)
                dve.wait_ge(found_zero, 1)
                def head(n, par, nth):
                    dve.wait_ge(q_hi, n + 1)
                    dve.wait_ge(scored, n + 1)
                    nc.vector.tensor_tensor(ql[:, par, :], c.bank(par), f32(qh[:, par, :]), ALU.subtract).then_inc(q_lo, 1)
                    dve.wait_ge(relued, n + 3)
                    for b in range(B):
                        dve.wait_ge(summed, n * B + (B + 1 + b))
                        nc.vector.scalar_tensor_tensor(score[:, b, :], relu[:, par, b, :],
                                                       c.IW[:, 2 * b + 1, bass.ds(n, 1)], score[:, b, :],
                                                       ALU.mult, ALU.add).then_inc(summed, 1)
                heads(dve, head)
                dve.wait_ge(base, 1)
                nc.vector.tensor_copy(score[:, :, :], work[:, :, :]).then_inc(base, 1)
                dve.wait_ge(base, 2)
                dve.sem_inc(replaced, B)
                with dve.Fori(0, TOPK // 8) as r:
                    dve.wait_ge(replaced, r * B + B)
                    dve.sem_inc(step, 1)
                    for b in range(B):
                        nc.vector.max(max8[:, b, :], work[:, b, :]).then_inc(found, 1)
                    dve.wait_ge(found, r * B + B)
                    dve.sem_inc(step, 1)
                    for b in range(B):
                        nc.vector.match_replace(work[:, b, :], max8[:, b, :], work[:, b, :], 10 * NEG
                                                ).then_inc(replaced, 1)
                dve.wait_ge(replaced, B + TOPK // 8 * B)
                nc.vector.tensor_tensor(same[:, :, :], score[:, :, :], work[:, :, :], ALU.is_equal).then_inc(compared, 1)
                dve.wait_ge(compared, 1)
                dve.wait_ge(masked, 2)
                nc.vector.tensor_scalar(c.mask[:, :, 1, :], same[:, :, :], NEG, None, ALU.mult).then_inc(compared, 1)


def attention0(c):
    nc = c.nc
    NPR = G0 // 2
    NU = B * NPR
    NQ = 2 * G0
    HALF = T // 2
    with ExitStack() as ctx:
        sb = lambda n, s, d=F32: ctx.enter_context(nc.sbuf_tensor(f"a0_{n}", s, d))
        sem = lambda n: c.sem(f"a0_{n}")
        raw = sb("raw", [P, R0])
        o = 0
        views = []
        for n in (R_QN, R_KK, R_KV, R_OW, R_PE):
            views.append(raw[:, o:o + n])
            o += n
        qn = views[0].rearrange("p (h n) -> p h n", h=G0)
        kk = views[1].rearrange("p (h n) -> p h n", h=G0)
        kv = views[2].rearrange("p (h n) -> p h n", h=G0)
        ow = views[3].rearrange("p (h n) -> p h n", h=G0)
        qpe = views[4].rearrange("p (h c n) -> p h c n", h=G0, c=2)
        w1h, w1l, w2 = sb("w1h", [P, G0, P], F32R), sb("w1l", [P, G0, P], F32R), sb("w2", [P, G0, P], F32R)
        w2t = sb("w2t", [P, G0, P], F32R)
        woh, wol = sb("woh", [P, NPR, D], F32R), sb("wol", [P, NPR, D], F32R)
        qf, vc, sw = sb("qf", [P, 2, HALF]), sb("vc", [P, 2, HALF]), sb("sw", [P, 2, HALF])
        cosq, sinq = sb("cosq", [P, S]), sb("sinq", [P, S])
        qh, ql = sb("qh", [P, G0, T], F32R), sb("ql", [P, G0, T], F32R)
        prob = sb("prob", [P, 2, 2, 2, S])
        nmax, den, rec = sb("nmax", [P, 2, 4]), sb("den", [P, 2, 4]), sb("rec", [P, 2, 4])
        recx = sb("recx", [P, 2, 2, 2, 64])
        p0h, p0l, p1 = sb("p0h", [P, 2, S], F32R), sb("p0l", [P, 2, S], F32R), sb("p1", [P, 2, P])
        rs, ot = sb("rs", [P, 2, S]), sb("ot", [P, 2, S])
        oh, ol = sb("oh", [P, NPR, T], F32R), sb("ol", [P, NPR, T], F32R)

        tables, loaded, absorbed, values_in = sem("tables"), sem("loaded"), sem("absorbed"), sem("values")
        w_hi, w_lo, raw_read, wo_hi, wo_lo = sem("w_hi"), sem("w_lo"), sem("raw_read"), sem("wo_hi"), sem("wo_lo")
        q_prod, q_plain, q_cos, q_swap, q_sin, q_full, q_hi, q_lo = (sem("q_prod"), sem("q_plain"), sem("q_cos"),
            sem("q_swap"), sem("q_sin"), sem("q_full"), sem("q_hi"), sem("q_lo"))
        scored, maxed, exped, turned = sem("scored"), sem("maxed"), sem("exped"), sem("turned")
        recd, spread, r_turned, r_copied = sem("recd"), sem("spread"), sem("r_turned"), sem("r_copied")
        pt_hi, pt_lo, pv_done, ot_done, o_hi, o_lo = (sem("pt_hi"), sem("pt_lo"), sem("pv"), sem("ot"), sem("o_hi"),
                                                      sem("o_lo"))
        projected, added, w_part = sem("projected"), sem("added"), sem("w_part")
        slot = lambda k: c.bank(k)
        PT0, PT1, PO, PR = c.bank(4), c.bank(5), c.bank(6), c.bank(7)
        pe_rows = slice(64, 128)

        with nc.Block() as block:

            @block.sync
            def _(sp):
                sp.dma_start(cosq[pe_rows, :], c.ins["query_cos"]).then_inc(tables, 16)
                sp.dma_start(sinq[pe_rows, :], c.ins["query_sin"]).then_inc(tables, 16)
                with sp.Fori(0, NG0) as g:
                    sp.wait_ge(absorbed, g * 2 + 1)
                    sp.wait_ge(raw_read, g * 2 + 1)
                    sp.wait_ge(w_part, g * 2 + 1)
                    sp.dma_start(raw[:, :], c.ins["group0"][bass.ds(g, 1), :, :].rearrange("o p n -> (o p) n")
                                 ).then_inc(loaded, 16)

            @block.gpsimd
            def _(pool):
                pool.sem_inc(q_full, 2)
                pool.wait_ge(tables, 32)
                with pool.Fori(0, NG0) as g:
                    for k in range(NQ):
                        n, par = g * NQ + k, k % 2
                        wide = sinq[pe_rows, :].unsqueeze(1).broadcast_to([64, 2, S])
                        half = lambda ap: ap.rearrange("p (b s) -> p b s", b=2)
                        pool.wait_ge(q_swap, n + 1)
                        nc.gpsimd.tensor_tensor(half(sw[pe_rows, par, :]), half(sw[pe_rows, par, :]), wide, ALU.mult
                                                ).then_inc(q_sin, 1)
                        pool.wait_ge(q_sin, n + 1)
                        pool.wait_ge(q_cos, n + 1)
                        pool.wait_ge(q_lo, n + 1)
                        nc.gpsimd.tensor_tensor(qf[pe_rows, par, :], vc[pe_rows, par, :], sw[pe_rows, par, :], ALU.add
                                                ).then_inc(q_full, 1)

            @block.tensor
            def _(pe):
                pe.sem_inc(absorbed, 1)
                pe.sem_inc(q_prod, 1)
                pe.sem_inc(turned, 2)
                pe.sem_inc(pv_done, 1)
                pe.sem_inc(projected, 1)

                def scores(g, u):
                    b, pr = u // NPR, u % NPR
                    n = g * NU + u
                    if u < 2:
                        pe.wait_ge(q_lo, g * NQ + (2 + NQ))
                    else:
                        pe.wait_ge(exped, n * 4 + 4)
                    for h in range(2):
                        out = slot(2 * (u % 2) + h)
                        pe.matmul(out, c.ident_bf[:, :], c.mask[:, b, :, :].rearrange("p t s -> p (t s)"),
                                  start=True, stop=False)
                        for t in range(2):
                            rows = slice(b * S + t * P, b * S + (t + 1) * P)
                            q = [x[:, 2 * pr + h, rows] for x in (qh, ql)]
                            k = [x[:, 2, b * S:(b + 1) * S] for x in (c.UH, c.UL)]
                            last = passes(pe, out[:, t * S:(t + 1) * S], three(*q, *k), start=False, stop=t == 1)
                    last.then_inc(scored, 1)

                def turn(g, u):
                    n = g * NU + u
                    pe.wait_ge(exped, n * 4 + 12)
                    pe.wait_ge(pt_lo, n + 1)
                    s = u % 2
                    for h in range(2):
                        pe.transpose(PT0[:, h * S:h * S + P], prob[:, s, h, 0, 0:P], c.ident[:, :])
                        pe.transpose(PT0[:, h * S + P:(h + 1) * S], prob[:, s, h, 1, 0:P], c.ident[:, :])
                        last = pe.transpose(PT1[:, h * P:(h + 1) * P], prob[:, s, h, 1, P:S], c.ident[:, :])
                    last.then_inc(turned, 1)

                def weigh(g, u):
                    n, b = g * NU + u, u // NPR
                    pe.wait_ge(spread, n + 1)
                    pe.wait_ge(r_copied, n + 1)
                    for t in range(2):
                        last = pe.transpose(PR[:, t * P:(t + 1) * P],
                                            recx[:, u % 2, t, :, :].rearrange("p h r -> p (h r)"), c.ident[:, :])
                    last.then_inc(r_turned, 1)
                    pe.wait_ge(pt_lo, n + 2)
                    pe.wait_ge(ot_done, n + 1)
                    for h in range(2):
                        cols = slice(64, 192) if h == 0 else slice(0, 128)
                        vh, vl, v = (x[:, 2 * b, cols] for x in (c.VH, c.VL, c.V))
                        passes(pe, PO[:, 0:S], three(vh, vl, p0h[:, h, :], p0l[:, h, :]), start=h == 0, stop=False)
                        last = pe.matmul(PO[:, P:S], c.V[:, 2 * b + 1, cols], p1[:, h, :], start=False, stop=h == 1)
                    last.then_inc(pv_done, 1)

                with pe.Fori(0, NG0) as g:
                    pe.wait_ge(loaded, g * 16 + 16)
                    pe.wait_ge(added, g * TT + 1)
                    pe.wait_ge(r_copied, g * NU + 1)
                    for h in range(G0):
                        for ch in range(2):
                            last = pe.matmul(PR[:, (2 * h + ch) * 64:(2 * h + ch + 1) * 64], qn[:, h, ch * P:(ch + 1) * P],
                                             kk[:, h, :], start=True, stop=True)
                    last.then_inc(absorbed, 1)
                    for h in range(G0):
                        rows = slice(64 * (h % 2), 64 * (h % 2) + 64)
                        last = pe.matmul(slot(h // 2)[rows, :], kv[:, h, :], ow[:, h, :], start=True, stop=True)
                    last.then_inc(absorbed, 1)
                    pe.wait_ge(w_lo, g + 1)
                    for k in range(NQ):
                        h, half = k // 2, k % 2
                        bank = (k + 2) % 4
                        if k in (2, 3):
                            pe.wait_ge(wo_lo, g + 1)
                        if k >= 4:
                            pe.wait_ge(q_cos, g * NQ + (k - 3))
                            pe.wait_ge(q_swap, g * NQ + (k - 3))
                            pe.wait_ge(q_plain, g * NQ + (k - 3))
                        toks = slice(half * HALF, (half + 1) * HALF)
                        q1h, q1l, q2h, q2l = c.UH[:, 0, toks], c.UL[:, 0, toks], c.UH[:, 1, toks], c.UL[:, 1, toks]
                        pairs = three(w1h[:, h, :], w1l[:, h, :], q1h, q1l) + [(w2[:, h, :], q2h), (w2[:, h, :], q2l)]
                        passes(pe, slot(bank), pairs).then_inc(q_prod, 1)
                    scores(g, 0)
                    scores(g, 1)
                    for u in range(NU):
                        turn(g, u)
                        if u + 2 < NU:
                            scores(g, u + 2)
                        weigh(g, u)
                    pe.wait_ge(o_lo, g * NU + (NU + 1))
                    for t in range(TT):
                        if t >= 4:
                            pe.wait_ge(added, g * TT + (t - 3 + 1))
                        pairs = []
                        for pr in range(NPR):
                            x = [y[:, pr, t * P:(t + 1) * P] for y in (oh, ol)]
                            pairs += three(*x, woh[:, pr, :], wol[:, pr, :])
                        passes(pe, slot(t % 4), pairs).then_inc(projected, 1)

            @block.scalar
            def _(act):
                act.sem_inc(r_copied, 1)
                act.sem_inc(exped, 8)
                act.sem_inc(o_hi, 1)
                act.wait_ge(tables, 32)
                with act.Fori(0, NG0) as g:
                    act.wait_ge(absorbed, g * 2 + 2)
                    act.wait_ge(q_prod, g * NQ + 1)
                    absw = PR.rearrange("p (h c n) -> p h c n", h=G0, c=2)
                    for part, src in ((slice(0, 64), absw), (slice(64, 128), qpe)):
                        nc.scalar.activation(w1h[:, :, part], src[:, :, 0, :], ACT.Copy).then_inc(w_hi, 1)
                        nc.scalar.activation(w2[0:64, :, part], src[0:64, :, 1, :], ACT.Copy).then_inc(w_hi, 1)
                        nc.scalar.activation(w2t[64:128, :, part], src[64:128, :, 1, :], ACT.Copy).then_inc(w_hi, 1)
                    act.wait_ge(absorbed, g * 2 + 3)
                    act.wait_ge(projected, g * TT + 1)
                    nc.scalar.activation(woh[:, :, :].rearrange("p a n -> p (a n)"), c.banks(0, 2), ACT.Copy
                                         ).then_inc(wo_hi, 1)

                    def q_high(k):
                        act.wait_ge(q_full, g * NQ + (k + 3))
                        act.wait_ge(q_plain, g * NQ + (k + 1))
                        h, half = k // 2, k % 2
                        toks = slice(half * HALF, (half + 1) * HALF)
                        if k == 0:
                            act.wait_ge(scored, g * NU + 1)
                        nc.scalar.activation(qh[:, h, toks], qf[:, k % 2, :], ACT.Copy).then_inc(q_hi, 1)

                    for k in range(NQ):
                        act.wait_ge(q_prod, g * NQ + (k + 2))
                        act.wait_ge(q_lo, g * NQ + (k + 1))
                        nc.scalar.activation(qf[0:64, k % 2, :], slot((k + 2) % 4)[0:64, :], ACT.Copy, scale=SCALE0
                                             ).then_inc(q_plain, 1)
                        if k:
                            q_high(k - 1)
                    q_high(NQ - 1)

                    def exps(u):
                        n, s = g * NU + u, u % 2
                        act.wait_ge(maxed, n + 1)
                        act.wait_ge(turned, n + 1)
                        act.wait_ge(recd, n + 1)
                        for h in range(2):
                            for t in range(2):
                                w = (t + 1) * P
                                nc.scalar.activation(prob[:, s, h, t, 0:w], slot(2 * s + h)[:, t * S:t * S + w], ACT.Exp,
                                                     bias=nmax[:, s, 2 * h + t:2 * h + t + 1],
                                                     accum_out=den[:, s, 2 * h + t:2 * h + t + 1]).then_inc(exped, 1)

                    def o_high(u):
                        n, b, pr = g * NU + u, u // NPR, u % NPR
                        act.wait_ge(ot_done, n + 2)
                        if u == 0:
                            act.wait_ge(projected, g * TT + 1)
                        nc.scalar.activation(oh[:, pr, b * S:(b + 1) * S], ot[:, u % 2, :], ACT.Copy).then_inc(o_hi, 1)

                    exps(0)
                    for u in range(NU):
                        n = g * NU + u
                        if u + 1 < NU:
                            exps(u + 1)
                        if u:
                            o_high(u - 1)
                        act.wait_ge(turned, n + 3)
                        act.wait_ge(pv_done, n + 1)
                        nc.scalar.activation(p0h[:, :, :].rearrange("p h s -> p (h s)"), PT0, ACT.Copy).then_inc(pt_hi, 1)
                        nc.scalar.activation(p1[:, :, :].rearrange("p h s -> p (h s)"), PT1[:, 0:2 * P], ACT.Copy
                                             ).then_inc(pt_hi, 1)
                        act.wait_ge(r_turned, n + 1)
                        act.wait_ge(ot_done, n + 1)
                        nc.scalar.activation(rs[:, u % 2, :], PR[:, 0:S], ACT.Copy).then_inc(r_copied, 1)
                    o_high(NU - 1)

            @block.vector
            def _(dve):
                dve.sem_inc(raw_read, 1)
                dve.sem_inc(w_part, 1)
                dve.sem_inc(q_lo, 2)
                dve.sem_inc(recd, 2)
                dve.sem_inc(pt_lo, 1)
                dve.sem_inc(ot_done, 1)
                dve.sem_inc(o_lo, 1)
                dve.sem_inc(added, 1)
                dve.sem_inc(scored, 1)
                dve.wait_ge(tables, 32)
                with dve.Fori(0, NG0) as g:
                    absw = PR.rearrange("p (h c n) -> p h c n", h=G0, c=2)
                    dve.wait_ge(w_hi, g * 6 + 6)
                    for part, src in ((slice(0, 64), absw), (slice(64, 128), qpe)):
                        nc.vector.tensor_tensor(w1l[:, :, part], src[:, :, 0, :], f32(w1h[:, :, part]), ALU.subtract
                                                ).then_inc(raw_read, 1)
                        last = nc.vector.tensor_tensor(w2[64:128, :, part], src[64:128, :, 1, :],
                                                       f32(w2t[64:128, :, part]), ALU.subtract)
                        last.then_inc(w_part, 1)
                    dve.wait_ge(raw_read, g * 2 + 3)
                    dve.wait_ge(w_part, g * 2 + 3)
                    dve.sem_inc(w_lo, 1)
                    dve.wait_ge(wo_hi, g + 1)
                    nc.vector.tensor_tensor(wol[:, :, :].rearrange("p a n -> p (a n)"), c.banks(0, 2),
                                            f32(woh[:, :, :]).rearrange("p a n -> p (a n)"), ALU.subtract).then_inc(wo_lo, 1)

                    def q_low(k):
                        h, half = k // 2, k % 2
                        toks = slice(half * HALF, (half + 1) * HALF)
                        dve.wait_ge(q_hi, g * NQ + (k + 1))
                        nc.vector.tensor_tensor(ql[:, h, toks], qf[:, k % 2, :], f32(qh[:, h, toks]), ALU.subtract
                                                ).then_inc(q_lo, 1)

                    for k in range(NQ):
                        n, par = g * NQ + k, k % 2
                        bank = slot((k + 2) % 4)
                        half = lambda ap: ap.rearrange("p (b s) -> p b s", b=2)
                        dve.wait_ge(q_prod, n + 2)
                        dve.wait_ge(q_full, n + 1)
                        nc.vector.tensor_tensor(half(vc[pe_rows, par, :]), half(bank[pe_rows, :]),
                                                cosq[pe_rows, :].unsqueeze(1).broadcast_to([64, 2, S]), ALU.mult
                                                ).then_inc(q_cos, 1)
                        nc.vector.stream_shuffle(sw[pe_rows, par, :], bank[pe_rows, :], SWAP16).then_inc(q_swap, 1)
                        if k:
                            q_low(k - 1)
                    q_low(NQ - 1)

                    def maxes(u):
                        n, s = g * NU + u, u % 2
                        dve.wait_ge(scored, n + 2)
                        dve.wait_ge(exped, n * 4 + 4)
                        nc.vector.tensor_reduce(nmax[:, s, :], c.banks(2 * s, 2).rearrange("p (a n) -> p a n", a=4),
                                                AX_X, ALU.max, negate=True).then_inc(maxed, 1)

                    def outputs(u):
                        n, b, pr = g * NU + u, u // NPR, u % NPR
                        dve.wait_ge(pv_done, n + 2)
                        dve.wait_ge(r_copied, n + 2)
                        dve.wait_ge(o_lo, n + 1)
                        nc.vector.tensor_tensor(ot[:, u % 2, :], PO[:, 0:S], rs[:, u % 2, :], ALU.mult).then_inc(ot_done, 1)
                        dve.wait_ge(o_hi, n + 2)
                        nc.vector.tensor_tensor(ol[:, pr, b * S:(b + 1) * S], ot[:, u % 2, :],
                                                f32(oh[:, pr, b * S:(b + 1) * S]), ALU.subtract).then_inc(o_lo, 1)

                    maxes(0)
                    for u in range(NU):
                        n, s = g * NU + u, u % 2
                        if u + 1 < NU:
                            maxes(u + 1)
                        dve.wait_ge(exped, n * 4 + 12)
                        nc.vector.reciprocal(rec[:, s, :], den[:, s, :]).then_inc(recd, 1)
                        dve.wait_ge(recd, n + 3)
                        nc.vector.tensor_copy(recx[:, s, :, :, :],
                                              rec[:, s, :].rearrange("p (h t) -> p t h", h=2).unsqueeze(3)
                                              .broadcast_to([P, 2, 2, 64])).then_inc(spread, 1)
                        if u:
                            outputs(u - 1)
                        dve.wait_ge(pt_hi, n * 2 + 2)
                        nc.vector.tensor_tensor(p0l[:, :, :].rearrange("p h s -> p (h s)"), PT0,
                                                f32(p0h[:, :, :]).rearrange("p h s -> p (h s)"), ALU.subtract
                                                ).then_inc(pt_lo, 1)
                    outputs(NU - 1)
                    for t in range(TT):
                        dve.wait_ge(projected, g * TT + (t + 2))
                        nc.vector.tensor_tensor(c.X[:, t, :], slot(t % 4), c.X[:, t, :], ALU.add).then_inc(added, 1)


def gather(c):
    nc = c.nc
    with ExitStack() as ctx:
        idx = ctx.enter_context(nc.sbuf_tensor("ga_idx", [1, NSEL], I32))
        listed, copied = c.sem("ga_listed"), c.sem("ga_copied")
        with nc.Block() as block:

            @block.sync
            def _(sp):
                sp.dma_start(idx[:, :], c.ins["block_idx"].unsqueeze(0)).then_inc(listed, 16)
                sp.wait_ge(listed, 16)
                with sp.Fori(0, NSEL) as i:
                    blk = sp.value_load(idx[0:1, bass.ds(i, 1)], min_val=0, max_val=NBLK - 1)
                    for src, dst in ((c.ins["k_cache"], c.ks), (c.ins["v_cache"], c.vs)):
                        sp.dma_start(dst[bass.ds(i * BLOCK, BLOCK), :],
                                     src[bass.ds(blk, 1), :, :].rearrange("o r n -> (o r) n")).then_inc(copied, 16)
                sp.wait_ge(copied, 32 * NSEL)


def norm_only(c, name):
    with ExitStack() as ctx:
        norm = Norm(c, ctx, name)
        with c.nc.Block() as block:

            @block.tensor
            def _(pe):
                for t in range(TT):
                    norm.turn(pe, t)

            @block.scalar
            def _(act):
                norm.scalar_std(act)
                for t in range(TT):
                    norm.scalar_hi(act, t)

            @block.vector
            def _(dve):
                norm.vector(dve)


def attention1(c):
    nc = c.nc
    NV = TT
    NQT = REP * NV
    NUN = NQT // 2
    HALF = T // 2
    NQ = REP * 2
    HK = NKEY // 2
    with ExitStack() as ctx:
        sb = lambda n, s, d=F32: ctx.enter_context(nc.sbuf_tensor(f"a1_{n}", s, d))
        sem = lambda n: c.sem(f"a1_{n}")
        raw, rot = sb("raw", [P, KT * WG]), sb("rot", [P, 4, REP + 1, HD // 2])
        fc, fs = sb("cos", [P, HD // 2]), sb("sin", [P, HD // 2])
        wh, wl = sb("wh", [P, KT * WG], F32R), sb("wl", [P, KT * WG], F32R)
        raw_w, *qkv = [x[:, :].rearrange("p (k n) -> p k n", k=KT) for x in (raw, wh, wl)]
        raw_o, *outw = [x[:, 0:REP * D].rearrange("p (h n) -> p h n", h=REP) for x in (raw, wh, wl)]
        kc, vc = sb("kc", [P, NKT, HD]), sb("vc", [P, NKT, HD])
        kh, kl = sb("kh", [P, NKEY], F32R), sb("kl", [P, NKEY], F32R)
        vh, vl = sb("vh", [P, NKT, HD], F32R), sb("vl", [P, NKT, HD], F32R)
        qh, ql = sb("qh", [P, REP, T], F32R), sb("ql", [P, REP, T], F32R)
        prob = sb("prob", [P, 2, NKEY])
        nmax, den, rec = sb("nmax", [P, 2]), sb("den", [P, 2]), sb("rec", [P, 4])
        ph, pl = sb("ph", [P, 2, NKT, S], F32R), sb("pl", [P, 2, NKT, S], F32R)
        rs, ot = sb("rs", [P, S]), sb("ot", [P, 2, S])
        oh, ol = sb("oh", [P, REP, T], F32R), sb("ol", [P, REP, T], F32R)

        tables, w_loaded, rotated, rot_part, w_hi, w_lo = (sem("tables"), sem("w_loaded"), sem("rotated"),
                                                           sem("rot_part"), sem("w_hi"), sem("w_lo"))
        wo_loaded, wo_hi, wo_lo = sem("wo_loaded"), sem("wo_hi"), sem("wo_lo")
        kv_loaded, kv_prod, kv_copied, k_turned, k_hi, k_lo, v_hi, v_lo = (sem("kv_loaded"), sem("kv_prod"),
            sem("kv_copied"), sem("k_turned"), sem("k_hi"), sem("k_lo"), sem("v_hi"), sem("v_lo"))
        q_prod, q_hi, q_lo = sem("q_prod"), sem("q_hi"), sem("q_lo")
        scored, maxed, exped, turned, pt_hi, pt_lo = (sem("scored"), sem("maxed"), sem("exped"), sem("turned"),
                                                      sem("pt_hi"), sem("pt_lo"))
        recd, r_turned, r_copied, pv_done, ot_done, o_hi, o_lo = (sem("recd"), sem("r_turned"), sem("r_copied"),
            sem("pv"), sem("ot"), sem("o_hi"), sem("o_lo"))
        projected, added = sem("projected"), sem("added")
        PO, PR = c.bank(6), c.bank(7)
        turned_banks = c.psum[:, 4:6, 0:HK].rearrange("p a (k n) -> p a k n", n=P)
        key_tiles = lambda ap: ap.rearrange("p (a k) n -> p a k n", a=2)

        with nc.Block() as block:

            @block.sync
            def _(sp):
                sp.dma_start(fc[:, :], c.ins["cos1"].partition_broadcast(P)).then_inc(tables, 16)
                sp.dma_start(fs[:, :], c.ins["sin1"].partition_broadcast(P)).then_inc(tables, 16)
                with sp.Fori(0, NKV) as g:
                    sp.wait_ge(wo_lo, g + 1)
                    sp.dma_start(raw_w, c.ins["group1"].rearrange("g (k p) n -> g p k n", p=P)
                                 [bass.ds(g, 1), :, :, :].rearrange("o p k n -> (o p) k n")).then_inc(w_loaded, 16)
                    sp.wait_ge(k_turned, g + 1)
                    sp.wait_ge(v_lo, g + 1)
                    for src, dst in ((c.ks, kc), (c.vs, vc)):
                        sp.dma_start(dst[:, 0:CT, :], src.rearrange("(t p) n -> p t n", p=P)
                                     [:, :, bass.ds(g * HD, HD)]).then_inc(kv_loaded, 16)
                    sp.wait_ge(w_lo, g + 2)
                    sp.dma_start(raw_o, c.ins["wo1"].rearrange("(h p) n -> p h n", p=P)
                                 [:, bass.ds(g * REP, REP), :]).then_inc(wo_loaded, 16)

            @block.gpsimd
            def _(pool):
                pool.sem_inc(wo_lo, 1)
                pool.sem_inc(rotated, 1)
                pool.wait_ge(tables, 32)
                NR = REP + 1
                with pool.Fori(0, NKV) as g:
                    pool.wait_ge(w_loaded, g * 16 + 16)
                    for k in range(KT):
                        x = raw_w[:, k, 0:NR * HD].rearrange("p (h f e) -> p h f e", h=NR, e=2)
                        cos, sin = (y[:, :].unsqueeze(1).broadcast_to([P, NR, HD // 2]) for y in (fc, fs))
                        pool.wait_ge(rotated, g * 2 * KT + (2 * k + 1))
                        for i, (side, table) in enumerate(((0, cos), (1, sin), (0, sin), (1, cos))):
                            nc.gpsimd.tensor_tensor(rot[:, i, :, :], x[:, :, :, side], table, ALU.mult
                                                    ).then_inc(rot_part, 1)
                        pool.wait_ge(rot_part, g * 4 * KT + (4 * k + 4))
                        nc.gpsimd.tensor_tensor(x[:, :, :, 0], rot[:, 0, :, :], rot[:, 1, :, :], ALU.subtract
                                                ).then_inc(rotated, 1)
                        nc.gpsimd.tensor_tensor(x[:, :, :, 1], rot[:, 2, :, :], rot[:, 3, :, :], ALU.add
                                                ).then_inc(rotated, 1)
                    pool.wait_ge(wo_hi, g + 1)
                    nc.gpsimd.tensor_tensor(outw[1], raw_o, f32(outw[0]), ALU.subtract).then_inc(wo_lo, 1)

            @block.tensor
            def _(pe):
                pe.sem_inc(k_turned, 1)
                pe.sem_inc(turned, 2)
                pe.sem_inc(pv_done, 2)
                pe.sem_inc(projected, 1)

                def scores(g, v):
                    n, h = g * NQT + v, v // NV
                    if v >= 2:
                        pe.wait_ge(exped, n + 1)
                    rows = slice((v % NV) * P, (v % NV + 1) * P)
                    for a in range(2):
                        cols = slice(a * HK, (a + 1) * HK)
                        last = passes(pe, c.psum[:, 2 * (v % 2) + a, 0:HK],
                                      three(qh[:, h, rows], ql[:, h, rows], kh[:, cols], kl[:, cols]))
                    last.then_inc(scored, 1)

                def turn(g, v):
                    n = g * NQT + v
                    pe.wait_ge(exped, n + 3)
                    pe.wait_ge(pt_lo, n + 1)
                    for k in range(NKT):
                        last = pe.transpose(c.psum[:, 4 + k // 3, (k % 3) * P:(k % 3 + 1) * P],
                                            prob[:, v % 2, k * P:(k + 1) * P], c.ident[:, :])
                    last.then_inc(turned, 1)

                def weigh(g, m):
                    n = g * NUN + m
                    pe.wait_ge(recd, n * 2 + 4)
                    pe.wait_ge(r_copied, n + 1)
                    for t in range(2):
                        v = 2 * m + t
                        last = pe.transpose(PR[:, t * P:(t + 1) * P], rec[:, v % 4:v % 4 + 1].broadcast_to([P, P]),
                                            c.ident[:, :])
                    last.then_inc(r_turned, 1)
                    pe.wait_ge(pt_lo, n * 2 + 3)
                    pe.wait_ge(ot_done, n + 1)
                    pairs = []
                    for k in range(NKT):
                        pairs += three(vh[:, k, :], vl[:, k, :], ph[:, m % 2, k, :], pl[:, m % 2, k, :])
                    passes(pe, PO[:, 0:S], pairs).then_inc(pv_done, 1)

                with pe.Fori(0, NKV) as g:
                    pe.wait_ge(w_lo, g + 2)
                    pe.wait_ge(added, g * TT + 1)
                    for t in range(2):
                        z = [x[:, :, t * P:(t + 1) * P] for x in (c.ZH, c.ZL)]
                        pairs = []
                        for k in range(KT):
                            pairs += three(z[0][:, k, :], z[1][:, k, :], *[w[:, k, REP * HD:WG] for w in qkv])
                        passes(pe, c.bank(t)[:, 0:2 * HD], pairs).then_inc(kv_prod, 1)
                    for k in range(NQ):
                        h, half = k // 2, k % 2
                        if k >= 2:
                            pe.wait_ge(q_lo, g * NQ + k)
                        pairs = []
                        for d in range(KT):
                            w = [x[:, d, h * HD:(h + 1) * HD] for x in qkv]
                            z = [x[:, d, half * HALF:(half + 1) * HALF] for x in (c.ZH, c.ZL)]
                            pairs += three(*w, *z)
                        passes(pe, c.bank(2 + k % 2), pairs).then_inc(q_prod, 1)
                        if k == 1:
                            pe.wait_ge(kv_loaded, g * 32 + 32)
                            pe.wait_ge(kv_copied, g * 4 + 4)
                            pe.wait_ge(pt_lo, g * NQT + 1)
                            for j in range(NKT):
                                last = pe.transpose(c.psum[:, 4 + j // 3, (j % 3) * P:(j % 3 + 1) * P], kc[:, j, :],
                                                    c.ident[:, :])
                            last.then_inc(k_turned, 1)
                    pe.wait_ge(q_lo, g * NQ + (NQ + 1))
                    pe.wait_ge(k_lo, g + 1)
                    pe.wait_ge(v_lo, g + 2)
                    scores(g, 0)
                    scores(g, 1)
                    for v in range(NQT):
                        turn(g, v)
                        if v + 2 < NQT:
                            scores(g, v + 2)
                        if v % 2 == 0 and v:
                            weigh(g, v // 2 - 1)
                    weigh(g, NUN - 1)
                    pe.wait_ge(o_lo, g * NUN + (NUN + 1))
                    pe.wait_ge(wo_lo, g + 2)
                    for t in range(TT):
                        if t >= 4:
                            pe.wait_ge(added, g * TT + (t - 2))
                        pairs = []
                        for h in range(REP):
                            x = [y[:, h, t * P:(t + 1) * P] for y in (oh, ol)]
                            pairs += three(*x, *[w[:, h, :] for w in outw])
                        passes(pe, c.bank(t % 4), pairs).then_inc(projected, 1)

            @block.scalar
            def _(act):
                act.sem_inc(exped, 2)
                act.sem_inc(r_copied, 1)
                with act.Fori(0, NKV) as g:
                    act.wait_ge(rotated, g * 2 * KT + (2 * KT + 1))
                    act.wait_ge(projected, g * TT + 1)
                    nc.scalar.activation(wh[:, :], raw[:, :], ACT.Copy).then_inc(w_hi, 1)
                    act.wait_ge(k_turned, g + 1)
                    act.wait_ge(v_lo, g + 1)
                    for t in range(2):
                        act.wait_ge(kv_prod, g * 2 + (t + 1))
                        for i, x in enumerate((kc, vc)):
                            nc.scalar.activation(x[:, CT + t, :], c.bank(t)[:, i * HD:(i + 1) * HD], ACT.Copy
                                                 ).then_inc(kv_copied, 1)
                    act.wait_ge(scored, g * NQT + 1)
                    for k in range(NQ):
                        h, half = k // 2, k % 2
                        act.wait_ge(q_prod, g * NQ + (k + 1))
                        nc.scalar.activation(qh[:, h, half * HALF:(half + 1) * HALF], c.bank(2 + k % 2), ACT.Copy,
                                             scale=SCALE1).then_inc(q_hi, 1)
                        if k == 1:
                            act.wait_ge(k_turned, g + 2)
                            nc.scalar.activation(kh[:, :].rearrange("p (a k n) -> p a k n", a=2, n=P), turned_banks,
                                                 ACT.Copy).then_inc(k_hi, 1)
                            act.wait_ge(kv_loaded, g * 32 + 32)
                            act.wait_ge(kv_copied, g * 4 + 4)
                            act.wait_ge(pv_done, g * NUN + 2)
                            nc.scalar.activation(vh[:, :, :], vc[:, :, :], ACT.Copy).then_inc(v_hi, 1)

                    def exp_of(v):
                        n, s = g * NQT + v, v % 2
                        act.wait_ge(maxed, n + 1)
                        act.wait_ge(turned, n + 1)
                        act.wait_ge(recd, n + 1)
                        nc.scalar.activation(prob[:, s, :].rearrange("p (a n) -> p a n", a=2),
                                             c.psum[:, 2 * s:2 * s + 2, 0:HK], ACT.Exp, bias=nmax[:, s:s + 1],
                                             accum_out=den[:, s:s + 1]).then_inc(exped, 1)

                    def o_high(m):
                        n, h = g * NUN + m, m // 4
                        act.wait_ge(ot_done, n + 2)
                        nc.scalar.activation(oh[:, h, (m % 4) * S:(m % 4 + 1) * S], ot[:, m % 2, :], ACT.Copy
                                             ).then_inc(o_hi, 1)

                    def r_copy(m):
                        n = g * NUN + m
                        act.wait_ge(r_turned, n + 1)
                        act.wait_ge(ot_done, n + 1)
                        nc.scalar.activation(rs[:, :], PR[:, 0:S], ACT.Copy).then_inc(r_copied, 1)

                    exp_of(0)
                    for v in range(NQT):
                        n, m = g * NQT + v, v // 2
                        if v + 1 < NQT:
                            exp_of(v + 1)
                        if v % 2 and m:
                            o_high(m - 1)
                        act.wait_ge(turned, n + 3)
                        act.wait_ge(pv_done, g * NUN + (m + 1))
                        nc.scalar.activation(key_tiles(ph[:, m % 2, :, (v % 2) * P:(v % 2 + 1) * P]), turned_banks,
                                             ACT.Copy).then_inc(pt_hi, 1)
                        if v % 2 == 0 and m:
                            r_copy(m - 1)
                        if v == 4:
                            act.wait_ge(wo_loaded, g * 16 + 16)
                            act.wait_ge(q_prod, g * NQ + NQ)
                            nc.scalar.activation(outw[0], raw_o, ACT.Copy).then_inc(wo_hi, 1)
                    r_copy(NUN - 1)
                    o_high(NUN - 1)

            @block.vector
            def _(dve):
                for s in (w_lo, v_lo, q_lo, scored, pt_lo, ot_done, o_lo, added):
                    dve.sem_inc(s, 1)
                dve.sem_inc(recd, 2)
                with dve.Fori(0, NKV) as g:
                    dve.wait_ge(w_hi, g + 1)
                    nc.vector.tensor_tensor(wl[:, :], raw[:, :], f32(wh[:, :]), ALU.subtract).then_inc(w_lo, 1)
                    for k in range(NQ):
                        h, half = k // 2, k % 2
                        toks = slice(half * HALF, (half + 1) * HALF)
                        dve.wait_ge(q_hi, g * NQ + (k + 1))
                        nc.vector.scalar_tensor_tensor(ql[:, h, toks], c.bank(2 + k % 2), SCALE1, f32(qh[:, h, toks]),
                                                       ALU.mult, ALU.subtract).then_inc(q_lo, 1)
                        if k == 1:
                            dve.wait_ge(k_hi, g + 1)
                            nc.vector.tensor_tensor(kl[:, :].rearrange("p (a n) -> p a n", a=2),
                                                    c.psum[:, 4:6, 0:HK],
                                                    f32(kh[:, :]).rearrange("p (a n) -> p a n", a=2), ALU.subtract
                                                    ).then_inc(k_lo, 1)
                            dve.wait_ge(v_hi, g + 1)
                            nc.vector.tensor_tensor(vl[:, :, :], vc[:, :, :], f32(vh[:, :, :]), ALU.subtract
                                                    ).then_inc(v_lo, 1)

                    def max_of(v):
                        n, s = g * NQT + v, v % 2
                        dve.wait_ge(scored, n + 2)
                        dve.wait_ge(exped, n + 1)
                        nc.vector.tensor_reduce(nmax[:, s:s + 1], c.psum[:, 2 * s:2 * s + 2, 0:HK],
                                                mybir.AxisListType.XY, ALU.max, negate=True).then_inc(maxed, 1)

                    def output(m):
                        n, h = g * NUN + m, m // 4
                        toks = slice((m % 4) * S, (m % 4 + 1) * S)
                        dve.wait_ge(pv_done, n + 3)
                        dve.wait_ge(r_copied, n + 2)
                        dve.wait_ge(o_lo, n + 1)
                        nc.vector.tensor_tensor(ot[:, m % 2, :], PO[:, 0:S], rs[:, :], ALU.mult).then_inc(ot_done, 1)
                        dve.wait_ge(o_hi, n + 1)
                        nc.vector.tensor_tensor(ol[:, h, toks], ot[:, m % 2, :], f32(oh[:, h, toks]), ALU.subtract
                                                ).then_inc(o_lo, 1)

                    max_of(0)
                    for v in range(NQT):
                        n, m = g * NQT + v, v // 2
                        if v + 1 < NQT:
                            max_of(v + 1)
                        dve.wait_ge(exped, n + 3)
                        nc.vector.reciprocal(rec[:, v % 4:v % 4 + 1], den[:, v % 2:v % 2 + 1]).then_inc(recd, 1)
                        if v % 2 and m:
                            output(m - 1)
                        dve.wait_ge(pt_hi, n + 1)
                        cols = slice((v % 2) * P, (v % 2 + 1) * P)
                        nc.vector.tensor_tensor(key_tiles(pl[:, m % 2, :, cols]), turned_banks,
                                                f32(key_tiles(ph[:, m % 2, :, cols])), ALU.subtract).then_inc(pt_lo, 1)
                    output(NUN - 1)
                    for t in range(TT):
                        dve.wait_ge(projected, g * TT + (t + 2))
                        nc.vector.tensor_tensor(c.X[:, t, :], c.bank(t % 4), c.X[:, t, :], ALU.add).then_inc(added, 1)


def store(c):
    nc = c.nc
    stored = c.sem("stored")
    with nc.Block() as block:

        @block.sync
        def _(sp):
            sp.dma_start(c.out.rearrange("(t p) n -> p t n", p=P), c.X[:, :, :]).then_inc(stored, 16)
            sp.wait_ge(stored, 16)


def macaron(nc, ins, out):
    c = Chip()
    c.nc, c.ins, c.out = nc, ins, out
    with ExitStack() as whole:
        c.sems = []
        c.sem = lambda n: c.sems.append(nc.alloc_semaphore(name=n)) or c.sems[-1]
        sb = lambda ctx, n, s, d=F32: ctx.enter_context(nc.sbuf_tensor(n, s, d))
        c.psum = whole.enter_context(nc.psum_tensor("psum", [P, 8, 512], F32))
        c.bank = lambda i: c.psum[:, i, :]
        c.banks = lambda i, n: c.psum[:, i:i + n, :].rearrange("p a n -> p (a n)")
        dram = lambda n, s: nc.dram_tensor(n, s, F32, kind="Internal").ap()
        c.dq12, c.dq3 = dram("dq12", (2 * FHP, D)), dram("dq3", (D, FHP))
        c.wd = dram("wd", (FC, P, 3 * D))
        c.ks, c.vs = dram("k_chosen", (NSEL * BLOCK, NKV * HD)), dram("v_chosen", (NSEL * BLOCK, NKV * HD))
        c.X = sb(whole, "X", [P, TT, D])
        c.ident = sb(whole, "ident", [P, P])
        with ExitStack() as ctx:
            c.ident_bf, c.zero_bf = sb(ctx, "ident_bf", [P, P], BF16), sb(ctx, "zero_bf", [P, D], BF16)
            c.bias, c.nf_bias = sb(ctx, "bias", [P, D]), sb(ctx, "nf_bias", [P, len(NF4_STEPS)])
            c.W0H, c.W0L = sb(ctx, "W0H", [P, KT, D], F32R), sb(ctx, "W0L", [P, KT, D], F32R)
            setup(c)
            dequant(c)
            turn_weights(c)
            gather(c)
            with ExitStack() as l0:
                c.UH, c.UL = sb(l0, "UH", [P, 4, T], F32R), sb(l0, "UL", [P, 4, T], F32R)
                c.V = sb(l0, "V", [P, TT, 192])
                c.VH, c.VL = sb(l0, "VH", [P, TT, 192], F32R), sb(l0, "VL", [P, TT, 192], F32R)
                c.IW, c.mask = sb(l0, "IW", [P, TT, IDX_H]), sb(l0, "mask", [P, B, 2, S], BF16)
                with ExitStack() as z:
                    c.ZH, c.ZL = sb(z, "ZH0", [P, KT, T], F32R), sb(z, "ZL0", [P, KT, T], F32R)
                    ffn0(c, "f0")
                    latents(c)
                    indexer(c)
                attention0(c)
            recycle(c)
            with ExitStack() as l0:
                c.ZH, c.ZL = sb(l0, "ZH1", [P, KT, T], F32R), sb(l0, "ZL1", [P, KT, T], F32R)
                ffn0(c, "f1")
                ffn1(c, "g0")
        with ExitStack() as l1:
            c.ZH, c.ZL = sb(l1, "ZH2", [P, KT, T], F32R), sb(l1, "ZL2", [P, KT, T], F32R)
            norm_only(c, "n1")
            attention1(c)
        with ExitStack() as l1:
            c.ZH, c.ZL = sb(l1, "ZH3", [P, KT, T], F32R), sb(l1, "ZL3", [P, KT, T], F32R)
            c.zero_bf = sb(l1, "zero_bf2", [P, D], BF16)
            zero(c)
            ffn1(c, "g1")
        store(c)


def recycle(c):
    c.nc.clear_and_free_semaphores(c.sems)
    c.sems = []
    with c.nc.Block() as block:

        @block.gpsimd
        def _(pool):
            pass


def zero(c):
    zeroed = c.sem("zeroed")
    with c.nc.Block() as block:

        @block.gpsimd
        def _(pool):
            c.nc.gpsimd.memset(c.zero_bf[:, :], 0.0).then_inc(zeroed, 1)



def rope_order(a):
    a = a.reshape(a.shape[:-1] + (2, 16, 2))
    return np.ascontiguousarray(np.moveaxis(a, -1, -2)).reshape(a.shape[:-3] + (ROPE,))


def rope_tables():
    freq = (1.0 / THETA ** (np.arange(0, ROPE, 2, dtype=np.float32) / ROPE)).astype(np.float32)
    ang = (np.arange(S, dtype=np.float32)[:, None] * freq[None, :]).astype(np.float32)
    cos, sin = np.cos(ang), np.sin(ang)
    two = lambda x0, x1: rope_order(np.stack([x0, x1], -1).reshape(S, ROPE))
    return two(cos, cos).astype(np.float32), two(-sin, sin).astype(np.float32)


def lay_out(a):
    np_ = lambda n: np.asarray(a[n])
    out = {"x": np_("L0_attn_hidden_states").reshape(T, D)}
    out["lora_a"] = np_("L0_ffn_lora_A").reshape(P, D)
    out["lora_b"] = np_("L0_ffn_lora_B").transpose(0, 2, 1).reshape(P, D)
    out["lora_w"] = np_("L0_ffn_lora_weights")
    out["w0"] = np_("L0_ffn_W").T
    out["bias"] = np_("L0_ffn_bias")
    out["nf_bias"] = (-NF4_BOUNDS * np.float32(STEEP)).astype(np.float32)
    kva = np_("L0_attn_kv_a_w")
    out["proj"] = np.concatenate([np_("L0_attn_q_a_w"), kva[:, :KV_RANK], rope_order(kva[:, KV_RANK:]),
                                  np_("L0_attn_idx_wk_w"), np_("L0_attn_idx_weights_w")], axis=1)
    out["q_norm"], out["kv_norm"] = np_("L0_attn_q_a_norm_w"), np_("L0_attn_kv_a_norm_w")
    cos, sin = rope_tables()
    out["key_cos"], out["key_sin"] = cos, sin
    scale = np.float32(SCALE0)
    out["query_cos"], out["query_sin"] = cos.T * scale, sin.T * scale
    out["idx_wq"] = np_("L0_attn_idx_wq_w")
    qb = np_("L0_attn_q_b_w").reshape(Q_RANK, H0, NOPE + ROPE)
    kvb = np_("L0_attn_kv_b_w").reshape(KV_RANK, H0, NOPE + VD)
    twice = lambda w: np.concatenate([w[:P], w[P:], w[P:]])
    heads = lambda w: w.reshape(NG0, G0, P, -1).transpose(0, 2, 1, 3).reshape(NG0, P, -1)
    qn = heads(twice(qb[:, :, :NOPE]).transpose(1, 2, 0))
    kk = heads(kvb[:, :, :NOPE].transpose(1, 2, 0))
    kv = heads(kvb[:, :, NOPE:].transpose(1, 2, 0))
    ow = heads(np_("L0_attn_o_w").reshape(H0, VD, D))
    pe = twice(rope_order(qb[:, :, NOPE:])).reshape(2, P, NG0, G0, ROPE).transpose(2, 1, 3, 0, 4).reshape(NG0, P, -1)
    out["group0"] = np.concatenate([qn, kk, kv, ow, pe], axis=2)
    out["cos1"], out["sin1"] = np_("L1_attn_freqs_cos").reshape(-1), np_("L1_attn_freqs_sin").reshape(-1)
    wq = np_("L1_attn_wq").reshape(NKV, REP * HD, D)
    wk, wv = (np_(f"L1_attn_w{x}").reshape(NKV, HD, D) for x in "kv")
    out["group1"] = np.concatenate([wq, wk, wv], axis=1).transpose(0, 2, 1)
    out["wo1"] = np_("L1_attn_wo").T
    out["k_cache"], out["v_cache"] = (np_(f"L1_attn_{x}_cache").reshape(NBLK, BLOCK, NKV * HD) for x in "kv")
    out["block_idx"] = np_("L1_attn_block_idx")
    for i in "123":
        out[f"w{i}"] = np_(f"L1_ffn_w{i}")
    return {n: np.ascontiguousarray(x) for n, x in out.items()}


def kernel(**inputs):
    import concourse.bacc as _bacc
    from concourse.bass_utils import run_bass_kernel_spmd as _run

    nc = _bacc.Bacc("TRN2", target_bir_lowering=False, num_devices=1)
    arrays = {f"in_{n}": x for n, x in lay_out(inputs).items()}
    ins = {n[3:]: nc.dram_tensor(n, x.shape, mybir.dt.from_np(x.dtype), kind="ExternalInput").ap()
           for n, x in arrays.items()}
    out = nc.dram_tensor("out", (T, D), F32, kind="ExternalOutput").ap()
    macaron(nc, ins, out)
    r = _run(nc, [arrays], core_ids=[0])
    return r.results[0]["out"].reshape(B, S, D)
```

```python
from contextlib import ExitStack

import numpy as np

import concourse.bass as bass
from concourse import mybir

F32 = mybir.dt.float32
F32R = mybir.dt.float32r
BF16 = mybir.dt.bfloat16
I32 = mybir.dt.int32
ALU = mybir.AluOpType
ACT = mybir.ActivationFunctionType
AX_X = mybir.AxisListType.X

P = 128
D = 512
KT = D // P
B, S = 4, 256
T = B * S
TT = T // P
EPS = 1e-5
NEG = -1e30

H0, NOPE, ROPE, VD = 32, 128, 64, 128
Q_RANK, KV_RANK = 192, 64
IDX_H, IDX_D, TOPK = 16, 128, 128
SCALE0 = float(NOPE + ROPE) ** -0.5
THETA = 10000.0
PROJ = Q_RANK + KV_RANK + ROPE + IDX_D + IDX_H
G0 = 4
NG0 = H0 // G0
R_QN, R_KK, R_KV, R_OW, R_PE = G0 * 256, G0 * 64, G0 * 64, G0 * D, G0 * 128
R0 = R_QN + R_KK + R_KV + R_OW + R_PE

LORA_N, LORA_R, ALPHA = 8, 16, 32

NKV, HD, REP = 8, 128, 4
BLOCK, NBLK, NSEL = 32, 128, 16
CT = NSEL * BLOCK // P
NKT = CT + S // P
NKEY = NKT * P
SCALE1 = float(HD) ** -0.5
WG = REP * HD + 2 * HD

FH = 1376
FC = (FH + P - 1) // P
FHP = FC * P
QB = 64
NF4 = np.array([-1.0, -0.6961928009986877, -0.5250730514526367, -0.39491748809814453, -0.28444138169288635,
                -0.18477343022823334, -0.09105003625154495, 0.0, 0.07958029955625534, 0.16093020141124725,
                0.24611230194568634, 0.33791524171829224, 0.44070982933044434, 0.5626170039176941,
                0.7229568362236023, 1.0], np.float32)
NF4_BOUNDS = (NF4[:-1] + NF4[1:]) * np.float32(0.5)
NF4_STEPS = NF4[1:] - NF4[:-1]
STEEP = 2.0 ** 60
NF_W1, NF_W2, NF_W3 = 0, FC * D, 2 * FC * D
NF_PARTS = 3 * NG0
NF_W = -(-(NF_W3 + 4 * FH) // (NF_PARTS * QB)) * QB

SWAP16 = [(i + 16) % 32 for i in range(32)]


class Chip:
    pass


def passes(pe, out, pairs, start=True, stop=True):
    n = len(pairs)
    for i, (w, x) in enumerate(pairs):
        last = pe.matmul(out, w, x, start=start and i == 0, stop=stop and i == n - 1)
    return last


def three(wh, wl, xh, xl):
    return [(wh, xh), (wh, xl), (wl, xh)]


def f32(ap):
    return ap.bitcast(F32)


class Norm:

    def __init__(self, c, ctx, name):
        self.c = c
        nc = c.nc
        sem = lambda n: c.sem(f"{name}_{n}")
        self.stats_done, self.stats_chain = sem("stats_done"), sem("stats_chain")
        self.var_ready, self.std_ready, self.rstd_chain = sem("var_ready"), sem("std_ready"), sem("rstd_chain")
        self.z_ready, self.z_turned = sem("z_ready"), sem("z_turned")
        self.hi_done, self.lo_done = sem("hi_done"), sem("lo_done")
        sb = lambda n, s, d=F32: ctx.enter_context(nc.sbuf_tensor(f"{name}_{n}", s, d))
        self.stats, self.mv = sb("stats", [P, TT, 6]), sb("mv", [P, TT, 2])
        self.tmp = sb("tmp", [P, 5, TT])
        self.z = sb("z", [P, 2, D])

    def vector(self, dve, after=lambda t: None):
        c, nc = self.c, self.c.nc
        for t in range(TT):
            nc.vector.bn_stats(self.stats[:, t, :], c.X[:, t, :]).then_inc(self.stats_done, 1)
        for t in range(TT):
            dve.wait_ge(self.stats_done, t + 1)
            nc.vector.bn_aggr(self.mv[:, t, :], self.stats[:, t, :]).then_inc(self.stats_chain, 1)
        dve.wait_ge(self.stats_chain, TT)
        ve, std, r0, a, rstd = (self.tmp[:, i, :] for i in range(5))
        nc.vector.tensor_scalar(ve, self.mv[:, :, 1], EPS, None, ALU.add).then_inc(self.var_ready, 1)
        dve.wait_ge(self.std_ready, 1)
        newton(nc, dve, self.rstd_chain, ve, std, r0, a, rstd)
        for t in range(TT):
            if t >= 2:
                dve.wait_ge(self.z_turned, t - 1)
            nc.vector.tensor_scalar(self.z[:, t % 2, :], c.X[:, t, :], self.mv[:, t, 0:1], rstd[:, t:t + 1],
                                    ALU.subtract, ALU.mult).then_inc(self.z_ready, 1)
            if t:
                self.low(dve, t - 1)
                after(t - 1)
        self.low(dve, TT - 1)
        after(TT - 1)

    def low(self, dve, t):
        c = self.c
        cols = slice(t * P, (t + 1) * P)
        dve.wait_ge(self.hi_done, t + 1)
        c.nc.vector.tensor_tensor(c.ZL[:, :, cols], c.bank(t % 2).rearrange("p (k n) -> p k n", k=KT),
                                  f32(c.ZH[:, :, cols]), ALU.subtract).then_inc(self.lo_done, 1)

    def scalar_std(self, act):
        act.wait_ge(self.var_ready, 1)
        self.c.nc.scalar.activation(self.tmp[:, 1, :], self.tmp[:, 0, :], ACT.Sqrt).then_inc(self.std_ready, 1)

    def scalar_hi(self, act, t):
        c = self.c
        act.wait_ge(self.z_turned, t + 1)
        c.nc.scalar.activation(c.ZH[:, :, t * P:(t + 1) * P], c.bank(t % 2).rearrange("p (k n) -> p k n", k=KT),
                               ACT.Copy).then_inc(self.hi_done, 1)

    def turn(self, pe, t):
        c = self.c
        pe.wait_ge(self.z_ready, t + 1)
        if t >= 2:
            pe.wait_ge(self.lo_done, t - 1)
        for k in range(KT):
            last = pe.transpose(c.bank(t % 2)[:, k * P:(k + 1) * P], self.z[:, t % 2, k * P:(k + 1) * P], c.ident[:, :])
        last.then_inc(self.z_turned, 1)


def newton(nc, dve, chain, v, std, r0, a, rstd):
    nc.vector.reciprocal(r0, std).then_inc(chain, 1)
    dve.wait_ge(chain, 1)
    nc.vector.tensor_tensor(a, v, r0, ALU.mult).then_inc(chain, 1)
    dve.wait_ge(chain, 2)
    nc.vector.tensor_tensor(rstd, a, r0, ALU.mult).then_inc(chain, 1)
    dve.wait_ge(chain, 3)
    nc.vector.tensor_scalar(a, rstd, -0.5, 1.5, ALU.mult, ALU.add).then_inc(chain, 1)
    dve.wait_ge(chain, 4)
    nc.vector.tensor_tensor(rstd, r0, a, ALU.mult).then_inc(chain, 1)
    dve.wait_ge(chain, 5)


def setup(c):
    nc = c.nc
    with ExitStack() as ctx:
        sb = lambda n, s, d=F32: ctx.enter_context(nc.sbuf_tensor(n, s, d))
        w_raw, la, lb, lw = sb("w_raw", [P, KT, D]), sb("lora_a", [P, D]), sb("lora_b", [P, D]), sb("lora_w", [P, 1])
        loaded, ident_made, scaled, merged = c.sem("su_loaded"), c.sem("su_ident"), c.sem("su_scaled"), c.sem("su_mm")
        summed, kept = c.sem("su_summed"), c.sem("su_kept")
        x_loaded = c.sem("su_x")
        with nc.Block() as block:

            @block.sync
            def _(sp):
                sp.dma_start(la[:, :], c.ins["lora_a"]).then_inc(loaded, 16)
                sp.dma_start(lb[:, :], c.ins["lora_b"]).then_inc(loaded, 16)
                sp.dma_start(lw[:, :], c.ins["lora_w"].unsqueeze(1).broadcast_to([LORA_N, LORA_R]).unsqueeze(2)
                             ).then_inc(loaded, 16)
                sp.dma_start(w_raw[:, :, :], c.ins["w0"].rearrange("(k p) n -> p k n", p=P)).then_inc(loaded, 16)
                sp.dma_start(c.X[:, :, :], c.ins["x"].rearrange("(t p) n -> p t n", p=P)).then_inc(x_loaded, 16)
                sp.dma_start(c.nf_bias[:, :], c.ins["nf_bias"].partition_broadcast(P)).then_inc(x_loaded, 16)
                sp.wait_ge(summed, KT)
                sp.dma_start(c.w0.rearrange("(k p) n -> p k n", p=P), w_raw[:, :, :]).then_inc(kept, 16)
                sp.wait_ge(kept, 16)
                sp.wait_ge(x_loaded, 32)

            @block.gpsimd
            def _(pool):
                nc.gpsimd.memset(c.ident[:, :], 0.0).then_inc(ident_made, 1)
                pool.wait_ge(ident_made, 1)
                nc.gpsimd.affine_select(out=c.ident[:, :], in_=c.ident[:, :], compare_op=ALU.not_equal, fill=1.0,
                                        base=0, pattern=[[-1, P]], channel_multiplier=1).then_inc(ident_made, 1)
                nc.gpsimd.memset(c.zero_bf[:, :], 0.0).then_inc(ident_made, 1)
                pool.wait_ge(ident_made, 2)
                nc.gpsimd.tensor_copy(c.ident_bf[:, :], c.ident[:, :]).then_inc(ident_made, 1)

            @block.vector
            def _(dve):
                dve.wait_ge(loaded, 64)
                nc.vector.tensor_scalar(lb[:, :], lb[:, :], lw[:, 0:1], float(ALPHA) / LORA_R, ALU.mult, ALU.mult
                                        ).then_inc(scaled, 1)
                for k in range(KT):
                    dve.wait_ge(merged, k + 1)
                    nc.vector.tensor_tensor(w_raw[:, k, :], c.bank(k), w_raw[:, k, :], ALU.add).then_inc(summed, 1)

            @block.tensor
            def _(pe):
                pe.wait_ge(scaled, 1)
                for k in range(KT):
                    pe.matmul(c.bank(k), la[:, k * P:(k + 1) * P], lb[:, :], start=True, stop=True).then_inc(merged, 1)


class Dequant:

    STEPS = len(NF4_STEPS)
    SLOTS = 3 * STEPS
    RING = 5

    def __init__(self, c, ctx):
        self.c = c
        nc, nb = c.nc, NF_W // QB
        sb = lambda n, s: ctx.enter_context(nc.sbuf_tensor(f"dq_{n}", s, F32))
        sem = lambda n: c.sem(f"dq_{n}")
        self.v, self.acc = sb("v", [P, 3, NF_W]), sb("acc", [P, 3, NF_W])
        self.rel = ctx.enter_context(nc.sbuf_tensor("dq_rel", [P, self.RING, NF_W], BF16))
        self.amax, self.safe, self.inv = sb("amax", [P, 3, nb]), sb("safe", [P, nb]), sb("inv", [P, nb])
        self.loaded, self.stored = [sem(f"loaded{j}") for j in range(3)], [sem(f"stored{j}") for j in range(3)]
        self.prepared, self.v_ready, self.acc_ready = sem("prepared"), sem("v_ready"), sem("acc_ready")
        self.rel_ready, self.stepped, self.finished = sem("rel_ready"), sem("stepped"), sem("finished")

    def load(self, act, g, j):
        act.wait_ge(self.rel_ready, g.count(self.SLOTS, self.STEPS * max(j - 2, 0) + 1))
        act.dma_start(self.v[:, j % 3, :], self.c.ins["nf"][:, bass.ds(g.count(3 * NF_W, j * NF_W), NF_W)]
                      ).then_inc(self.loaded[j % 3], 16)

    def store(self, act, g, j):
        act.wait_ge(self.finished, g.count(3, j + 4))
        act.dma_start(self.c.dq[:, bass.ds(g.count(3 * NF_W, (j + 1) * NF_W), NF_W)], self.acc[:, j % 3, :]
                      ).then_inc(self.stored[j % 3], 16)

    def scalar_begin(self, act):
        act.sem_inc(self.rel_ready, 1)
        for j in range(2):
            act.sem_inc(self.stored[j], 16)
            self.load(act, Group(None, 0), j)

    def scalar(self, act, g, slot):
        if slot >= self.SLOTS:
            return
        j, s = divmod(slot, self.STEPS)
        if s == 0:
            self.load(act, g, j + 2)
            act.wait_ge(self.v_ready, g.count(3, j + 1))
        if s == 8:
            self.store(act, g, j - 1)
        act.wait_ge(self.stepped, g.count(self.SLOTS, slot + 1))
        self.c.nc.scalar.activation(self.rel[:, s % self.RING, :], self.v[:, j, :], ACT.Relu,
                                    bias=self.c.nf_bias[:, s:s + 1], scale=STEEP).then_inc(self.rel_ready, 1)

    def vector_begin(self, dve):
        dve.sem_inc(self.stepped, self.RING)
        self.c.nc.vector.memset(self.acc[:, 2, :], 0.0).then_inc(self.finished, 3)
        self.prepare(dve, Group(None, 0), 0)

    def vector(self, dve, g, slot):
        if slot >= self.SLOTS:
            return
        j, s = divmod(slot, self.STEPS)
        if s == 0:
            dve.wait_ge(self.acc_ready, g.count(3, j + 1))
        dve.wait_ge(self.stepped, g.count(self.SLOTS, slot + self.RING))
        dve.wait_ge(self.rel_ready, g.count(self.SLOTS, slot + 2))
        self.c.nc.vector.scalar_tensor_tensor(self.acc[:, j, :], self.rel[:, s % self.RING, :], float(NF4_STEPS[s]),
                                              self.acc[:, j, :], ALU.min, ALU.add).then_inc(self.stepped, 1)

    def blocks(self, ap):
        return ap.rearrange("p (b n) -> p b n", n=QB)

    def prepare(self, dve, g, j):
        nc, b = self.c.nc, j % 3
        n = lambda more, per=1: g.count(3 * per, j * per + more)
        wide = lambda ap: ap.unsqueeze(2).broadcast_to([P, NF_W // QB, QB])
        v = self.blocks(self.v[:, b, :])
        dve.wait_ge(self.loaded[b], g.count(16, 16 * (j // 3 + 1)))
        dve.wait_ge(self.finished, n(1))
        nc.vector.tensor_reduce(self.amax[:, b, :], v, AX_X, ALU.max, apply_absolute_value=True
                                ).then_inc(self.prepared, 1)
        dve.wait_ge(self.prepared, n(1, 3))
        nc.vector.tensor_scalar(self.safe[:, :], self.amax[:, b, :], 1e-37, None, ALU.max).then_inc(self.prepared, 1)
        dve.wait_ge(self.prepared, n(2, 3))
        nc.vector.reciprocal(self.inv[:, :], self.safe[:, :]).then_inc(self.prepared, 1)
        dve.wait_ge(self.prepared, n(3, 3))
        nc.vector.tensor_tensor(v, v, wide(self.inv[:, :]), ALU.mult).then_inc(self.v_ready, 1)
        dve.wait_ge(self.stored[b], g.count(16, 16 * (j // 3 + 1)))
        nc.vector.memset(self.acc[:, b, :], float(NF4[0])).then_inc(self.acc_ready, 1)

    def finish(self, dve, g, j):
        nc = self.c.nc
        wide = self.amax[:, j, :].unsqueeze(2).broadcast_to([P, NF_W // QB, QB])
        acc = self.blocks(self.acc[:, j, :])
        dve.wait_ge(self.stepped, g.count(self.SLOTS, self.STEPS * (j + 1) + self.RING))
        nc.vector.tensor_tensor(acc, acc, wide, ALU.mult).then_inc(self.finished, 1)


def turn_weights(c):
    nc = c.nc
    with ExitStack() as ctx:
        sb = lambda n, s, d=F32: ctx.enter_context(nc.sbuf_tensor(n, s, d))
        rows, w3c, out = sb("tw_rows", [P, 2, D]), sb("tw_w3", [P, KT, P]), sb("tw_out", [P, 3, D])
        loaded, turned, copied, stored = c.sem("tw_loaded"), c.sem("tw_turned"), c.sem("tw_copied"), c.sem("tw_stored")
        with nc.Block() as block:

            @block.sync
            def _(sp):
                def load(i):
                    sp.wait_ge(turned, i + 1)
                    w12 = c.dq[:, NF_W:NF_W + NF_W3].rearrange("p (m n) -> p m n", m=2)
                    sp.dma_start(rows[:, :, :], w12[:, :, bass.ds(i * D, D)]).then_inc(loaded, 16)
                    for k in range(KT):
                        sp.dma_start(w3c[:, k, :], c.dq[:, bass.ds(i * P + (NF_W + NF_W3 + k * FH), P)]
                                     ).then_inc(loaded, 16)

                def keep(i):
                    sp.wait_ge(copied, i * 3 + 3)
                    sp.dma_start(c.wd[bass.ds(i, 1), :, :].rearrange("o p n -> (o p) n"),
                                 out[:, :, :].rearrange("p m n -> p (m n)")).then_inc(stored, 16)

                sp.sem_inc(stored, 16)
                load(0)
                with sp.Fori(0, FC - 1) as i:
                    load(i + 1)
                    keep(i)
                keep(FC - 1)
                sp.wait_ge(stored, 16 * FC + 16)

            @block.tensor
            def _(pe):
                pe.sem_inc(turned, 1)
                with pe.Fori(0, FC) as i:
                    pe.wait_ge(loaded, i * 80 + 80)
                    pe.wait_ge(stored, i * 16 + 16)
                    for m in range(3):
                        for k in range(KT):
                            src = rows[:, m, k * P:(k + 1) * P] if m < 2 else w3c[:, k, :]
                            last = pe.transpose(c.bank(m)[:, k * P:(k + 1) * P], src, c.ident[:, :])
                    last.then_inc(turned, 1)

            @block.scalar
            def _(act):
                with act.Fori(0, FC) as i:
                    act.wait_ge(turned, i + 2)
                    act.wait_ge(stored, i * 16 + 16)
                    nc.scalar.activation(out[:, 0, :], c.bank(0), ACT.Copy).then_inc(copied, 1)
                    nc.scalar.activation(out[:, 1, :], c.bank(1), ACT.Copy).then_inc(copied, 1)

            @block.vector
            def _(dve):
                with dve.Fori(0, FC) as i:
                    dve.wait_ge(turned, i + 2)
                    dve.wait_ge(stored, i * 16 + 16)
                    nc.vector.tensor_copy(out[:, 2, :].rearrange("p (t q e) -> p t e q", t=2, e=2),
                                          c.bank(2).rearrange("p (t e q) -> p t e q", t=2, e=2)).then_inc(copied, 1)


def ffn0(c, name, beside=None):
    nc = c.nc
    with ExitStack() as ctx:
        norm = Norm(c, ctx, name)
        product, biased, added = c.sem(f"{name}_product"), c.sem(f"{name}_biased"), c.sem(f"{name}_added")
        sb = lambda n, s, d=F32: ctx.enter_context(nc.sbuf_tensor(f"{name}_{n}", s, d))
        w, wh, wl, bias = (sb("w", [P, KT, D]), sb("wh", [P, KT, D], F32R), sb("wl", [P, KT, D], F32R),
                           sb("bias", [P, D]))
        w_loaded, bias_loaded, w_hi, w_lo = (c.sem(f"{name}_{n}") for n in ("w_loaded", "bias_loaded", "w_hi", "w_lo"))
        job = beside(c, ctx) if beside else None
        with nc.Block() as block:

            @block.sync
            def _(sp):
                sp.dma_start(w[:, :, :], c.w0.rearrange("(k p) n -> p k n", p=P)).then_inc(w_loaded, 16)
                sp.dma_start(bias[:, :], c.ins["bias"].partition_broadcast(P)).then_inc(bias_loaded, 16)
                if job:
                    job(sp)

            @block.gpsimd
            def _(pool):
                pool.wait_ge(w_hi, 1)
                nc.gpsimd.tensor_tensor(wl[:, :, :], w[:, :, :], f32(wh[:, :, :]), ALU.subtract).then_inc(w_lo, 1)

            @block.tensor
            def _(pe):
                def product_of(t):
                    pe.wait_ge(norm.lo_done, t + 1)
                    if t >= 4:
                        pe.wait_ge(added, t - 3)
                    pairs = []
                    for k in range(KT):
                        zh, zl = (z[:, k, t * P:(t + 1) * P] for z in (c.ZH, c.ZL))
                        pairs += three(zh, zl, wh[:, k, :], wl[:, k, :])
                    passes(pe, c.bank(2 + t % 4), pairs).then_inc(product, 1)

                for t in range(TT):
                    norm.turn(pe, t)
                    if t == 1:
                        pe.wait_ge(w_lo, 1)
                    if t:
                        product_of(t - 1)
                product_of(TT - 1)

            @block.scalar
            def _(act):
                act.wait_ge(w_loaded, 16)
                nc.scalar.activation(wh[:, :, :], w[:, :, :], ACT.Copy).then_inc(w_hi, 1)
                norm.scalar_std(act)
                for t in range(TT):
                    norm.scalar_hi(act, t)

            @block.vector
            def _(dve):
                def add(t):
                    dve.wait_ge(product, t + 1)
                    dve.wait_ge(biased, t + 1)
                    nc.vector.scalar_tensor_tensor(c.X[:, t, :], c.bank(2 + t % 4), 0.5, c.X[:, t, :],
                                                   ALU.mult, ALU.add).then_inc(added, 1)

                def after(t):
                    dve.wait_ge(norm.z_ready, t + 1)
                    dve.wait_ge(bias_loaded, 16)
                    nc.vector.scalar_tensor_tensor(c.X[:, t, :], bias[:, :], 0.5, c.X[:, t, :],
                                                   ALU.mult, ALU.add).then_inc(biased, 1)
                    if t >= 2:
                        add(t - 2)

                norm.vector(dve, after)
                add(TT - 2)
                add(TT - 1)


def ffn1(c, name):
    nc = c.nc
    HALF = T // 2
    with ExitStack() as ctx:
        norm = Norm(c, ctx, name)
        sb = lambda n, s, d=F32: ctx.enter_context(nc.sbuf_tensor(f"{name}_{n}", s, d))
        raw = sb("raw", [P, 2, 3, D])
        wh, wl = sb("wh", [P, 2, 3, D], F32R), sb("wl", [P, 2, 3, D], F32R)
        act_g, h = sb("silu", [P, 2, D]), sb("h", [P, 2, D])
        hh, hl = sb("hh", [P, 2, D], F32R), sb("hl", [P, 2, D], F32R)
        sem = lambda n: c.sem(f"{name}_{n}")
        in_loaded, out_loaded = [sem("in_loaded0"), sem("in_loaded1")], [sem("out_loaded0"), sem("out_loaded1")]
        in_hi, in_lo, out_hi, out_lo = sem("in_hi"), sem("in_lo"), sem("out_hi"), sem("out_lo")
        gated, silu_done = sem("gated"), sem("silu")
        h_done, h_hi, h_lo, down, summed, added = (sem("h"), sem("h_hi"), sem("h_lo"), sem("down"), sem("summed"),
                                                   sem("added"))
        gate = lambda p: c.bank(p)
        up = lambda p: c.bank(2 + p)
        accs = [c.bank(4 + t) for t in range(4)]
        CH = 2 * FC

        def chunks(eng, f, half):
            first = half * FC
            with eng.Fori(0, FC // 2) as i:
                for e in range(2):
                    f(i * 2 + (first + e), (first + e) % 2, i + (first + e) // 2)
            last = first + FC - 1
            f(last, last % 2, last // 2)

        def ahead(first, eng, second, first_end=None, second_end=None):
            def both(n, par, nth):
                for f in ((first if n < CH - 2 else first_end), (second if n < CH - 1 else second_end)):
                    if f:
                        f(n, par, nth)

            with eng.Fori(0, (CH - 2) // 2) as i:
                for e in range(2):
                    first(i * 2 + e, e, i)
                    second(i * 2 + e, e, i)
            for n in range(CH - 2, CH):
                both(n, n % 2, n // 2)

        with nc.Block() as block:

            @block.sync
            def _(sp):
                def load(n, par, half):
                    src = c.wd[bass.ds(n - half * FC, 1), :, :].rearrange("o p (m n) -> (o p) m n", m=3)
                    sp.wait_ge(in_lo, n + 1)
                    sp.dma_start(raw[:, par, 0:2, :], src[:, 0:2, :]).then_inc(in_loaded[par], 16)
                    sp.wait_ge(out_lo, n + 1)
                    sp.dma_start(raw[:, par, 2, :], src[:, 2, :]).then_inc(out_loaded[par], 16)
                for half in range(2):
                    chunks(sp, lambda n, par, nth: load(n, par, half), half)

            @block.gpsimd
            def _(pool):
                pool.sem_inc(in_lo, 2)
                pool.sem_inc(out_lo, 2)

                def in_low(n, par):
                    pool.wait_ge(in_hi, n + 1)
                    nc.gpsimd.tensor_tensor(wl[:, par, 0:2, :], raw[:, par, 0:2, :], f32(wh[:, par, 0:2, :]),
                                            ALU.subtract).then_inc(in_lo, 1)

                def out_low(n, par):
                    pool.wait_ge(out_hi, n + 1)
                    nc.gpsimd.tensor_tensor(wl[:, par, 2, :], raw[:, par, 2, :], f32(wh[:, par, 2, :]), ALU.subtract
                                            ).then_inc(out_lo, 1)

                in_low(0, 0)
                in_low(1, 1)
                out_low(0, 0)
                ahead(lambda n, par, nth: in_low(n + 2, par), pool, lambda n, par, nth: out_low(n + 1, 1 - par))

            @block.tensor
            def _(pe):
                pe.sem_inc(down, 2)
                pe.sem_inc(gated, 2)

                def gate_up(n, par, half):
                    pe.wait_ge(in_lo, n + 3)
                    pe.wait_ge(h_done, n + 1)
                    for m, bank in ((0, gate(par)), (1, up(par))):
                        pairs = []
                        for k in range(KT):
                            w = [x[:, par, m, k * P:(k + 1) * P] for x in (wh, wl)]
                            z = [x[:, k, half * HALF:(half + 1) * HALF] for x in (c.ZH, c.ZL)]
                            pairs += three(*w, *z)
                        last = passes(pe, bank, pairs)
                    last.then_inc(gated, 1)

                def down_of(n, par, stop=False):
                    pe.wait_ge(h_lo, n + 3)
                    pe.wait_ge(out_lo, n + 3)
                    for t in range(4):
                        hhl = [x[:, par, t * P:(t + 1) * P] for x in (hh, hl)]
                        last = passes(pe, accs[t], three(*hhl, wh[:, par, 2, :], wl[:, par, 2, :]), start=False, stop=stop)
                    last.then_inc(down, 1)

                for t in range(TT):
                    norm.turn(pe, t)
                pe.wait_ge(norm.lo_done, TT)
                for half in range(2):
                    first = half * FC
                    if half:
                        pe.wait_ge(added, 4)
                    for t in range(4):
                        pe.matmul(accs[t], c.zero_bf[:, 0:P], c.zero_bf[:, :], start=True, stop=False)
                    gate_up(first, first % 2, half)
                    with pe.Fori(0, FC // 2) as i:
                        for e in range(2):
                            gate_up(i * 2 + (first + e + 1), (first + e + 1) % 2, half)
                            down_of(i * 2 + (first + e), (first + e) % 2)
                    down_of(first + FC - 1, (first + FC - 1) % 2, stop=True)

            @block.scalar
            def _(act):
                act.sem_inc(h_hi, 2)
                norm.scalar_std(act)
                for t in range(TT):
                    norm.scalar_hi(act, t)

                def in_high(n, par, nth):
                    act.wait_ge(in_loaded[par], nth * 16 + 16)
                    act.wait_ge(gated, n + 1)
                    nc.scalar.activation(wh[:, par, 0:2, :], raw[:, par, 0:2, :], ACT.Copy).then_inc(in_hi, 1)

                def out_high(n, par, nth):
                    act.wait_ge(out_loaded[par], nth * 16 + 16)
                    act.wait_ge(down, n + 1)
                    nc.scalar.activation(wh[:, par, 2, :], raw[:, par, 2, :], ACT.Copy).then_inc(out_hi, 1)

                def silu(n, par):
                    act.wait_ge(gated, n + 3)
                    act.wait_ge(h_done, n + 1)
                    nc.scalar.activation(act_g[:, par, :], gate(par), ACT.Silu).then_inc(silu_done, 1)

                def h_high(n, par):
                    act.wait_ge(h_done, n + 3)
                    act.wait_ge(down, n + 1)
                    nc.scalar.activation(hh[:, par, :], h[:, par, :], ACT.Copy).then_inc(h_hi, 1)

                in_high(0, 0, 0)
                in_high(1, 1, 0)
                out_high(0, 0, 0)

                def first(n, par, nth):
                    silu(n, par)
                    in_high(n + 2, par, nth + 1)

                def second(n, par, nth):
                    h_high(n, par)
                    out_high(n + 1, 1 - par, nth + par)

                ahead(first, act, second, lambda n, par, nth: silu(n, par), lambda n, par, nth: h_high(n, par))

            @block.vector
            def _(dve):
                dve.sem_inc(h_done, 2)
                dve.sem_inc(h_lo, 2)
                norm.vector(dve)

                def hidden(n, par, nth):
                    dve.wait_ge(silu_done, n + 1)
                    dve.wait_ge(h_lo, n + 1)
                    nc.vector.tensor_tensor(h[:, par, :], act_g[:, par, :], up(par), ALU.mult).then_inc(h_done, 1)
                    dve.wait_ge(h_hi, n + 3)
                    nc.vector.tensor_tensor(hl[:, par, :], h[:, par, :], f32(hh[:, par, :]), ALU.subtract
                                            ).then_inc(h_lo, 1)

                for half in range(2):
                    chunks(dve, hidden, half)
                    dve.wait_ge(down, (half + 1) * FC + 2)
                    for t in range(4):
                        x = c.X[:, 4 * half + t, :]
                        nc.vector.scalar_tensor_tensor(x, accs[t], 0.5, x, ALU.mult, ALU.add).then_inc(added, 1)


def latents(c):
    nc = c.nc
    with ExitStack() as ctx:
        norm = Norm(c, ctx, "lt_norm")
        sb = lambda n, s, d=F32: ctx.enter_context(nc.sbuf_tensor(f"lt_{n}", s, d))
        sem = lambda n: c.sem(f"lt_{n}")
        w = sb("w", [P, KT, PROJ])
        wh, wl = sb("wh", [P, KT, PROJ], F32R), sb("wl", [P, KT, PROJ], F32R)
        pj, junk, ss = sb("pj", [P, TT, PROJ]), sb("junk", [P, Q_RANK]), sb("ss", [P, 2, TT])
        qw, kw, cos, sin = sb("qw", [P, Q_RANK]), sb("kw", [P, KV_RANK]), sb("cos", [P, 2, ROPE]), sb("sin", [P, 2, ROPE])
        tmp, u, rot = sb("tmp", [P, 5, 2 * TT]), sb("u", [P, 2, 512]), sb("rot", [P, 2, 2, ROPE])
        w_loaded, w_hi, w_lo, tables = sem("w_loaded"), sem("w_hi"), sem("w_lo"), sem("tables")
        projected, copied, squared, ms_ready, rms_ready, chain = (sem("projected"), sem("copied"), sem("squared"),
                                                                  sem("ms"), sem("rms"), sem("chain"))
        turned_part, u_ready, u_turned, u_hi, u_lo = sem("part"), sem("u"), sem("u_turned"), sem("u_hi"), sem("u_lo")
        v_base, v_hi, iw_done = sem("v"), sem("v_hi"), sem("iw")
        KV0, KP0, IK0, IW0 = Q_RANK, Q_RANK + KV_RANK, Q_RANK + KV_RANK + ROPE, PROJ - IDX_H
        with nc.Block() as block:

            def sums(act, t):
                bank = c.bank(2 + t % 2)
                act.wait_ge(projected, t + 1)
                nc.scalar.activation(pj[:, t, :], bank[:, 0:PROJ], ACT.Copy).then_inc(copied, 1)
                if t:
                    act.wait_ge(squared, 2 * t)
                nc.scalar.activation(junk[:, 0:Q_RANK], bank[:, 0:Q_RANK], ACT.Square,
                                     accum_out=ss[:, 0, t:t + 1]).then_inc(squared, 1)
                act.wait_ge(squared, 2 * t + 1)
                nc.scalar.activation(junk[:, 0:KV_RANK], bank[:, KV0:KP0], ACT.Square,
                                     accum_out=ss[:, 1, t:t + 1]).then_inc(squared, 1)

            @block.sync
            def _(sp):
                sp.dma_start(w[:, :, :], c.ins["proj"].rearrange("(k p) n -> p k n", p=P)).then_inc(w_loaded, 16)
                sp.dma_start(qw[:, :], c.ins["q_norm"].partition_broadcast(P)).then_inc(tables, 16)
                sp.dma_start(kw[:, :], c.ins["kv_norm"].partition_broadcast(P)).then_inc(tables, 16)
                sp.dma_start(cos[:, :, :], c.ins["key_cos"].rearrange("(h p) n -> p h n", p=P)).then_inc(tables, 16)
                sp.dma_start(sin[:, :, :], c.ins["key_sin"].rearrange("(h p) n -> p h n", p=P)).then_inc(tables, 16)

            @block.gpsimd
            def _(pool):
                pool.wait_ge(w_hi, 1)
                nc.gpsimd.tensor_tensor(wl[:, :, :], w[:, :, :], f32(wh[:, :, :]), ALU.subtract).then_inc(w_lo, 1)

            @block.tensor
            def _(pe):
                def project(t):
                    pe.wait_ge(norm.lo_done, t + 1)
                    if t >= 2:
                        pe.wait_ge(squared, 2 * t - 2)
                    pairs = []
                    for k in range(KT):
                        z = [x[:, k, t * P:(t + 1) * P] for x in (c.ZH, c.ZL)]
                        pairs += three(*z, wh[:, k, :], wl[:, k, :])
                    passes(pe, c.bank(2 + t % 2)[:, 0:PROJ], pairs).then_inc(projected, 1)

                for t in range(TT):
                    norm.turn(pe, t)
                    if t == 1:
                        pe.wait_ge(w_lo, 1)
                    if t:
                        project(t - 1)
                project(TT - 1)
                for t in range(TT):
                    pe.wait_ge(u_ready, t + 1)
                    if t >= 2:
                        pe.wait_ge(u_lo, 2 * t - 2)
                    for k in range(4):
                        last = pe.transpose(c.bank(4 + t % 2)[:, k * P:(k + 1) * P], u[:, t % 2, k * P:(k + 1) * P],
                                            c.ident[:, :])
                    last.then_inc(u_turned, 1)

            @block.scalar
            def _(act):
                act.wait_ge(w_loaded, 16)
                nc.scalar.activation(wh[:, :, :], w[:, :, :], ACT.Copy).then_inc(w_hi, 1)
                norm.scalar_std(act)
                for t in range(TT):
                    norm.scalar_hi(act, t)
                    if t:
                        sums(act, t - 1)
                sums(act, TT - 1)
                act.wait_ge(ms_ready, 1)
                nc.scalar.activation(tmp[:, 1, :], tmp[:, 0, :], ACT.Sqrt).then_inc(rms_ready, 1)
                for t in range(TT):
                    act.wait_ge(u_turned, t + 1)
                    bank = c.bank(4 + t % 2)
                    nc.scalar.activation(c.UH[:, :, t * P:(t + 1) * P],
                                         bank[:, 0:3 * P].rearrange("p (k n) -> p k n", k=3), ACT.Copy
                                         ).then_inc(u_hi, 1)
                    nc.scalar.activation(c.IKH[:, t * P:(t + 1) * P], bank[:, 3 * P:], ACT.Copy).then_inc(u_hi, 1)
                act.wait_ge(v_base, TT + 1)
                nc.scalar.activation(c.VH[:, :, :], c.V[:, :, :], ACT.Copy).then_inc(v_hi, 1)

            @block.vector
            def _(dve):
                norm.vector(dve)
                nc.vector.memset(c.V[:, :, :], 0.0).then_inc(v_base, 1)
                dve.wait_ge(squared, 2 * TT)
                ms, rms, r0, a, rinv = (tmp[:, i, :] for i in range(5))
                for i, n in enumerate((Q_RANK, KV_RANK)):
                    nc.vector.tensor_scalar(ms[:, i * TT:(i + 1) * TT], ss[:, i, :], 1.0 / n, EPS, ALU.mult, ALU.add
                                            ).then_inc(ms_part := c.sem(f"lt_ms{i}"), 1)
                    dve.wait_ge(ms_part, 1)
                dve.sem_inc(ms_ready, 1)
                dve.wait_ge(rms_ready, 1)
                newton(nc, dve, chain, ms, rms, r0, a, rinv)
                dve.wait_ge(copied, TT)
                dve.wait_ge(tables, 64)
                nc.vector.tensor_scalar(c.IW[:, :, :], pj[:, :, IW0:PROJ], float(IDX_H) ** -0.5, float(IDX_D) ** -0.5,
                                        ALU.mult, ALU.mult).then_inc(iw_done, 1)
                dve.wait_ge(v_base, 1)

                def u_low(t):
                    dve.wait_ge(u_hi, 2 * t + 2)
                    cols, bank = slice(t * P, (t + 1) * P), c.bank(4 + t % 2)
                    nc.vector.tensor_tensor(c.UL[:, :, cols], bank[:, 0:3 * P].rearrange("p (k n) -> p k n", k=3),
                                            f32(c.UH[:, :, cols]), ALU.subtract).then_inc(u_lo, 1)
                    nc.vector.tensor_tensor(c.IKL[:, cols], bank[:, 3 * P:], f32(c.IKH[:, cols]), ALU.subtract
                                            ).then_inc(u_lo, 1)

                parts = 0
                for t in range(TT):
                    row, par, x = u[:, t % 2, :], t % 2, pj[:, t, :]
                    if t >= 2:
                        dve.wait_ge(u_turned, t - 1)
                    rq, rk = rinv[:, t:t + 1], rinv[:, TT + t:TT + t + 1]
                    nc.vector.scalar_tensor_tensor(row[:, 0:Q_RANK], x[:, 0:Q_RANK], rq, qw[:, :], ALU.mult, ALU.mult
                                                   ).then_inc(turned_part, 1)
                    nc.vector.scalar_tensor_tensor(row[:, Q_RANK:256], x[:, P:Q_RANK], rq, qw[:, P:Q_RANK],
                                                   ALU.mult, ALU.mult).then_inc(turned_part, 1)
                    nc.vector.scalar_tensor_tensor(row[:, 256:320], x[:, KV0:KP0], rk, kw[:, :], ALU.mult, ALU.mult
                                                   ).then_inc(turned_part, 1)
                    nc.vector.scalar_tensor_tensor(c.V[:, t, 64:128], x[:, KV0:KP0], rk, kw[:, :], ALU.mult, ALU.mult
                                                   ).then_inc(v_base, 1)
                    pe_ = x[:, KP0:IK0]
                    halves = lambda ap: ap.rearrange("p (q s f) -> p q s f", q=2, s=2)
                    r = rot[:, par, :, :]
                    nc.vector.tensor_tensor(r[:, 0, :], pe_, cos[:, par, :], ALU.mult).then_inc(turned_part, 1)
                    for s in range(2):
                        nc.vector.tensor_tensor(halves(r[:, 1, :])[:, :, s, :], halves(pe_)[:, :, 1 - s, :],
                                                halves(sin[:, par, :])[:, :, s, :], ALU.mult).then_inc(turned_part, 1)
                    nc.vector.tensor_copy(row[:, 384:512], x[:, IK0:IW0]).then_inc(turned_part, 1)
                    parts += 7
                    dve.wait_ge(turned_part, parts)
                    nc.vector.tensor_tensor(row[:, 320:384], r[:, 0, :], r[:, 1, :], ALU.add).then_inc(u_ready, 1)
                    if t:
                        u_low(t - 1)
                u_low(TT - 1)
                dve.wait_ge(v_hi, 1)
                nc.vector.tensor_tensor(c.VL[:, :, :], c.V[:, :, :], f32(c.VH[:, :, :]), ALU.subtract).then_inc(v_hi, 1)


def indexer(c):
    nc = c.nc
    with ExitStack() as ctx:
        sb = lambda n, s, d=F32: ctx.enter_context(nc.sbuf_tensor(f"ix_{n}", s, d))
        sem = lambda n: c.sem(f"ix_{n}")
        raw = sb("raw", [P, 2, KT, IDX_D])
        wh, wl = sb("wh", [P, 2, KT, IDX_D], F32R), sb("wl", [P, 2, KT, IDX_D], F32R)
        qh, ql = sb("qh", [P, 2, B * P], F32R), sb("ql", [P, 2, B * P], F32R)
        relu = sb("relu", [P, 2, B, S])
        score, work, same = sb("score", [P, B, S]), sb("work", [P, B, S]), sb("same", [P, B, S])
        max8 = sb("max8", [P, B, 8])
        loaded = [sem("loaded0"), sem("loaded1")]
        w_hi, w_lo, q_done, q_hi, q_lo = ( sem("w_hi"), sem("w_lo"), sem("q"), sem("q_hi"),
                                                  sem("q_lo"))
        scored, relued, summed = sem("scored"), sem("relu"), sem("summed")
        step = sem("step")
        base, masked, found, replaced, compared = sem("base"), sem("masked"), sem("found"), sem("replaced"), sem("same")
        pairs_of_heads = IDX_H // 2

        def heads(eng, f):
            with eng.Fori(0, pairs_of_heads) as i:
                for e in range(2):
                    f(i * 2 + e, e, i)

        with nc.Block() as block:

            @block.sync
            def _(sp):
                def load(n, par, nth):
                    sp.wait_ge(w_lo, n + 1)
                    sp.dma_start(raw[:, par, :, :], c.ins["idx_wq"].rearrange("(k p) n -> p k n", p=P)
                                 [:, :, bass.ds(n * IDX_D, IDX_D)]).then_inc(loaded[par], 16)
                heads(sp, load)

            @block.gpsimd
            def _(pool):
                pool.sem_inc(w_lo, 2)
                nc.gpsimd.memset(c.mask[:, :, :, :], 0.0).then_inc(masked, 1)
                pool.wait_ge(masked, 1)
                nc.gpsimd.affine_select(out=c.mask[:, :, 0, :], in_=c.mask[:, :, 0, :], compare_op=ALU.is_ge, fill=NEG,
                                        base=0, pattern=[[0, B], [-1, S]], channel_multiplier=1).then_inc(masked, 1)

                def w_low(n, par, nth):
                    pool.wait_ge(w_hi, n + 1)
                    nc.gpsimd.tensor_tensor(wl[:, par, :, :], raw[:, par, :, :], f32(wh[:, par, :, :]), ALU.subtract
                                            ).then_inc(w_lo, 1)
                heads(pool, w_low)
                pool.wait_ge(summed, IDX_H * B + 2 * B)
                nc.gpsimd.affine_select(out=work[:, :, :], in_=score[:, :, :], compare_op=ALU.is_ge, fill=NEG,
                                        base=P, pattern=[[0, B], [-1, S]], channel_multiplier=1).then_inc(base, 1)

            @block.tensor
            def _(pe):
                pe.sem_inc(q_done, 2)
                def head(n, par):
                    pe.wait_ge(w_lo, n + 3)
                    pe.wait_ge(q_lo, n + 1)
                    pairs = []
                    for k in range(KT):
                        z = [x[:, k, :].rearrange("p (b s) -> p b s", b=B)[:, :, P:S] for x in (c.ZH, c.ZL)]
                        pairs += three(wh[:, par, k, :], wl[:, par, k, :], *z)
                    passes(pe, c.bank(par), pairs).then_inc(q_done, 1)

                def score_of(n, par):
                    pe.wait_ge(q_lo, n + 3)
                    pe.wait_ge(relued, n + 1)
                    for b in range(B):
                        q = [x[:, par, b * P:(b + 1) * P] for x in (qh, ql)]
                        k = [x[:, b * S:(b + 1) * S] for x in (c.IKH, c.IKL)]
                        out = c.bank(2 + 2 * par + b // 2)[:, (b % 2) * S:(b % 2 + 1) * S]
                        last = passes(pe, out, three(*q, *k))
                    last.then_inc(scored, 1)

                heads(pe, lambda n, par, nth: (head(n, par), score_of(n, par)))

            @block.scalar
            def _(act):
                act.sem_inc(relued, 2)
                def head(n, par, nth):
                    act.wait_ge(loaded[par], nth * 16 + 16)
                    act.wait_ge(q_done, n + 1)
                    nc.scalar.activation(wh[:, par, :, :], raw[:, par, :, :], ACT.Copy).then_inc(w_hi, 1)
                    act.wait_ge(q_done, n + 3)
                    act.wait_ge(scored, n + 1)
                    nc.scalar.activation(qh[:, par, :], c.bank(par), ACT.Copy).then_inc(q_hi, 1)
                    act.wait_ge(scored, n + 3)
                    act.wait_ge(summed, n * B + 1)
                    nc.scalar.activation(relu[:, par, :, :].rearrange("p b s -> p (b s)"),
                                         c.banks(2 + 2 * par, 2), ACT.Relu).then_inc(relued, 1)
                heads(act, head)

            @block.vector
            def _(dve):
                dve.sem_inc(q_lo, 2)
                dve.sem_inc(scored, 2)
                dve.sem_inc(summed, 2 * B)
                nc.vector.memset(score[:, :, :], 0.0).then_inc(found_zero := sem("score_zero"), 1)
                dve.wait_ge(found_zero, 1)
                def head(n, par, nth):
                    dve.wait_ge(q_hi, n + 1)
                    dve.wait_ge(scored, n + 1)
                    nc.vector.tensor_tensor(ql[:, par, :], c.bank(par), f32(qh[:, par, :]), ALU.subtract).then_inc(q_lo, 1)
                    dve.wait_ge(relued, n + 3)
                    for b in range(B):
                        dve.wait_ge(summed, n * B + (B + 1 + b))
                        nc.vector.scalar_tensor_tensor(score[:, b, :], relu[:, par, b, :],
                                                       c.IW[:, 2 * b + 1, bass.ds(n, 1)], score[:, b, :],
                                                       ALU.mult, ALU.add).then_inc(summed, 1)
                heads(dve, head)
                dve.wait_ge(base, 1)
                nc.vector.tensor_copy(score[:, :, :], work[:, :, :]).then_inc(base, 1)
                dve.wait_ge(base, 2)
                dve.sem_inc(replaced, B)
                with dve.Fori(0, TOPK // 8) as r:
                    dve.wait_ge(replaced, r * B + B)
                    dve.sem_inc(step, 1)
                    for b in range(B):
                        nc.vector.max(max8[:, b, :], work[:, b, :]).then_inc(found, 1)
                    dve.wait_ge(found, r * B + B)
                    dve.sem_inc(step, 1)
                    for b in range(B):
                        nc.vector.match_replace(work[:, b, :], max8[:, b, :], work[:, b, :], 10 * NEG
                                                ).then_inc(replaced, 1)
                dve.wait_ge(replaced, B + TOPK // 8 * B)
                nc.vector.tensor_tensor(same[:, :, :], score[:, :, :], work[:, :, :], ALU.is_equal).then_inc(compared, 1)
                dve.wait_ge(compared, 1)
                dve.wait_ge(masked, 2)
                nc.vector.tensor_scalar(c.mask[:, :, 1, :], same[:, :, :], NEG, None, ALU.mult).then_inc(compared, 1)


def attention0(c):
    nc = c.nc
    NPR = G0 // 2
    NU = B * NPR
    NQ = 2 * G0
    HALF = T // 2
    with ExitStack() as ctx:
        sb = lambda n, s, d=F32: ctx.enter_context(nc.sbuf_tensor(f"a0_{n}", s, d))
        sem = lambda n: c.sem(f"a0_{n}")
        raw = sb("raw", [P, R0])
        o = 0
        views = []
        for n in (R_QN, R_KK, R_KV, R_OW, R_PE):
            views.append(raw[:, o:o + n])
            o += n
        qn = views[0].rearrange("p (h n) -> p h n", h=G0)
        kk = views[1].rearrange("p (h n) -> p h n", h=G0)
        kv = views[2].rearrange("p (h n) -> p h n", h=G0)
        ow = views[3].rearrange("p (h n) -> p h n", h=G0)
        qpe = views[4].rearrange("p (h c n) -> p h c n", h=G0, c=2)
        w1h, w1l, w2 = sb("w1h", [P, G0, P], F32R), sb("w1l", [P, G0, P], F32R), sb("w2", [P, G0, P], F32R)
        w2t = sb("w2t", [P, G0, P], F32R)
        woh, wol = sb("woh", [P, NPR, D], F32R), sb("wol", [P, NPR, D], F32R)
        qf, vc, sw = sb("qf", [P, 2, HALF]), sb("vc", [P, 2, HALF]), sb("sw", [P, 2, HALF])
        cosq, sinq = sb("cosq", [P, S]), sb("sinq", [P, S])
        qh, ql = sb("qh", [P, G0, T], F32R), sb("ql", [P, G0, T], F32R)
        prob = sb("prob", [P, 2, 2, 2, S])
        nmax, den, rec = sb("nmax", [P, 2, 4]), sb("den", [P, 2, 4]), sb("rec", [P, 2, 4])
        recx = sb("recx", [P, 2, 2, 2, 64])
        p0h, p0l, p1 = sb("p0h", [P, 2, 2, S], F32R), sb("p0l", [P, 2, 2, S], F32R), sb("p1", [P, 2, 2, P])
        rs, ot = sb("rs", [P, 2, S]), sb("ot", [P, 2, S])
        oh, ol = sb("oh", [P, NPR, T], F32R), sb("ol", [P, NPR, T], F32R)

        tables, loaded, absorbed, values_in = sem("tables"), sem("loaded"), sem("absorbed"), sem("values")
        w_hi, w_lo, raw_read, wo_hi, wo_lo = sem("w_hi"), sem("w_lo"), sem("raw_read"), sem("wo_hi"), sem("wo_lo")
        q_prod, q_plain, q_cos, q_swap, q_sin, q_full, q_hi, q_lo = (sem("q_prod"), sem("q_plain"), sem("q_cos"),
            sem("q_swap"), sem("q_sin"), sem("q_full"), sem("q_hi"), sem("q_lo"))
        scored, maxed, exped, turned = sem("scored"), sem("maxed"), sem("exped"), sem("turned")
        recd, spread, r_turned, r_copied = sem("recd"), sem("spread"), sem("r_turned"), sem("r_copied")
        pt_hi, pt_lo, pv_done, ot_done, o_hi, o_lo = (sem("pt_hi"), sem("pt_lo"), sem("pv"), sem("ot"), sem("o_hi"),
                                                      sem("o_lo"))
        projected, added, w_part = sem("projected"), sem("added"), sem("w_part")
        slot = lambda k: c.bank(k)
        PT0, PT1, PO, PR = c.bank(4), c.bank(5), c.bank(6), c.bank(7)
        pe_rows = slice(64, 128)
        beside = Dequant(c, ctx)
        product_slots = lambda k: range(2 * k, 2 * k + 2)
        unit_slots = lambda u: range(2 * NQ + 4 * u, 2 * NQ + 4 * u + 4)
        place = lambda u: (u % B, u // B)

        with nc.Block() as block:

            @block.sync
            def _(sp):
                sp.dma_start(cosq[pe_rows, :], c.ins["query_cos"]).then_inc(tables, 16)
                sp.dma_start(sinq[pe_rows, :], c.ins["query_sin"]).then_inc(tables, 16)
                with sp.Fori(0, NG0) as g:
                    sp.wait_ge(absorbed, g * 2 + 1)
                    sp.wait_ge(raw_read, g * 2 + 1)
                    sp.wait_ge(w_part, g * 2 + 1)
                    sp.dma_start(raw[:, :], c.ins["group0"][bass.ds(g, 1), :, :].rearrange("o p n -> (o p) n")
                                 ).then_inc(loaded, 16)

            @block.gpsimd
            def _(pool):
                pool.sem_inc(q_full, 2)
                pool.sem_inc(o_lo, 2)
                pool.wait_ge(tables, 32)
                with pool.Fori(0, NG0) as g:
                    for k in range(NQ):
                        n, par = g * NQ + k, k % 2
                        wide = sinq[pe_rows, :].unsqueeze(1).broadcast_to([64, 2, S])
                        half = lambda ap: ap.rearrange("p (b s) -> p b s", b=2)
                        if k == 0:
                            pool.wait_ge(o_lo, g * NU + 2)
                        pool.wait_ge(q_swap, n + 1)
                        nc.gpsimd.tensor_tensor(half(sw[pe_rows, par, :]), half(sw[pe_rows, par, :]), wide, ALU.mult
                                                ).then_inc(q_sin, 1)
                        pool.wait_ge(q_sin, n + 1)
                        pool.wait_ge(q_cos, n + 1)
                        pool.wait_ge(q_lo, n + 1)
                        nc.gpsimd.tensor_tensor(qf[pe_rows, par, :], vc[pe_rows, par, :], sw[pe_rows, par, :], ALU.add
                                                ).then_inc(q_full, 1)
                    pool.wait_ge(q_full, g * NQ + (NQ + 2))
                    for u in range(NU):
                        n, (b, pr) = g * NU + u, place(u)
                        pool.wait_ge(o_hi, n + 2)
                        nc.gpsimd.tensor_tensor(ol[:, pr, b * S:(b + 1) * S], ot[:, u % 2, :],
                                                f32(oh[:, pr, b * S:(b + 1) * S]), ALU.subtract).then_inc(o_lo, 1)

            @block.tensor
            def _(pe):
                pe.sem_inc(absorbed, 1)
                pe.sem_inc(q_prod, 1)
                pe.sem_inc(turned, 2)
                pe.sem_inc(pv_done, 2)
                pe.sem_inc(r_turned, 2)
                pe.sem_inc(projected, 1)

                def scores(g, u):
                    (b, pr) = place(u)
                    n = g * NU + u
                    if b == 0:
                        pe.wait_ge(q_lo, g * NQ + (2 + NQ // NPR * (pr + 1)))
                    if u < 2:
                        for read in (q_plain, q_cos, q_swap):
                            pe.wait_ge(read, g * NQ + NQ)
                    else:
                        pe.wait_ge(exped, n * 4 + 4)
                    for h in range(2):
                        out = slot(2 * (u % 2) + h)
                        pe.matmul(out, c.ident_bf[:, :], c.mask[:, b, :, :].rearrange("p t s -> p (t s)"),
                                  start=True, stop=False)
                        for t in range(2):
                            rows = slice(b * S + t * P, b * S + (t + 1) * P)
                            q = [x[:, 2 * pr + h, rows] for x in (qh, ql)]
                            k = [x[:, 2, b * S:(b + 1) * S] for x in (c.UH, c.UL)]
                            last = passes(pe, out[:, t * S:(t + 1) * S], three(*q, *k), start=False, stop=t == 1)
                    last.then_inc(scored, 1)

                def turn(g, u):
                    n = g * NU + u
                    pe.wait_ge(exped, n * 4 + 12)
                    pe.wait_ge(pt_lo, n + 1)
                    s = u % 2
                    for h in range(2):
                        pe.transpose(PT0[:, h * S:h * S + P], prob[:, s, h, 0, 0:P], c.ident[:, :])
                        pe.transpose(PT0[:, h * S + P:(h + 1) * S], prob[:, s, h, 1, 0:P], c.ident[:, :])
                        last = pe.transpose(PT1[:, h * P:(h + 1) * P], prob[:, s, h, 1, P:S], c.ident[:, :])
                    last.then_inc(turned, 1)

                def weigh(g, u):
                    n, b = g * NU + u, u % B
                    pe.wait_ge(spread, n + 1)
                    pe.wait_ge(r_copied, n + 1)
                    for t in range(2):
                        last = pe.transpose(PR[:, t * P:(t + 1) * P],
                                            recx[:, u % 2, t, :, :].rearrange("p h r -> p (h r)"), c.ident[:, :])
                    last.then_inc(r_turned, 1)
                    pe.wait_ge(pt_lo, n + 2)
                    pe.wait_ge(ot_done, n + 1)
                    for h in range(2):
                        cols = slice(64, 192) if h == 0 else slice(0, 128)
                        vh, vl, v = (x[:, 2 * b, cols] for x in (c.VH, c.VL, c.V))
                        passes(pe, PO[:, 0:S], three(vh, vl, p0h[:, u % 2, h, :], p0l[:, u % 2, h, :]), start=h == 0,
                               stop=False)
                        last = pe.matmul(PO[:, P:S], c.V[:, 2 * b + 1, cols], p1[:, u % 2, h, :], start=False,
                                         stop=h == 1)
                    last.then_inc(pv_done, 1)

                with pe.Fori(0, NG0) as g:
                    pe.wait_ge(loaded, g * 16 + 16)
                    pe.wait_ge(r_copied, g * NU + 1)
                    for h in range(G0):
                        for ch in range(2):
                            last = pe.matmul(PR[:, (2 * h + ch) * 64:(2 * h + ch + 1) * 64], qn[:, h, ch * P:(ch + 1) * P],
                                             kk[:, h, :], start=True, stop=True)
                    last.then_inc(absorbed, 1)
                    pe.wait_ge(added, g * TT + 1)
                    for h in range(G0):
                        rows = slice(64 * (h % 2), 64 * (h % 2) + 64)
                        last = pe.matmul(slot(h // 2)[rows, :], kv[:, h, :], ow[:, h, :], start=True, stop=True)
                    last.then_inc(absorbed, 1)
                    pe.wait_ge(w_lo, g + 1)
                    for k in range(NQ):
                        h, half = k // 2, k % 2
                        bank = (k + 2) % 4
                        if k in (2, 3):
                            pe.wait_ge(wo_lo, g + 1)
                        if k >= 4:
                            pe.wait_ge(q_cos, g * NQ + (k - 3))
                            pe.wait_ge(q_swap, g * NQ + (k - 3))
                            pe.wait_ge(q_plain, g * NQ + (k - 3))
                        toks = slice(half * HALF, (half + 1) * HALF)
                        q1h, q1l, q2h, q2l = c.UH[:, 0, toks], c.UL[:, 0, toks], c.UH[:, 1, toks], c.UL[:, 1, toks]
                        pairs = three(w1h[:, h, :], w1l[:, h, :], q1h, q1l) + [(w2[:, h, :], q2h), (w2[:, h, :], q2l)]
                        passes(pe, slot(bank), pairs).then_inc(q_prod, 1)
                    scores(g, 0)
                    scores(g, 1)
                    for u in range(NU):
                        turn(g, u)
                        if u + 2 < NU:
                            scores(g, u + 2)
                        if u:
                            weigh(g, u - 1)
                    weigh(g, NU - 1)
                    pe.wait_ge(o_lo, g * NU + (NU + 2))
                    for t in range(TT):
                        if t >= 4:
                            pe.wait_ge(added, g * TT + (t - 3 + 1))
                        pairs = []
                        for pr in range(NPR):
                            x = [y[:, pr, t * P:(t + 1) * P] for y in (oh, ol)]
                            pairs += three(*x, woh[:, pr, :], wol[:, pr, :])
                        passes(pe, slot(t % 4), pairs).then_inc(projected, 1)

            @block.scalar
            def _(act):
                act.sem_inc(r_copied, 1)
                act.sem_inc(exped, 8)
                act.sem_inc(o_hi, 1)
                beside.scalar_begin(act)
                act.wait_ge(tables, 32)
                with act.Fori(0, NG0) as g:
                    act.wait_ge(absorbed, g * 2 + 2)
                    act.wait_ge(q_prod, g * NQ + 1)
                    absw = PR.rearrange("p (h c n) -> p h c n", h=G0, c=2)
                    for part, src in ((slice(0, 64), absw), (slice(64, 128), qpe)):
                        nc.scalar.activation(w1h[:, :, part], src[:, :, 0, :], ACT.Copy).then_inc(w_hi, 1)
                        nc.scalar.activation(w2[0:64, :, part], src[0:64, :, 1, :], ACT.Copy).then_inc(w_hi, 1)
                        nc.scalar.activation(w2t[64:128, :, part], src[64:128, :, 1, :], ACT.Copy).then_inc(w_hi, 1)
                    act.wait_ge(absorbed, g * 2 + 3)
                    act.wait_ge(projected, g * TT + 1)
                    nc.scalar.activation(woh[:, :, :].rearrange("p a n -> p (a n)"), c.banks(0, 2), ACT.Copy
                                         ).then_inc(wo_hi, 1)

                    def q_high(k):
                        act.wait_ge(q_full, g * NQ + (k + 3))
                        act.wait_ge(q_plain, g * NQ + (k + 1))
                        h, half = k // 2, k % 2
                        toks = slice(half * HALF, (half + 1) * HALF)
                        if k == 0:
                            act.wait_ge(scored, g * NU + 1)
                        nc.scalar.activation(qh[:, h, toks], qf[:, k % 2, :], ACT.Copy).then_inc(q_hi, 1)

                    for k in range(NQ):
                        act.wait_ge(q_prod, g * NQ + (k + 2))
                        act.wait_ge(q_lo, g * NQ + (k + 1))
                        nc.scalar.activation(qf[0:64, k % 2, :], slot((k + 2) % 4)[0:64, :], ACT.Copy, scale=SCALE0
                                             ).then_inc(q_plain, 1)
                        if k:
                            q_high(k - 1)
                        for slot_ in product_slots(k):
                            beside.scalar(act, Group(g, 0), slot_)
                    q_high(NQ - 1)

                    def exps(u):
                        n, s = g * NU + u, u % 2
                        act.wait_ge(maxed, n + 1)
                        act.wait_ge(turned, n + 1)
                        act.wait_ge(recd, n + 1)
                        for h in range(2):
                            for t in range(2):
                                w = (t + 1) * P
                                nc.scalar.activation(prob[:, s, h, t, 0:w], slot(2 * s + h)[:, t * S:t * S + w], ACT.Exp,
                                                     bias=nmax[:, s, 2 * h + t:2 * h + t + 1],
                                                     accum_out=den[:, s, 2 * h + t:2 * h + t + 1]).then_inc(exped, 1)

                    def o_high(u):
                        n, (b, pr) = g * NU + u, place(u)
                        act.wait_ge(ot_done, n + 2)
                        if u == 0:
                            act.wait_ge(projected, g * TT + 1)
                        nc.scalar.activation(oh[:, pr, b * S:(b + 1) * S], ot[:, u % 2, :], ACT.Copy).then_inc(o_hi, 1)

                    def r_copy(u):
                        n = g * NU + u
                        act.wait_ge(r_turned, n + 3)
                        act.wait_ge(ot_done, n + 1)
                        nc.scalar.activation(rs[:, u % 2, :], PR[:, 0:S], ACT.Copy).then_inc(r_copied, 1)

                    exps(0)
                    for u in range(NU):
                        n = g * NU + u
                        act.wait_ge(turned, n + 3)
                        act.wait_ge(pv_done, n + 1)
                        nc.scalar.activation(p0h[:, u % 2, :, :].rearrange("p h s -> p (h s)"), PT0, ACT.Copy
                                             ).then_inc(pt_hi, 1)
                        nc.scalar.activation(p1[:, u % 2, :, :].rearrange("p h s -> p (h s)"), PT1[:, 0:2 * P], ACT.Copy
                                             ).then_inc(pt_hi, 1)
                        if u + 1 < NU:
                            exps(u + 1)
                        if u:
                            r_copy(u - 1)
                        if u >= 2:
                            o_high(u - 2)
                        for slot_ in unit_slots(u):
                            beside.scalar(act, Group(g, 0), slot_)
                    r_copy(NU - 1)
                    o_high(NU - 2)
                    o_high(NU - 1)
                beside.store(act, Group(None, NG0), -1)
                for j in range(3):
                    act.wait_ge(beside.stored[j], 16 * NG0 + 16)
                    act.wait_ge(beside.loaded[j], 16 * NG0 + (16 if j < 2 else 0))

            @block.vector
            def _(dve):
                dve.sem_inc(raw_read, 1)
                dve.sem_inc(q_lo, 2)
                dve.sem_inc(w_part, 1)
                dve.sem_inc(recd, 2)
                dve.sem_inc(pt_lo, 1)
                dve.sem_inc(ot_done, 1)
                dve.sem_inc(added, 1)
                dve.sem_inc(scored, 1)
                beside.vector_begin(dve)
                dve.wait_ge(tables, 32)
                with dve.Fori(0, NG0) as g:
                    absw = PR.rearrange("p (h c n) -> p h c n", h=G0, c=2)
                    dve.wait_ge(w_hi, g * 6 + 6)
                    for part, src in ((slice(0, 64), absw), (slice(64, 128), qpe)):
                        nc.vector.tensor_tensor(w1l[:, :, part], src[:, :, 0, :], f32(w1h[:, :, part]), ALU.subtract
                                                ).then_inc(raw_read, 1)
                        last = nc.vector.tensor_tensor(w2[64:128, :, part], src[64:128, :, 1, :],
                                                       f32(w2t[64:128, :, part]), ALU.subtract)
                        last.then_inc(w_part, 1)
                    dve.wait_ge(raw_read, g * 2 + 3)
                    dve.wait_ge(w_part, g * 2 + 3)
                    dve.sem_inc(w_lo, 1)
                    dve.wait_ge(wo_hi, g + 1)
                    nc.vector.tensor_tensor(wol[:, :, :].rearrange("p a n -> p (a n)"), c.banks(0, 2),
                                            f32(woh[:, :, :]).rearrange("p a n -> p (a n)"), ALU.subtract).then_inc(wo_lo, 1)

                    def q_low(k):
                        h, half = k // 2, k % 2
                        toks = slice(half * HALF, (half + 1) * HALF)
                        dve.wait_ge(q_hi, g * NQ + (k + 1))
                        nc.vector.tensor_tensor(ql[:, h, toks], qf[:, k % 2, :], f32(qh[:, h, toks]), ALU.subtract
                                                ).then_inc(q_lo, 1)

                    for k in range(NQ):
                        n, par = g * NQ + k, k % 2
                        bank = slot((k + 2) % 4)
                        half = lambda ap: ap.rearrange("p (b s) -> p b s", b=2)
                        dve.wait_ge(q_prod, n + 2)
                        dve.wait_ge(q_full, n + 1)
                        nc.vector.tensor_tensor(half(vc[pe_rows, par, :]), half(bank[pe_rows, :]),
                                                cosq[pe_rows, :].unsqueeze(1).broadcast_to([64, 2, S]), ALU.mult
                                                ).then_inc(q_cos, 1)
                        nc.vector.stream_shuffle(sw[pe_rows, par, :], bank[pe_rows, :], SWAP16).then_inc(q_swap, 1)
                        if k:
                            q_low(k - 1)
                            for slot_ in product_slots(k - 1):
                                beside.vector(dve, Group(g, 0), slot_)
                        if k == 4:
                            beside.prepare(dve, Group(g, 0), 1)

                    q_low(NQ - 1)

                    def maxes(u):
                        n, s = g * NU + u, u % 2
                        dve.wait_ge(scored, n + 2)
                        dve.wait_ge(exped, n * 4 + 4)
                        nc.vector.tensor_reduce(nmax[:, s, :], c.banks(2 * s, 2).rearrange("p (a n) -> p a n", a=4),
                                                AX_X, ALU.max, negate=True).then_inc(maxed, 1)

                    def outputs(u):
                        n, (b, pr) = g * NU + u, place(u)
                        dve.wait_ge(pv_done, n + 3)
                        dve.wait_ge(r_copied, n + 2)
                        dve.wait_ge(o_lo, n + 1)
                        nc.vector.tensor_tensor(ot[:, u % 2, :], PO[:, 0:S], rs[:, u % 2, :], ALU.mult).then_inc(ot_done, 1)

                    maxes(0)
                    for u in range(NU):
                        n, s = g * NU + u, u % 2
                        if u + 1 < NU:
                            maxes(u + 1)
                        dve.wait_ge(exped, n * 4 + 12)
                        nc.vector.reciprocal(rec[:, s, :], den[:, s, :]).then_inc(recd, 1)
                        dve.wait_ge(recd, n + 3)
                        dve.wait_ge(r_turned, n + 1)
                        nc.vector.tensor_copy(recx[:, s, :, :, :],
                                              rec[:, s, :].rearrange("p (h t) -> p t h", h=2).unsqueeze(3)
                                              .broadcast_to([P, 2, 2, 64])).then_inc(spread, 1)
                        dve.wait_ge(pt_hi, n * 2 + 2)
                        flat = lambda ap: ap.rearrange("p h s -> p (h s)")
                        nc.vector.tensor_tensor(flat(p0l[:, s, :, :]), PT0, flat(f32(p0h[:, s, :, :])), ALU.subtract
                                                ).then_inc(pt_lo, 1)
                        if u >= 2:
                            outputs(u - 2)
                        for slot_ in unit_slots(u - 1) if u else product_slots(NQ - 1):
                            beside.vector(dve, Group(g, 0), slot_)
                        if u in (0, 4):
                            beside.finish(dve, Group(g, 0), u // 4)
                        if u in (2, 5):
                            beside.prepare(dve, Group(g, 0), 2 + u // 5)
                    outputs(NU - 2)
                    outputs(NU - 1)
                    for t in range(TT):
                        dve.wait_ge(projected, g * TT + (t + 2))
                        nc.vector.tensor_tensor(c.X[:, t, :], slot(t % 4), c.X[:, t, :], ALU.add).then_inc(added, 1)
                    for slot_ in unit_slots(NU - 1):
                        beside.vector(dve, Group(g, 0), slot_)
                    beside.finish(dve, Group(g, 0), 2)


def gather(c, ctx):
    idx = ctx.enter_context(c.nc.sbuf_tensor("ga_idx", [1, NSEL], I32))
    listed, copied = c.sem("ga_listed"), c.sem("ga_copied")

    def copy(sp):
        sp.dma_start(idx[:, :], c.ins["block_idx"].unsqueeze(0)).then_inc(listed, 16)
        sp.wait_ge(listed, 16)
        with sp.Fori(0, NSEL) as i:
            blk = sp.value_load(idx[0:1, bass.ds(i, 1)], min_val=0, max_val=NBLK - 1)
            for src, dst in ((c.ins["k_cache"], c.ks), (c.ins["v_cache"], c.vs)):
                sp.dma_start(dst[bass.ds(i * BLOCK, BLOCK), :],
                             src[bass.ds(blk, 1), :, :].rearrange("o r n -> (o r) n")).then_inc(copied, 16)
        sp.wait_ge(copied, 32 * NSEL)

    return copy


class Group:

    def __init__(self, i, off):
        self.i, self.off = i, off

    def count(self, per, more):
        const = self.off * per + more
        return const if self.i is None else self.i * per + const

    def later(self, n=1):
        return Group(self.i, self.off + n)

    def row(self):
        return self.count(1, 0)

    def is_(self, n):
        return self.i is None and self.off == n


def at_least(eng, sem, value):
    if not isinstance(value, int) or value > 0:
        eng.wait_ge(sem, value)


def attention1(c):
    nc = c.nc
    NT = REP * TT
    NUN = NT // 2
    NUH = TT // 2
    HALF = T // 2
    HK = NKEY // 2
    LAST = NKV - 1
    FIRST_ITEMS = 6
    with ExitStack() as ctx:
        norm = Norm(c, ctx, "n1")
        sb = lambda n, s, d=F32: ctx.enter_context(nc.sbuf_tensor(f"a1_{n}", s, d))
        sem = lambda n: c.sem(f"a1_{n}")
        raw, rot = sb("raw", [P, KT, WG]), sb("rot", [P, 4, REP + 1, HD // 2])
        fc, fs = sb("cos", [P, HD // 2]), sb("sin", [P, HD // 2])
        wh, wl = sb("wh", [P, KT, WG], F32R), sb("wl", [P, KT, WG], F32R)
        raw_o, woh, wol = sb("raw_o", [P, 2, D]), sb("woh", [P, 2, D], F32R), sb("wol", [P, 2, D], F32R)
        kv, kt = sb("kv", [P, NKT, 2, HD]), sb("kt", [P, NKEY])
        kh, kl = sb("kh", [P, NKEY], F32R), sb("kl", [P, NKEY], F32R)
        vh, vl = sb("vh", [P, NKT, HD], F32R), sb("vl", [P, NKT, HD], F32R)
        qh, ql = sb("qh", [P, 2, T], F32R), sb("ql", [P, 2, T], F32R)
        prob = sb("prob", [P, 2, NKEY])
        nmax, den, rec = sb("nmax", [P, 2]), sb("den", [P, 2]), sb("rec", [P, 4])
        ph, pl = sb("ph", [P, 2, NKT, S], F32R), sb("pl", [P, 2, NKT, S], F32R)
        rs, ot = sb("rs", [P, S]), sb("ot", [P, 2, S])
        oh, ol = sb("oh", [P, 2, T], F32R), sb("ol", [P, 2, T], F32R)

        tables, w_loaded, rotated, rot_part, w_hi, w_lo = (sem("tables"), sem("w_loaded"), sem("rotated"),
                                                           sem("rot_part"), sem("w_hi"), sem("w_lo"))
        wo_loaded, wo_hi, wo_lo = sem("wo_loaded"), sem("wo_hi"), sem("wo_lo")
        k_loaded, v_loaded, k_hi, k_lo, v_hi, v_lo = (sem("k_loaded"), sem("v_loaded"), sem("k_hi"), sem("k_lo"),
                                                      sem("v_hi"), sem("v_lo"))
        work_done, work_read, q_hi = sem("work_done"), sem("work_read"), sem("q_hi")
        scored, maxed, exped, turned, pt_hi, pt_lo = (sem("scored"), sem("maxed"), sem("exped"), sem("turned"),
                                                      sem("pt_hi"), sem("pt_lo"))
        recd, r_copied, pv_done, ot_done, o_hi, o_lo = (sem("recd"), sem("r_copied"),
            sem("pv"), sem("ot"), sem("o_hi"), sem("o_lo"))
        PO, WORK = c.bank(6)[:, 0:S], c.bank(7)
        PR = c.psum[:, 4:6, HK:512]
        turned_banks = c.psum[:, 4:6, 0:HK].rearrange("p a (k n) -> p a k n", n=P)
        key_tiles = lambda ap: ap.rearrange("p (a k) n -> p a k n", a=2)

        def items_at(g, h, v):
            early = late = None
            if h % 2 == 0:
                if not (g.is_(0) and h == 0):
                    late = ("output", h // 2, v)
                if v in (2, 5):
                    early = ("query", h + 1, v // 3)
            elif h == 1:
                if v in (1, 4):
                    late = ("query", 2, v // 3)
            elif not g.is_(LAST):
                late = {0: ("keys", 0, 0), 1: ("kv", 0, 0), 2: ("kv", 0, 1), 3: ("keys", 0, 1), 4: ("query", 0, 0),
                        5: ("query", 0, 1)}.get(v)
            return early, late

        order, number = [], {}
        for h in range(REP):
            for v in range(TT):
                for item in items_at(Group(None, 1), h, v):
                    if item:
                        number[(h, item)] = len(order)
                        order.append(item)
        PER = len(order)

        def nth(g, item, h):
            if g.is_(0) and h == 0:
                return FIRST_ITEMS + item[2]
            return g.count(PER, FIRST_ITEMS - TT + number[(h, item)])

        def query_item(g, h, half):
            if h == 0:
                if g.is_(0):
                    return FIRST_ITEMS - 2 + half
                return nth(g.later(-1), ("query", 0, half), 3)
            return nth(g, ("query", h, half), h - 1)

        def output_item(g, h, t):
            return nth(g, ("output", h // 2, t), h)

        def key_item(g, what):
            if g.is_(0):
                return [("keys", 0, 0), ("kv", 0, 0), ("kv", 0, 1), ("keys", 0, 1)].index(what)
            return nth(g.later(-1), what, 3)

        def ahead(g, h, v, d):
            v += d
            h, v = h + v // TT, v % TT
            if h == REP:
                g, h = g.later(), 0
                if g.is_(NKV):
                    return None
            return g, h, v

        tile = lambda g, h, v, more=0: g.count(NT, h * TT + v + more)
        unit = lambda g, h, v, more=0: g.count(NUN, h * NUH + v // 2 + more)
        through = lambda n: n + 1
        begun = lambda g, h, v, steps: not (g.is_(0) and h == 0 and v < steps)

        def unit_before(g, h, v, steps):
            v -= steps
            if v < 0:
                v, h = v + TT, h - 1
            if h < 0:
                g, h = g.later(-1), REP - 1
            return g, h, v // 2

        def walk(eng, step):
            for v in range(TT):
                step(Group(None, 0), 0, v)
            with eng.Fori(0, LAST) as i:
                for off, h in ((0, 1), (0, 2), (0, 3), (1, 0)):
                    for v in range(TT):
                        step(Group(i, off), h, v)
            for h in range(1, REP):
                for v in range(TT):
                    step(Group(None, LAST), h, v)

        with nc.Block() as block:

            @block.sync
            def _(sp):
                def load_w(g):
                    at_least(sp, w_lo, g.count(KT, 0))
                    sp.dma_start(raw[:, :, :], c.ins["group1"].rearrange("g (k p) n -> g p k n", p=P)
                                 [bass.ds(g.row(), 1), :, :, :].rearrange("o p k n -> (o p) k n")).then_inc(w_loaded, 16)

                def load_kv(g):
                    rows = lambda src: src.rearrange("(t p) n -> p t n", p=P)[:, :, bass.ds(g.count(HD, 0), HD)]
                    if not g.is_(0):
                        sp.wait_ge(work_done, through(key_item(g.later(-1), ("keys", 0, 1))))
                    sp.dma_start(kv[:, 0:CT, 0, :], rows(c.ks)).then_inc(k_loaded, 16)
                    at_least(sp, v_lo, g.count(1, 0))
                    sp.dma_start(kv[:, 0:CT, 1, :], rows(c.vs)).then_inc(v_loaded, 16)

                def load_wo(g, pair):
                    at_least(sp, wo_lo, g.count(2, pair))
                    sp.dma_start(raw_o[:, :, :], c.ins["wo1"].rearrange("(h p) n -> p h n", p=P)
                                 [:, bass.ds(g.count(REP, 2 * pair), 2), :]).then_inc(wo_loaded, 16)

                def rest(g):
                    if not g.is_(LAST):
                        load_w(g.later())
                        load_kv(g.later())
                    load_wo(g, 1)
                    if not g.is_(LAST):
                        load_wo(g.later(), 0)

                sp.dma_start(fc[:, :], c.ins["cos1"].partition_broadcast(P)).then_inc(tables, 16)
                sp.dma_start(fs[:, :], c.ins["sin1"].partition_broadcast(P)).then_inc(tables, 16)
                zero_g = Group(None, 0)
                load_w(zero_g)
                load_kv(zero_g)
                load_wo(zero_g, 0)
                rest(zero_g)
                with sp.Fori(0, LAST - 1) as i:
                    rest(Group(i, 1))
                rest(Group(None, LAST))

            @block.gpsimd
            def _(pool):
                NR = REP + 1

                def rotate(g, k):
                    x = raw[:, k, 0:NR * HD].rearrange("p (h f e) -> p h f e", h=NR, e=2)
                    cos, sin = (y[:, :].unsqueeze(1).broadcast_to([P, NR, HD // 2]) for y in (fc, fs))
                    pool.wait_ge(w_loaded, g.count(16, 16))
                    at_least(pool, rotated, g.count(2 * KT, 2 * k))
                    for i, (side, table) in enumerate(((0, cos), (1, sin), (0, sin), (1, cos))):
                        nc.gpsimd.tensor_tensor(rot[:, i, :, :], x[:, :, :, side], table, ALU.mult).then_inc(rot_part, 1)
                    pool.wait_ge(rot_part, g.count(4 * KT, 4 * k + 4))
                    nc.gpsimd.tensor_tensor(x[:, :, :, 0], rot[:, 0, :, :], rot[:, 1, :, :], ALU.subtract
                                            ).then_inc(rotated, 1)
                    nc.gpsimd.tensor_tensor(x[:, :, :, 1], rot[:, 2, :, :], rot[:, 3, :, :], ALU.add
                                            ).then_inc(rotated, 1)

                def w_low(g, k):
                    pool.wait_ge(w_hi, g.count(KT, k + 1))
                    nc.gpsimd.tensor_tensor(wl[:, k, :], raw[:, k, :], f32(wh[:, k, :]), ALU.subtract).then_inc(w_lo, 1)

                def o_low(j, h, m):
                    toks = slice(m * S, (m + 1) * S)
                    pool.wait_ge(o_hi, j(1))
                    nc.gpsimd.tensor_tensor(ol[:, h % 2, toks], ot[:, m % 2, :], f32(oh[:, h % 2, toks]), ALU.subtract
                                            ).then_inc(o_lo, 1)

                def step(g, h, v):
                    if v % 2 and begun(g, h, v, 5):
                        gg, hh, m = unit_before(g, h, v, 5)
                        o_low(lambda more: unit(gg, hh, 2 * m, more), hh, m)
                    if not g.is_(LAST) and (h, v) in ((1, 0), (1, 3), (1, 6), (2, 1)):
                        rotate(g.later(), 3 * (h - 1) + v // 3)
                    if not g.is_(LAST) and h == 2 and v >= 6:
                        for k in range(2):
                            w_low(g.later(), 2 * (v - 6) + k)
                    if h % 2 and v == 5:
                        pool.wait_ge(wo_hi, g.count(2, h // 2 + 1))
                        nc.gpsimd.tensor_tensor(wol[:, :, :], raw_o[:, :, :], f32(woh[:, :, :]), ALU.subtract
                                                ).then_inc(wo_lo, 1)

                pool.wait_ge(tables, 32)
                for k in range(KT):
                    rotate(Group(None, 0), k)
                    w_low(Group(None, 0), k)
                walk(pool, step)
                for m in range(NUH - 2, NUH):
                    o_low(lambda more: NKV * NUN - NUH + m + more, REP - 1, m)

            @block.tensor
            def _(pe):
                def scores(g, h, v):
                    n = lambda more: tile(g, h, v, more)
                    at_least(pe, exped, n(-1))
                    if v % 4 == 0:
                        pe.wait_ge(work_read, through(query_item(g, h, v // 4)))
                    if h == 0 and v == 0:
                        pe.wait_ge(k_lo, g.count(1, 1))
                    rows = slice(v * P, (v + 1) * P)
                    for a in range(2):
                        cols = slice(a * HK, (a + 1) * HK)
                        last = passes(pe, c.psum[:, 2 * (v % 2) + a, 0:HK],
                                      three(qh[:, h % 2, rows], ql[:, h % 2, rows], kh[:, cols], kl[:, cols]))
                    last.then_inc(scored, 1)

                def turn(g, h, v):
                    pe.wait_ge(exped, tile(g, h, v, 1))
                    at_least(pe, pt_lo, tile(g, h, v))
                    if v % 2:
                        at_least(pe, r_copied, unit(g, h, v))
                    for k in range(NKT):
                        last = pe.transpose(c.psum[:, 4 + k // 3, (k % 3) * P:(k % 3 + 1) * P],
                                            prob[:, v % 2, k * P:(k + 1) * P], c.ident[:, :])
                    if v % 2 == 0 and begun(g, h, v, 2):
                        pe.wait_ge(recd, tile(g, h, v))
                        last = turn_reciprocals((v + 2) % 4)
                    last.then_inc(turned, 1)

                def turn_reciprocals(s):
                    for t in range(2):
                        last = pe.transpose(PR[:, t, :], rec[:, s + t:s + t + 1].broadcast_to([P, P]), c.ident[:, :])
                    return last

                def weigh(g, h, m, part):
                    n = lambda more: unit(g, h, 2 * m, more)
                    if part == 0:
                        pe.wait_ge(pt_lo, tile(g, h, 2 * m, 2))
                        at_least(pe, ot_done, n(0))
                        if h == 0 and m == 0:
                            pe.wait_ge(v_lo, g.count(1, 1))
                    pairs = []
                    for k in range(part * NKT // 2, (part + 1) * NKT // 2):
                        pairs += three(vh[:, k, :], vl[:, k, :], ph[:, m % 2, k, :], pl[:, m % 2, k, :])
                    last = passes(pe, PO, pairs, start=part == 0, stop=part == 1)
                    if part:
                        last.then_inc(pv_done, 1)

                def query(h, half, bank):
                    pairs = []
                    for d in range(KT):
                        w = [x[:, d, h * HD:(h + 1) * HD] for x in (wh, wl)]
                        z = [x[:, d, half * HALF:(half + 1) * HALF] for x in (c.ZH, c.ZL)]
                        pairs += three(*w, *z)
                    return passes(pe, bank, pairs)

                def output(t, bank):
                    pairs = []
                    for h in range(2):
                        x = [y[:, h, t * P:(t + 1) * P] for y in (oh, ol)]
                        pairs += three(*x, woh[:, h, :], wol[:, h, :])
                    return passes(pe, bank, pairs)

                def own_kv(t, bank):
                    pairs = []
                    for k in range(KT):
                        pairs += three(*[x[:, k, t * P:(t + 1) * P] for x in (c.ZH, c.ZL)],
                                       *[w[:, k, REP * HD:WG] for w in (wh, wl)])
                    return passes(pe, bank[:, 0:2 * HD], pairs)

                def turn_keys(part, bank):
                    for i, j in enumerate(range(CT) if part == 0 else range(CT, NKT)):
                        last = pe.transpose(bank[:, i * P:(i + 1) * P], kv[:, j, 0, :], c.ident[:, :])
                    return last

                def work(g, item, n):
                    kind, a, part = item
                    at_least(pe, work_read, n)
                    if kind == "query":
                        if (a, part) == (0, 0):
                            pe.wait_ge(w_lo, g.count(KT, KT))
                        last = query(a, part, WORK)
                    elif kind == "kv":
                        pe.wait_ge(w_lo, g.count(KT, KT))
                        last = own_kv(part, WORK)
                    elif kind == "keys":
                        if part == 0:
                            pe.wait_ge(k_loaded, g.count(16, 16))
                        last = turn_keys(part, WORK)
                    else:
                        pair = g.count(2, a)
                        pe.wait_ge(wo_lo, pair)
                        pe.wait_ge(o_lo, g.count(NUN, 2 * NUH * a - NUH + part // 2 + 1))
                        last = output(part, WORK)
                    last.then_inc(work_done, 1)

                def step(g, h, v):
                    early, late = items_at(g, h, v)
                    item_number = lambda item: nth(g, item, h)
                    owner = g.later() if h == 3 else g
                    turn(g, h, v)
                    if early:
                        work(owner, early, item_number(early))
                    nxt = ahead(g, h, v, 2)
                    changes = nxt and nxt[1] == 0 and nxt[2] == 0
                    if nxt and not changes:
                        scores(*nxt)
                    if begun(g, h, v, 2):
                        gg, hh, m = unit_before(g, h, v - v % 2, 2)
                        weigh(gg, hh, m, v % 2)
                    if changes:
                        scores(*nxt)
                    if late:
                        work(owner, late, item_number(late))

                zero_g = Group(None, 0)
                for t in range(TT):
                    norm.turn(pe, t)
                pe.wait_ge(norm.lo_done, TT)
                for n, item in enumerate((("keys", 0, 0), ("kv", 0, 0), ("kv", 0, 1), ("keys", 0, 1), ("query", 0, 0),
                                          ("query", 0, 1))):
                    work(zero_g, item, n)
                scores(zero_g, 0, 0)
                scores(zero_g, 0, 1)
                walk(pe, step)
                last_g = Group(None, LAST)
                pe.wait_ge(pt_lo, NKV * NT)
                pe.wait_ge(recd, NKV * NT)
                turn_reciprocals(2).then_inc(turned, 1)
                for part in range(2):
                    weigh(last_g, REP - 1, NUH - 1, part)
                tail = output_item(last_g, 2, TT - 1) + 1
                pe.wait_ge(work_read, tail)
                pe.wait_ge(wo_lo, 2 * NKV)
                for t in range(TT):
                    pe.wait_ge(o_lo, NKV * NUN - NUH + t // 2 + 1)
                    if t >= 4:
                        pe.wait_ge(work_read, tail + t - 3)
                    output(t, c.bank(t % 4)).then_inc(work_done, 1)

            @block.scalar
            def _(act):
                def exp_of(g, h, v):
                    n, s = lambda more: tile(g, h, v, more), v % 2
                    act.wait_ge(maxed, n(1))
                    at_least(act, turned, n(-1))
                    at_least(act, recd, n(-1))
                    nc.scalar.activation(prob[:, s, :].rearrange("p (a n) -> p a n", a=2),
                                         c.psum[:, 2 * s:2 * s + 2, 0:HK], ACT.Exp, bias=nmax[:, s:s + 1],
                                         accum_out=den[:, s:s + 1]).then_inc(exped, 1)

                def high(g, h, v):
                    act.wait_ge(turned, tile(g, h, v, 1))
                    at_least(act, pv_done, unit(g, h, v, -1))
                    nc.scalar.activation(key_tiles(ph[:, (v // 2) % 2, :, (v % 2) * P:(v % 2 + 1) * P]), turned_banks,
                                         ACT.Copy).then_inc(pt_hi, 1)

                def r_copy(g, h, m):
                    act.wait_ge(turned, tile(g, h, 2 * m, 3))
                    at_least(act, ot_done, unit(g, h, 2 * m))
                    nc.scalar.activation(rs[:, :].rearrange("p (t n) -> p t n", t=2), PR, ACT.Copy).then_inc(r_copied, 1)

                def o_high(g, h, m):
                    act.wait_ge(ot_done, unit(g, h, 2 * m, 1))
                    if h % 2 == 0 and not (g.is_(0) and h == 0):
                        act.wait_ge(work_done, through(output_item(g, h, 2 * m + 1)))
                    elif h % 2 and not (g.is_(0) and h == 1):
                        act.wait_ge(work_done, through(output_item(g, h - 1, 2 * m + 1)))
                    nc.scalar.activation(oh[:, h % 2, m * S:(m + 1) * S], ot[:, m % 2, :], ACT.Copy).then_inc(o_hi, 1)

                def take(g, h, item, n):
                    kind, a, part = item
                    if kind == "output":
                        return
                    act.wait_ge(work_done, through(n))
                    if kind == "query":
                        head = g.count(REP, a)
                        at_least(act, scored, g.count(NT, (a - 1) * TT))
                        nc.scalar.activation(qh[:, a % 2, part * HALF:(part + 1) * HALF], WORK, ACT.Copy,
                                             scale=SCALE1).then_inc(q_hi, 1)
                    elif kind == "kv":
                        at_least(act, v_lo, g.count(1, 0))
                        nc.scalar.activation(kv[:, CT + part, :, :].rearrange("p e n -> p (e n)"), WORK[:, 0:2 * HD],
                                             ACT.Copy).then_inc(work_read, 1)
                    else:
                        at_least(act, k_lo, g.count(1, 0))
                        cols = slice(0, CT * P) if part == 0 else slice(CT * P, NKEY)
                        nc.scalar.activation(kt[:, cols], WORK[:, 0:cols.stop - cols.start], ACT.Copy
                                             ).then_inc(work_read, 1)

                def split_keys(g):
                    act.wait_ge(work_read, through(key_item(g, ("keys", 0, 1))))
                    at_least(act, scored, g.count(NT, 0))
                    nc.scalar.activation(kh[:, :], kt[:, :], ACT.Copy).then_inc(k_hi, 1)

                def split_values(g):
                    act.wait_ge(v_loaded, g.count(16, 16))
                    act.wait_ge(work_read, through(key_item(g, ("kv", 0, 1))))
                    at_least(act, pv_done, g.count(NUN, 0))
                    nc.scalar.activation(vh[:, :, :], kv[:, :, 1, :], ACT.Copy).then_inc(v_hi, 1)

                def split_w(g, k):
                    act.wait_ge(rotated, g.count(2 * KT, 2 * k + 2))
                    if not g.is_(0):
                        act.wait_ge(work_done, through(query_item(g.later(-1), 3, 1)))
                    nc.scalar.activation(wh[:, k, :], raw[:, k, :], ACT.Copy).then_inc(w_hi, 1)

                def step(g, h, v):
                    owner = g.later() if h == 3 else g
                    if begun(g, h, v, 1) and (h, v) != (1, 0):
                        pg, phd, pv = (g, h, v - 1) if v else ((g, h - 1, TT - 1) if h else (g.later(-1), 3, TT - 1))
                        _, late = items_at(pg, phd, pv)
                        if late:
                            take(pg.later() if phd == 3 else pg, phd, late, nth(pg, late, phd))
                    if h == 3 and v == 6 and not g.is_(LAST):
                        split_keys(g.later())
                    if h == 0 and v == 2 and not g.is_(0):
                        split_values(g)
                    high(g, h, v)
                    if v % 2 == 0 and begun(g, h, v, 2):
                        r_copy(*unit_before(g, h, v, 2))
                    nxt = ahead(g, h, v, 1)
                    if nxt:
                        exp_of(*nxt)
                    early, _ = items_at(g, h, v)
                    if early:
                        take(owner, h, early, nth(g, early, h))
                    if v % 2 and begun(g, h, v, 5):
                        o_high(*unit_before(g, h, v, 5))
                    if h == 2 and v >= 6 and not g.is_(LAST):
                        for k in range(2):
                            split_w(g.later(), 2 * (v - 6) + k)
                    if h % 2 and v == 5:
                        act.wait_ge(wo_loaded, g.count(32, 16 * (h // 2 + 1)))
                        if not (g.is_(0) and h == 1):
                            act.wait_ge(work_done, through(output_item(g, h - 1, TT - 1)))
                        nc.scalar.activation(woh[:, :, :], raw_o[:, :, :], ACT.Copy).then_inc(wo_hi, 1)

                zero_g = Group(None, 0)
                norm.scalar_std(act)
                for t in range(TT):
                    norm.scalar_hi(act, t)
                for k in range(KT):
                    split_w(zero_g, k)
                for n, item in enumerate((("keys", 0, 0), ("kv", 0, 0), ("kv", 0, 1), ("keys", 0, 1))):
                    take(zero_g, 0, item, n)
                split_keys(zero_g)
                for half in range(2):
                    take(zero_g, 0, ("query", 0, half), FIRST_ITEMS - 2 + half)
                split_values(zero_g)
                exp_of(zero_g, 0, 0)
                walk(act, step)
                last_g = Group(None, LAST)
                o_high(last_g, REP - 1, NUH - 2)
                r_copy(last_g, REP - 1, NUH - 1)
                o_high(last_g, REP - 1, NUH - 1)

            @block.vector
            def _(dve):
                def max_of(g, h, v):
                    n, s = lambda more: tile(g, h, v, more), v % 2
                    dve.wait_ge(scored, n(1))
                    at_least(dve, exped, n(-1))
                    nc.vector.tensor_reduce(nmax[:, s:s + 1], c.psum[:, 2 * s:2 * s + 2, 0:HK],
                                            mybir.AxisListType.XY, ALU.max, negate=True).then_inc(maxed, 1)

                def recip(g, h, v):
                    dve.wait_ge(exped, tile(g, h, v, 1))
                    at_least(dve, turned, tile(g, h, v, -1))
                    nc.vector.reciprocal(rec[:, v % 4:v % 4 + 1], den[:, v % 2:v % 2 + 1]).then_inc(recd, 1)

                def low(g, h, v):
                    m, cols = (v // 2) % 2, slice((v % 2) * P, (v % 2 + 1) * P)
                    dve.wait_ge(pt_hi, tile(g, h, v, 1))
                    at_least(dve, r_copied, unit(g, h, v))
                    nc.vector.tensor_tensor(key_tiles(pl[:, m, :, cols]), turned_banks, f32(key_tiles(ph[:, m, :, cols])),
                                            ALU.subtract).then_inc(pt_lo, 1)

                def output(g, h, m):
                    n = lambda more: unit(g, h, 2 * m, more)
                    dve.wait_ge(pv_done, n(1))
                    dve.wait_ge(r_copied, n(1))
                    at_least(dve, o_lo, n(-1))
                    nc.vector.tensor_tensor(ot[:, m % 2, :], PO, rs[:, :], ALU.mult).then_inc(ot_done, 1)

                def take(g, item, n):
                    kind, a, part = item
                    if kind == "query":
                        toks = slice(part * HALF, (part + 1) * HALF)
                        dve.wait_ge(q_hi, g.count(2 * REP, 2 * a + part + 1))
                        nc.vector.scalar_tensor_tensor(ql[:, a % 2, toks], WORK, SCALE1, f32(qh[:, a % 2, toks]),
                                                       ALU.mult, ALU.subtract).then_inc(work_read, 1)
                    elif kind == "output":
                        add(part, WORK, n)

                def add(t, bank, n):
                    dve.wait_ge(work_done, through(n))
                    nc.vector.tensor_tensor(c.X[:, t, :], bank, c.X[:, t, :], ALU.add).then_inc(work_read, 1)

                def split_keys(g):
                    dve.wait_ge(k_hi, g.count(1, 1))
                    nc.vector.tensor_tensor(kl[:, :], kt[:, :], f32(kh[:, :]), ALU.subtract).then_inc(k_lo, 1)

                def split_values(g):
                    dve.wait_ge(v_hi, g.count(1, 1))
                    nc.vector.tensor_tensor(vl[:, :, :], kv[:, :, 1, :], f32(vh[:, :, :]), ALU.subtract).then_inc(v_lo, 1)

                def step(g, h, v):
                    owner = g.later() if h == 3 else g
                    nxt = ahead(g, h, v, 1)
                    if nxt:
                        max_of(*nxt)
                    if begun(g, h, v, 1) and (h, v) != (1, 0):
                        pg, phd, pv = (g, h, v - 1) if v else ((g, h - 1, TT - 1) if h else (g.later(-1), 3, TT - 1))
                        _, late = items_at(pg, phd, pv)
                        if late:
                            take(pg.later() if phd == 3 else pg, late, nth(pg, late, phd))
                    if h == 3 and v == 6 and not g.is_(LAST):
                        split_keys(g.later())
                    if h == 0 and v == 2 and not g.is_(0):
                        split_values(g)
                    if v % 2 == 0 and begun(g, h, v, 4):
                        output(*unit_before(g, h, v, 4))
                    recip(g, h, v)
                    low(g, h, v)
                    early, late = items_at(g, h, v)
                    if early:
                        take(owner, early, nth(g, early, h))
                    if (h, v) == (0, TT - 1) and late:
                        take(g, late, nth(g, late, h))

                zero_g = Group(None, 0)
                norm.vector(dve)
                split_keys(zero_g)
                for half in range(2):
                    take(zero_g, ("query", 0, half), FIRST_ITEMS - 2 + half)
                split_values(zero_g)
                max_of(zero_g, 0, 0)
                walk(dve, step)
                last_g = Group(None, LAST)
                for m in range(NUH - 2, NUH):
                    output(last_g, REP - 1, m)
                tail = output_item(last_g, 2, TT - 1) + 1
                for t in range(TT):
                    add(t, c.bank(t % 4), tail + t)


def store(c):
    nc = c.nc
    stored = c.sem("stored")
    with nc.Block() as block:

        @block.sync
        def _(sp):
            sp.dma_start(c.out.rearrange("(t p) n -> p t n", p=P), c.X[:, :, :]).then_inc(stored, 16)
            sp.wait_ge(stored, 16)


def macaron(nc, ins, out):
    c = Chip()
    c.nc, c.ins, c.out = nc, ins, out
    with ExitStack() as whole:
        c.sems = []
        c.sem = lambda n: c.sems.append(nc.alloc_semaphore(name=n)) or c.sems[-1]
        sb = lambda ctx, n, s, d=F32: ctx.enter_context(nc.sbuf_tensor(n, s, d))
        c.psum = whole.enter_context(nc.psum_tensor("psum", [P, 8, 512], F32))
        c.bank = lambda i: c.psum[:, i, :]
        c.banks = lambda i, n: c.psum[:, i:i + n, :].rearrange("p a n -> p (a n)")
        dram = lambda n, s: nc.dram_tensor(n, s, F32, kind="Internal").ap()
        c.w0 = dram("w_joint", (D, D))
        c.dq = dram("dequantised", (P, (NF_PARTS + 1) * NF_W))
        c.wd = dram("wd", (FC, P, 3 * D))
        c.ks, c.vs = dram("k_chosen", (NSEL * BLOCK, NKV * HD)), dram("v_chosen", (NSEL * BLOCK, NKV * HD))
        c.X = sb(whole, "X", [P, TT, D])
        c.ident = sb(whole, "ident", [P, P])
        with ExitStack() as ctx:
            c.ident_bf, c.zero_bf = sb(ctx, "ident_bf", [P, P], BF16), sb(ctx, "zero_bf", [P, D], BF16)
            c.nf_bias = sb(ctx, "nf_bias", [P, len(NF4_STEPS)])
            setup(c)
            with ExitStack() as l0:
                c.UH, c.UL = sb(l0, "UH", [P, 3, T], F32R), sb(l0, "UL", [P, 3, T], F32R)
                c.V = sb(l0, "V", [P, TT, 192])
                c.VH, c.VL = sb(l0, "VH", [P, TT, 192], F32R), sb(l0, "VL", [P, TT, 192], F32R)
                c.IW, c.mask = sb(l0, "IW", [P, TT, IDX_H]), sb(l0, "mask", [P, B, 2, S], BF16)
                with ExitStack() as z:
                    c.ZH, c.ZL = sb(z, "ZH0", [P, KT, T], F32R), sb(z, "ZL0", [P, KT, T], F32R)
                    c.IKH, c.IKL = sb(z, "IKH", [P, T], F32R), sb(z, "IKL", [P, T], F32R)
                    ffn0(c, "f0", beside=gather)
                    latents(c)
                    indexer(c)
                attention0(c)
            recycle(c)
            turn_weights(c)
            with ExitStack() as l0:
                c.ZH, c.ZL = sb(l0, "ZH1", [P, KT, T], F32R), sb(l0, "ZL1", [P, KT, T], F32R)
                ffn0(c, "f1")
                ffn1(c, "g0")
        with ExitStack() as l1:
            c.ZH, c.ZL = sb(l1, "ZH2", [P, KT, T], F32R), sb(l1, "ZL2", [P, KT, T], F32R)
            attention1(c)
        with ExitStack() as l1:
            c.ZH, c.ZL = sb(l1, "ZH3", [P, KT, T], F32R), sb(l1, "ZL3", [P, KT, T], F32R)
            c.zero_bf = sb(l1, "zero_bf2", [P, D], BF16)
            zero(c)
            ffn1(c, "g1")
        store(c)


def recycle(c):
    c.nc.clear_and_free_semaphores(c.sems)
    c.sems = []
    with c.nc.Block() as block:

        @block.gpsimd
        def _(pool):
            pass


def zero(c):
    zeroed = c.sem("zeroed")
    with c.nc.Block() as block:

        @block.gpsimd
        def _(pool):
            c.nc.gpsimd.memset(c.zero_bf[:, :], 0.0).then_inc(zeroed, 1)



def rope_order(a):
    a = a.reshape(a.shape[:-1] + (2, 16, 2))
    return np.ascontiguousarray(np.moveaxis(a, -1, -2)).reshape(a.shape[:-3] + (ROPE,))


def rope_tables():
    freq = (1.0 / THETA ** (np.arange(0, ROPE, 2, dtype=np.float32) / ROPE)).astype(np.float32)
    ang = (np.arange(S, dtype=np.float32)[:, None] * freq[None, :]).astype(np.float32)
    cos, sin = np.cos(ang), np.sin(ang)
    two = lambda x0, x1: rope_order(np.stack([x0, x1], -1).reshape(S, ROPE))
    return two(cos, cos).astype(np.float32), two(-sin, sin).astype(np.float32)


def lay_out(a):
    np_ = lambda n: np.asarray(a[n])
    out = {"x": np_("L0_attn_hidden_states").reshape(T, D)}
    out["lora_a"] = np_("L0_ffn_lora_A").reshape(P, D)
    out["lora_b"] = np_("L0_ffn_lora_B").transpose(0, 2, 1).reshape(P, D)
    out["lora_w"] = np_("L0_ffn_lora_weights")
    out["w0"] = np_("L0_ffn_W").T
    out["bias"] = np_("L0_ffn_bias")
    out["nf_bias"] = (-NF4_BOUNDS * np.float32(STEEP)).astype(np.float32)
    kva = np_("L0_attn_kv_a_w")
    out["proj"] = np.concatenate([np_("L0_attn_q_a_w"), kva[:, :KV_RANK], rope_order(kva[:, KV_RANK:]),
                                  np_("L0_attn_idx_wk_w"), np_("L0_attn_idx_weights_w")], axis=1)
    out["q_norm"], out["kv_norm"] = np_("L0_attn_q_a_norm_w"), np_("L0_attn_kv_a_norm_w")
    cos, sin = rope_tables()
    out["key_cos"], out["key_sin"] = cos, sin
    scale = np.float32(SCALE0)
    out["query_cos"], out["query_sin"] = cos.T * scale, sin.T * scale
    out["idx_wq"] = np_("L0_attn_idx_wq_w")
    qb = np_("L0_attn_q_b_w").reshape(Q_RANK, H0, NOPE + ROPE)
    kvb = np_("L0_attn_kv_b_w").reshape(KV_RANK, H0, NOPE + VD)
    twice = lambda w: np.concatenate([w[:P], w[P:], w[P:]])
    heads = lambda w: w.reshape(NG0, G0, P, -1).transpose(0, 2, 1, 3).reshape(NG0, P, -1)
    qn = heads(twice(qb[:, :, :NOPE]).transpose(1, 2, 0))
    kk = heads(kvb[:, :, :NOPE].transpose(1, 2, 0))
    kv = heads(kvb[:, :, NOPE:].transpose(1, 2, 0))
    ow = heads(np_("L0_attn_o_w").reshape(H0, VD, D))
    pe = twice(rope_order(qb[:, :, NOPE:])).reshape(2, P, NG0, G0, ROPE).transpose(2, 1, 3, 0, 4).reshape(NG0, P, -1)
    out["group0"] = np.concatenate([qn, kk, kv, ow, pe], axis=2)
    out["cos1"], out["sin1"] = np_("L1_attn_freqs_cos").reshape(-1), np_("L1_attn_freqs_sin").reshape(-1)
    wq = np_("L1_attn_wq").reshape(NKV, REP * HD, D)
    wk, wv = (np_(f"L1_attn_w{x}").reshape(NKV, HD, D) for x in "kv")
    out["group1"] = np.concatenate([wq, wk, wv], axis=1).transpose(0, 2, 1)
    out["wo1"] = np_("L1_attn_wo").T
    out["k_cache"], out["v_cache"] = (np_(f"L1_attn_{x}_cache").reshape(NBLK, BLOCK, NKV * HD) for x in "kv")
    out["block_idx"] = np_("L1_attn_block_idx")
    rows = lambda w: np.concatenate([w, np.zeros((FHP - FH, D), w.dtype)]).reshape(FC, P, D).transpose(1, 0, 2)
    w3 = np_("L1_ffn_w3").reshape(2, P, 2, FH).transpose(1, 0, 2, 3)
    out["nf"] = np.zeros((P, (NF_PARTS + 2) * NF_W), w3.dtype)
    for at, w in ((NF_W1, rows(np_("L1_ffn_w1"))), (NF_W2, rows(np_("L1_ffn_w2"))), (NF_W3, w3)):
        w = w.reshape(P, -1)
        out["nf"][:, at:at + w.shape[1]] = w
    return {n: np.ascontiguousarray(x) for n, x in out.items()}


def kernel(**inputs):
    import concourse.bacc as _bacc
    from concourse.bass_utils import run_bass_kernel_spmd as _run

    nc = _bacc.Bacc("TRN2", target_bir_lowering=False, num_devices=1)
    arrays = {f"in_{n}": x for n, x in lay_out(inputs).items()}
    ins = {n[3:]: nc.dram_tensor(n, x.shape, mybir.dt.from_np(x.dtype), kind="ExternalInput").ap()
           for n, x in arrays.items()}
    out = nc.dram_tensor("out", (T, D), F32, kind="ExternalOutput").ap()
    macaron(nc, ins, out)
    r = _run(nc, [arrays], core_ids=[0])
    return r.results[0]["out"].reshape(B, S, D)
```
